# Optimizing a Trainium2 kernel written in Bass

```python
import numpy as np
import jax
import jax.numpy as jnp

def _softmax(x, axis=-1):
    return jax.nn.softmax(x, axis=axis)

def _gelu(x):
    return jax.nn.gelu(x, approximate=True)

def _silu(x):
    return jax.nn.silu(x)

def _sigmoid(x):
    return jax.nn.sigmoid(x)

def _layernorm(x, axis=-1, eps=1e-05):
    m = jnp.mean(x, axis=axis, keepdims=True)
    v = jnp.var(x, axis=axis, keepdims=True)
    return (x - m) / jnp.sqrt(v + eps)

def _scatter_add(tgt, idx, src, axis=0):
    return tgt.at[idx].add(src)

def _segment_sum(src, seg, n):
    return jax.ops.segment_sum(src, seg, n)
kernel_name = 'mk_xattn_ffn_d2_seqx_r8_d4b351'

def setup_inputs(seed: int=0):
    np.random.seed(seed)
    _w = jnp.asarray

    def _rec_inputs():
        import jax
        import jax.numpy as jnp
        _rk = jax.random.key(seed)
        x = -0.0002928 + 1 * jax.random.normal(jax.random.fold_in(_rk, 1), (8, 256, 128), jnp.float32)
        _lenS = 256 - jax.random.randint(jax.random.fold_in(_rk, 7), (8,), 0, max(1, 256 // 4) + 1, jnp.int32)
        _lenS2 = 256 - jax.random.randint(jax.random.fold_in(_rk, 8), (8,), 0, max(1, 256 // 4) + 1, jnp.int32)
        _ctx_512P = jax.random.normal(jax.random.fold_in(_rk, 11), (8, 16, 64), jnp.float32)
        _ctx_512c = jax.random.dirichlet(jax.random.fold_in(_rk, 511), 0.3 * jnp.ones((16,), jnp.float32), (8, 256))
        _ctx_512t = jnp.einsum('bsk,bkd->bsd', _ctx_512c, _ctx_512P)
        _ctx_512t = _ctx_512t * jax.lax.rsqrt(jnp.mean(jnp.square(_ctx_512t)) + 1e-12) * 0.953939
        ctx_512 = 0.00222621 + 0.99962 * (_ctx_512t + 0.3 * jax.random.normal(jax.random.fold_in(_rk, 611), (8, 256, 64), jnp.float32))
        return (x, ctx_512)
    x, ctx_512 = _rec_inputs()

    def _L0_xattn_setup():
        import jax, jax.numpy as jnp
        import numpy as np
        B, T, TC, C, CC, H = (2, 256, 64, 128, 64, 16)
        D = C // H

        def _heads(t):
            b, l, _ = t.shape
            return t.reshape(b, l, H, D).transpose(0, 2, 1, 3)
        key = jax.random.key(seed)
        ks = jax.random.split(key, 18)
        w = lambda k, i, o: jax.random.normal(k, (i, o), jnp.float32) / np.sqrt(i).astype(np.float32)
        return {'x': jax.random.normal(ks[0], (B, T, C), jnp.float32), 'cross_input': jax.random.normal(ks[1], (B, TC, CC), jnp.float32), 'Wk': w(ks[2], C, C), 'bk': jnp.zeros((C,), jnp.float32), 'Wq': w(ks[3], C, C), 'bq': jnp.zeros((C,), jnp.float32), 'Wv': w(ks[4], C, C), 'bv': jnp.zeros((C,), jnp.float32), 'Wck': w(ks[5], CC, C), 'bck': jnp.zeros((C,), jnp.float32), 'Wcq': w(ks[6], C, C), 'bcq': jnp.zeros((C,), jnp.float32), 'Wcv': w(ks[7], CC, C), 'bcv': jnp.zeros((C,), jnp.float32), 'Wp': w(ks[8], C, C), 'bp': jnp.zeros((C,), jnp.float32)}
    _L0_xattn_all = _L0_xattn_setup()
    _L0_xattn_in = {k: v for k, v in _L0_xattn_all.items() if k in ('Wk', 'bk', 'Wq', 'bq', 'Wv', 'bv', 'Wck', 'bck', 'Wcq', 'bcq', 'Wcv', 'bcv', 'Wp', 'bp')}
    del _L0_xattn_all

    def _L0_ffn_setup():
        import jax, jax.numpy as jnp
        import numpy as np
        N_EMBD = 128
        NUM_EXPERTS = 8
        TOP_K = 2
        D_FF = 4 * N_EMBD
        B, S = (4, 256)
        key = jax.random.key(seed)
        ks = jax.random.split(key, 7)
        scale = lambda fan_in: 1.0 / np.sqrt(fan_in)
        x = jax.random.normal(ks[0], (B, S, N_EMBD), dtype=jnp.float32)
        W_router = jax.random.normal(ks[1], (N_EMBD, NUM_EXPERTS), dtype=jnp.float32) * scale(N_EMBD)
        b_router = jnp.zeros((NUM_EXPERTS,), dtype=jnp.float32)
        W1 = jax.random.normal(ks[2], (NUM_EXPERTS, N_EMBD, D_FF), dtype=jnp.float32) * scale(N_EMBD)
        b1 = jnp.zeros((NUM_EXPERTS, D_FF), dtype=jnp.float32)
        W2 = jax.random.normal(ks[3], (NUM_EXPERTS, D_FF, N_EMBD), dtype=jnp.float32) * scale(D_FF)
        b2 = jnpp = jnp.zeros((NUM_EXPERTS, N_EMBD), dtype=jnp.float32)
        return {'x': x, 'W_router': W_router, 'b_router': b_router, 'W1': W1, 'b1': b1, 'W2': W2, 'b2': b2}
    _L0_ffn_all = _L0_ffn_setup()
    _L0_ffn_in = {k: v for k, v in _L0_ffn_all.items() if k in ('W_router', 'b_router', 'W1', 'b1', 'W2', 'b2')}
    del _L0_ffn_all

    def _L1_xattn_setup():
        import jax, jax.numpy as jnp
        import numpy as np
        B, LQ, LK = (8, 256, 256)
        QD, KD, VD = (128, 64, 64)
        key = jax.random.key(seed)
        ks = jax.random.split(key, 9)
        s = 0.02
        return {'query': jax.random.normal(ks[0], (B, LQ, QD), jnp.float32), 'key': jax.random.normal(ks[1], (B, LK, KD), jnp.float32), 'value': jax.random.normal(ks[2], (B, LK, VD), jnp.float32), 'Wq': jax.random.normal(ks[3], (QD, QD), jnp.float32) * s, 'bq': jnp.zeros((QD,), jnp.float32), 'Wk': jax.random.normal(ks[4], (KD, QD), jnp.float32) * s, 'bk': jnp.zeros((QD,), jnp.float32), 'Wv': jax.random.normal(ks[5], (VD, QD), jnp.float32) * s, 'bv': jnp.zeros((QD,), jnp.float32)}
    _L1_xattn_all = _L1_xattn_setup()
    _L1_xattn_in = {k: v for k, v in _L1_xattn_all.items() if k in ('Wq', 'bq', 'Wk', 'bk', 'Wv', 'bv')}
    del _L1_xattn_all

    def _L1_ffn_setup():
        import jax, jax.numpy as jnp
        import numpy as np
        B, T, DIM = (2, 256, 128)
        H, DH, E, K = (16, 64, 8, 2)
        key = jax.random.key(seed)
        ks = jax.random.split(key, 7)
        s = 0.02
        return {'x': jax.random.normal(ks[0], (B, T, DIM), jnp.float32), 'Wq': jax.random.normal(ks[1], (H, DH, DIM), jnp.float32) * s, 'Wk': jax.random.normal(ks[2], (H, DH, DIM), jnp.float32) * s, 'Wv': jax.random.normal(ks[3], (E, DH, DIM), jnp.float32) * s, 'Ws': jax.random.normal(ks[4], (H, E, DIM), jnp.float32) * s, 'Wd': jax.random.normal(ks[5], (H, E, DIM), jnp.float32) * s, 'Wo': jax.random.normal(ks[6], (E, DIM, DH), jnp.float32) * s}
    _L1_ffn_all = _L1_ffn_setup()
    _L1_ffn_in = {k: v for k, v in _L1_ffn_all.items() if k in ('Wq', 'Wk', 'Wv', 'Ws', 'Wd', 'Wo')}
    del _L1_ffn_all
    return {'x': x, 'ctx_512': ctx_512, 'L0_xattn_Wk': _L0_xattn_in['Wk'], 'L0_xattn_bk': _L0_xattn_in['bk'], 'L0_xattn_Wq': _L0_xattn_in['Wq'], 'L0_xattn_bq': _L0_xattn_in['bq'], 'L0_xattn_Wv': _L0_xattn_in['Wv'], 'L0_xattn_bv': _L0_xattn_in['bv'], 'L0_xattn_Wck': _L0_xattn_in['Wck'], 'L0_xattn_bck': _L0_xattn_in['bck'], 'L0_xattn_Wcq': _L0_xattn_in['Wcq'], 'L0_xattn_bcq': _L0_xattn_in['bcq'], 'L0_xattn_Wcv': _L0_xattn_in['Wcv'], 'L0_xattn_bcv': _L0_xattn_in['bcv'], 'L0_xattn_Wp': _L0_xattn_in['Wp'], 'L0_xattn_bp': _L0_xattn_in['bp'], 'L0_ffn_W_router': _L0_ffn_in['W_router'], 'L0_ffn_b_router': _L0_ffn_in['b_router'], 'L0_ffn_W1': _L0_ffn_in['W1'], 'L0_ffn_b1': _L0_ffn_in['b1'], 'L0_ffn_W2': _L0_ffn_in['W2'], 'L0_ffn_b2': _L0_ffn_in['b2'], 'L1_xattn_Wq': _L1_xattn_in['Wq'], 'L1_xattn_bq': _L1_xattn_in['bq'], 'L1_xattn_Wk': _L1_xattn_in['Wk'], 'L1_xattn_bk': _L1_xattn_in['bk'], 'L1_xattn_Wv': _L1_xattn_in['Wv'], 'L1_xattn_bv': _L1_xattn_in['bv'], 'L1_ffn_Wq': _L1_ffn_in['Wq'], 'L1_ffn_Wk': _L1_ffn_in['Wk'], 'L1_ffn_Wv': _L1_ffn_in['Wv'], 'L1_ffn_Ws': _L1_ffn_in['Ws'], 'L1_ffn_Wd': _L1_ffn_in['Wd'], 'L1_ffn_Wo': _L1_ffn_in['Wo']}

def reference(x, ctx_512, L0_xattn_Wk, L0_xattn_bk, L0_xattn_Wq, L0_xattn_bq, L0_xattn_Wv, L0_xattn_bv, L0_xattn_Wck, L0_xattn_bck, L0_xattn_Wcq, L0_xattn_bcq, L0_xattn_Wcv, L0_xattn_bcv, L0_xattn_Wp, L0_xattn_bp, L0_ffn_W_router, L0_ffn_b_router, L0_ffn_W1, L0_ffn_b1, L0_ffn_W2, L0_ffn_b2, L1_xattn_Wq, L1_xattn_bq, L1_xattn_Wk, L1_xattn_bk, L1_xattn_Wv, L1_xattn_bv, L1_ffn_Wq, L1_ffn_Wk, L1_ffn_Wv, L1_ffn_Ws, L1_ffn_Wd, L1_ffn_Wo):
    import jax
    import jax.numpy as jnp

    def _L0_xattn_ref(x, cross_input, Wk, bk, Wq, bq, Wv, bv, Wck, bck, Wcq, bcq, Wcv, bcv, Wp, bp):
        import jax, jax.numpy as jnp
        import numpy as np
        B, T, TC, C, CC, H = (2, 256, 64, 128, 64, 16)
        D = C // H

        def _heads(t):
            b, l, _ = t.shape
            return t.reshape(b, l, H, D).transpose(0, 2, 1, 3)
        scale = np.float32(1.0 / np.sqrt(D))
        q = _heads(x @ Wq + bq)
        k = _heads(x @ Wk + bk)
        v = _heads(x @ Wv + bv)
        att = jnp.einsum('bhqd,bhkd->bhqk', q, k) * scale
        causal = jnp.tril(jnp.ones((T, T), bool))
        att = jnp.where(causal[None, None], att, -jnp.inf)
        y = jnp.einsum('bhqk,bhkd->bhqd', jax.nn.softmax(att, axis=-1), v)
        qc = _heads(x @ Wcq + bcq)
        kc = _heads(cross_input @ Wck + bck)
        vc = _heads(cross_input @ Wcv + bcv)
        attc = jnp.einsum('bhqd,bhkd->bhqk', qc, kc) * scale
        y = y + jnp.einsum('bhqk,bhkd->bhqd', jax.nn.softmax(attc, axis=-1), vc)
        y = y.transpose(0, 2, 1, 3).reshape(x.shape[0], T, C)
        return y @ Wp + bp

    def _L0_ffn_ref(x, W_router, b_router, W1, b1, W2, b2):
        import jax, jax.numpy as jnp
        import numpy as np
        N_EMBD = 128
        NUM_EXPERTS = 8
        TOP_K = 2
        D_FF = 4 * N_EMBD
        B, S = (4, 256)
        Bv, Sv, D = x.shape
        flat_x = x.reshape(-1, D)
        T = flat_x.shape[0]
        logits = flat_x @ W_router + b_router
        top_vals, top_idx = jax.lax.top_k(logits, TOP_K)
        neg_inf = jnp.full_like(logits, -jnp.inf)
        sparse_logits = neg_inf.at[jnp.arange(T)[:, None], top_idx].set(top_vals)
        router_weights = jax.nn.softmax(sparse_logits, axis=-1)
        final_output = jnp.zeros_like(flat_x)
        for e in range(NUM_EXPERTS):
            expert_mask = jnp.any(top_idx == e, axis=-1)
            h = jax.nn.relu(flat_x @ W1[e] + b1[e])
            y = h @ W2[e] + b2[e]
            w = router_weights[:, e] * expert_mask.astype(x.dtype)
            final_output = final_output + y * w[:, None]
        return final_output.reshape(Bv, Sv, D)

    def _L1_xattn_ref(query, key, value, Wq, bq, Wk, bk, Wv, bv):
        import jax, jax.numpy as jnp
        import numpy as np
        B, LQ, LK = (8, 256, 256)
        QD, KD, VD = (128, 64, 64)
        q = jnp.einsum('bld,de->ble', query, Wq) + bq
        k = jnp.einsum('bld,de->ble', key, Wk) + bk
        v = jnp.einsum('bld,de->ble', value, Wv) + bv
        scores = jnp.einsum('bqe,bke->bqk', q, k)
        attn = jax.nn.softmax(scores, axis=-1)
        out = jnp.einsum('bqk,bke->bqe', attn, v)
        return out

    def _L1_ffn_ref(x, Wq, Wk, Wv, Ws, Wd, Wo):
        import jax, jax.numpy as jnp
        import numpy as np
        B, T, DIM = (2, 256, 128)
        H, DH, E, K = (16, 64, 8, 2)
        scale = DH ** (-0.5)
        q = jnp.einsum('btc,hdc->bhtd', x, Wq)
        k = jnp.einsum('btc,hdc->bhtd', x, Wk)
        gate_v = jnp.einsum('btc,hec->bthe', x, Ws)
        w, sel = jax.lax.top_k(gate_v, K)
        wsig = jax.nn.sigmoid(w)
        oh = jax.nn.one_hot(sel, E, dtype=x.dtype)
        mix_v = jnp.einsum('bthk,bthke->bthe', wsig, oh)
        proj_v = jnp.einsum('btc,edc->bted', x, Wv)
        v = jnp.einsum('bthe,bted->bhtd', mix_v, proj_v)
        scores = jnp.einsum('bhid,bhjd->bhij', q * scale, k)
        probs = jax.nn.softmax(scores, axis=-1)
        attn = jnp.einsum('bhij,bhjd->bihd', probs, v)
        gate_o = jnp.einsum('btc,hec->bthe', x, Wd)
        _, sel_o = jax.lax.top_k(gate_o, K)
        mask_o = jax.nn.one_hot(sel_o, E, dtype=x.dtype).sum(axis=3)
        res = jnp.einsum('bthe,bthd,efd->bthf', mask_o, attn, Wo)
        return res.sum(axis=2)
    x = x + _L0_xattn_ref(_layernorm(x, axis=-1), ctx_512, L0_xattn_Wk, L0_xattn_bk, L0_xattn_Wq, L0_xattn_bq, L0_xattn_Wv, L0_xattn_bv, L0_xattn_Wck, L0_xattn_bck, L0_xattn_Wcq, L0_xattn_bcq, L0_xattn_Wcv, L0_xattn_bcv, L0_xattn_Wp, L0_xattn_bp)
    x = x + _L0_ffn_ref(_layernorm(x, axis=-1), L0_ffn_W_router, L0_ffn_b_router, L0_ffn_W1, L0_ffn_b1, L0_ffn_W2, L0_ffn_b2)
    x = x + _L1_xattn_ref(_layernorm(x, axis=-1), ctx_512, ctx_512, L1_xattn_Wq, L1_xattn_bq, L1_xattn_Wk, L1_xattn_bk, L1_xattn_Wv, L1_xattn_bv)
    x = x + _L1_ffn_ref(_layernorm(x, axis=-1), L1_ffn_Wq, L1_ffn_Wk, L1_ffn_Wv, L1_ffn_Ws, L1_ffn_Wd, L1_ffn_Wo)
    return x

_drawn_inputs = setup_inputs


def setup_inputs(seed=0):
    import zlib

    import numpy as np

    out = dict(_drawn_inputs(seed))
    spreads = {'L0_xattn_bk': (0.0, 0.8),
     'L0_xattn_bq': (0.0, 0.1),
     'L0_xattn_bv': (0.0, 0.1),
     'L0_xattn_bck': (0.0, 0.8),
     'L0_xattn_bcq': (0.0, 0.1),
     'L0_xattn_bcv': (0.0, 0.1),
     'L0_xattn_bp': (0.0, 0.1),
     'L0_ffn_b_router': (0.0, 0.1),
     'L0_ffn_b1': (0.0, 0.1),
     'L0_ffn_b2': (0.0, 0.1),
     'L1_xattn_bq': (0.0, 0.8),
     'L1_xattn_bk': (0.0, 0.8),
     'L1_xattn_bv': (0.0, 0.1)}
    factors = {'L1_xattn_Wq': 4.923,
     'L1_xattn_Wk': 4.907,
     'L1_ffn_Wq': 8.0,
     'L1_ffn_Wk': 8.0,
     'L1_ffn_Ws': 2.914}
    for name, (base, spread) in spreads.items():
        noise = np.random.default_rng([zlib.crc32(name.encode()), seed]).standard_normal(out[name].shape)
        drawn = base * np.exp(spread * noise) if base else spread * noise
        out[name] = jnp.asarray(drawn.astype(out[name].dtype))
    for name, factor in factors.items():
        out[name] = (out[name] * factor).astype(out[name].dtype)
    return out
```

```python
from contextlib import ExitStack

import concourse.bass as bass
from concourse import mybir

F32 = mybir.dt.float32
F32R = mybir.dt.float32r
BF16 = mybir.dt.bfloat16
I32 = mybir.dt.int32
ALU = mybir.AluOpType
ACT = mybir.ActivationFunctionType
AX = mybir.AxisListType.X

P = 128
MASKED = -1.0e30
EPS = 1.0e-5
RSQRT_MAGIC = 0x5F3759DF
SELF, CROSS = 0, 1
Q0, K0, QC, KC = range(4)


def transformer_program(nc, a, out):
    B, T, C = a["x"].shape
    CC = a["ctx_512"].shape[2]
    H = 16
    D = C // H
    NT = T // P
    G = H // 4
    E = a["L0_ffn_W_router"].shape[1]
    F = a["L0_ffn_W1"].shape[2]
    FC = F // P
    HB, DH, _ = a["L1_ffn_Wq"].shape
    PR = HB // 2
    SC0 = float(D) ** -0.5
    SC1 = float(DH) ** -0.5
    assert (C, T, D, DH, NT, HB, E) == (P, 2 * P, 8, 64, 2, 16, 8)

    ctx = ExitStack()
    with ctx:
        def sb(name, shape, dt=F32):
            return ctx.enter_context(nc.sbuf_tensor(name, shape, dt))

        def sem(name):
            return ctx.enter_context(nc.semaphore(name))

        banks = [ctx.enter_context(nc.psum_tensor(f"bank{i}", [P, 512], F32)) for i in range(8)]
        BA, BB = banks[:4], banks[4:]

        ident = sb("ident", [P, P])
        ident_b = sb("ident_b", [P, P], BF16)
        mask_qk = sb("mask_qk", [P, P], BF16)
        mask_kq = sb("mask_kq", [P, P], BF16)
        ones = sb("ones", [1, P])
        w_stack = sb("w_stack", [P, 4, G, P])
        wv0 = sb("wv0", [P, P])
        wcv0 = sb("wcv0", [CC, P])
        wp0 = sb("wp0", [P, P])
        w_router = sb("w_router", [P, E])
        w1 = sb("w1", [P, E, F])
        w2 = sb("w2", [P, E, FC, P])
        b2 = sb("b2", [E, P])
        wq1 = sb("wq1", [P, P])
        wk1 = sb("wk1", [CC, P])
        wv1 = sb("wv1", [CC, P])
        wqk_t = sb("wqk_t", [P, 2, PR, P])
        wv_t = sb("wv_t", [P, E * DH])
        wgate_t = sb("wgate_t", [P, 2, HB * E])
        wo_t = sb("wo_t", [P, E // 2, P])
        brow = sb("brow", [1, 6, P])
        bias_c = sb("bias_c", [P, 4 * G])
        lo_c = sb("lo_c", [P, 2])
        lo_bias = sb("lo_bias", [P, 4 * G])
        b1_rows = sb("b1_rows", [E * FC, P])
        b1_c = sb("b1_c", [P, E * FC])
        bqk_rows = sb("bqk_rows", [2, P])
        bqk_c = sb("bqk_c", [P, 2])
        rank = sb("rank", [P, E])
        ident_r = sb("ident_r", [P, P], F32R)
        shift_c = sb("shift_c", [P, 1])

        x = sb("x", [P, NT, C])
        cx = sb("cx", [P, NT, CC])
        stat = sb("stat", [P, NT, 6])
        mv = sb("mv", [P, NT, 2])
        ve = sb("ve", [P, NT])
        rs_a = sb("rs_a", [P, NT])
        rs_b = sb("rs_b", [P, NT])
        rstd = sb("rstd", [P, NT])
        xn = sb("xn", [P, NT, C])
        xnT = sb("xnT", [P, T])
        cxT = sb("cxT", [CC, T])
        hi_part = sb("hi_part", [P, 4, T])
        qs = sb("qs", [P, 2, G, T], F32R)
        ks = sb("ks", [P, 2, G, T], F32R)
        DV = D + 1
        va = sb("va", [P, 2, NT, H * DV + 32 - DV])
        negmax = sb("negmax", [P, 3 * D + P + 32])
        NPA = 10
        pa = sb("pa", [P, NPA, 512])
        oT = sb("oT", [P, 2, 4, T])
        recA = sb("recA", [P, 2, H])
        yh = sb("yh", [P, 2, C])
        y = sb("y", [P, NT, C])
        yT = sb("yT", [P, T])
        lg = sb("lg", [P, NT, E])
        t_a = sb("t_a", [P, 2 * NT * HB * E])
        t_b = sb("t_b", [P, 2 * NT * HB * E])
        t_m = sb("t_m", [P, 2 * NT * HB])
        first1 = sb("first1", [P, 2 * NT * HB * E])
        first2 = sb("first2", [P, 2 * NT * HB * E])
        m1 = sb("m1", [P, NT])
        ex = sb("ex", [P, NT, E])
        wr = sb("wr", [P, NT, E])
        wrT = sb("wrT", [E, T])
        hT = pa[:, 0:4, :].rearrange("p u (c n) -> p u c n", c=2)
        q1T = sb("q1T", [P, T])
        k1T = sb("k1T", [P, T])
        v1 = sb("v1", [P, NT, P])
        nm1 = sb("nm1", [P, NT])
        rs1 = sb("rs1", [P, NT])
        rr1 = sb("rr1", [P, NT])
        p1_both = sb("p1_both", [P, 2, NT * T])
        p1 = p1_both[:, 0, :].rearrange("p (t n) -> p t n", t=NT)
        p1T = p1_both[:, 1, :].rearrange("p (t n) -> p t n", t=NT)
        gates = sb("gates", [P, 2, NT, HB * E])
        eg = sb("eg", [P, NT, HB * E])
        mix = sb("mix", [P, NT, HB * E])
        mout = sb("mout", [P, NT, HB * E])
        pvs = sb("pvs", [P, NT, E * DH])
        qk_hi = sb("qk_hi", [P, 2, PR, T], F32R)
        qk_lo = sb("qk_lo", [P, 2, PR, T], F32R)
        negc = sb("negc", [P, NT, P])
        cT = sb("cT", [P, T], F32R)
        prod = sb("prod", [P, 4 * E * DH])
        NPB = 8
        pb = pa[:, 0:NPB, :]
        vb = sb("vb", [P, NT, HB, DH + 1])
        at = sb("at", [P, NT, HB, DH + 1])
        recB = sb("recB", [P, NT * HB])
        z = p1_both[:, :, :]
        zT = pvs[:, :, :].rearrange("p t (c n) -> p t c n", c=E // 2)
        xo = sb("xo", [P, NT, C])

        bstack = oT[0:1, :, :, :].rearrange("p s j n -> p (s j n)").rearrange("p (k n) -> p k n", k=4)
        brow_raw = hi_part[0:1, 0:2, :].rearrange("p a n -> p (a n)").rearrange("p (k n) -> p k n", k=4)
        lo_row = hi_part[0:1, 2:4, :].rearrange("p a n -> p (a n)")[:, 0:3 * P].rearrange("p (k n) -> p k n", k=3)
        raw0 = prod[:, 0:4 * P].rearrange("p (k n) -> p k n", k=4)
        rawqk = pb[:, 0:4, :].rearrange("p a n -> p (a n)").rearrange("p (k r n) -> p k r n", k=2, r=PR)
        rawv = pb[:, 4, :].rearrange("p (r n) -> p r n", r=4)
        rawg = pb[:, 5, 0:2 * P].rearrange("p (r n) -> p r n", r=2)
        rawo = pb[:, 6, :].rearrange("p (e d) -> p e d", e=E)

        s_w = sem("s_w")
        s_const = sem("s_const")
        s_fill = sem("s_fill")
        s_spread = sem("s_spread")
        s_turn = sem("s_turn")
        s_turnc = sem("s_turnc")
        names = ["v_link", "a_in", "a_xn", "a_xt", "a_xc", "a_pj", "a_mh", "a_split", "a_vp", "a_vc", "a_s",
                 "a_mx", "a_ct", "a_qs", "a_st", "a_ex", "a_pv", "a_ot", "a_tr", "a_y", "a_yt", "a_yc", "a_o",
                 "a_x1", "a_lg", "a_lgc", "a_lx", "a_w", "a_h", "a_ha", "a_hd", "a_yp", "a_acc", "a_wt", "a_wtc",
                 "a_b2", "b_xn", "b_xt", "b_xc", "b_qk", "b_qc", "b_s1", "b_m1", "b_e1", "b_pt", "b_pc", "b_o1",
                 "b_g", "b_gc", "b_sg", "b_pvj", "b_pvc", "b_qkp", "b_hi", "b_lo", "b_s", "b_mx", "b_ct", "b_cc",
                 "b_st", "b_ex", "b_vm", "b_pv", "b_at", "b_z", "b_zt", "b_zc", "b_ro", "b_xo", "a_out"]
        S = {n: sem(n) for n in names}
        first_sem = min(s.num for s in S.values())
        assert max(s.num for s in S.values()) - first_sem == len(names) - 1
        seq_sems = range(first_sem, first_sem + len(names))

        with nc.Block() as block:
            loads = [
                (raw0[:, Q0, :], a["L0_xattn_Wq"]), (raw0[:, K0, :], a["L0_xattn_Wk"]),
                (raw0[:, QC, :], a["L0_xattn_Wcq"]), (raw0[0:CC, KC, :], a["L0_xattn_Wck"]),
                (brow_raw[0:1, Q0, :], a["L0_xattn_bq"].unsqueeze(0)), (brow_raw[0:1, K0, :], a["L0_xattn_bk"].unsqueeze(0)),
                (brow_raw[0:1, QC, :], a["L0_xattn_bcq"].unsqueeze(0)), (brow_raw[0:1, KC, :], a["L0_xattn_bck"].unsqueeze(0)),
                (brow[0:1, 0, :], a["L0_xattn_bv"].unsqueeze(0)), (brow[0:1, 1, :], a["L0_xattn_bcv"].unsqueeze(0)),
                (brow[0:1, 2, :], a["L0_xattn_bp"].unsqueeze(0)), (brow[0:1, 3, :], a["L1_xattn_bv"].unsqueeze(0)),
                (brow[0:1, 4, 0:E], a["L0_ffn_b_router"].unsqueeze(0)),
                (b1_rows[:, :], a["L0_ffn_b1"].rearrange("e (c n) -> (e c) n", n=P)),
                (bqk_rows[0:1, :], a["L1_xattn_bq"].unsqueeze(0)), (bqk_rows[1:2, :], a["L1_xattn_bk"].unsqueeze(0)),
                (wv0[:, :], a["L0_xattn_Wv"]), (wcv0[:, :], a["L0_xattn_Wcv"]), (wp0[:, :], a["L0_xattn_Wp"]),
                (w_router[:, :], a["L0_ffn_W_router"]), (b2[:, :], a["L0_ffn_b2"]),
                (wq1[:, :], a["L1_xattn_Wq"]), (wk1[:, :], a["L1_xattn_Wk"]), (wv1[:, :], a["L1_xattn_Wv"]),
                (rawg[:, 0, :], a["L1_ffn_Ws"].rearrange("h e c -> (h e) c")),
                (rawg[:, 1, :], a["L1_ffn_Wd"].rearrange("h e c -> (h e) c")),
                (rawv, a["L1_ffn_Wv"].rearrange("e d c -> (e d) c").rearrange("(r p) c -> p r c", p=P)),
                (rawo, a["L1_ffn_Wo"].rearrange("e f d -> f e d")),
                (rawqk[:, 0], a["L1_ffn_Wq"].rearrange("h d c -> (h d) c").rearrange("(r p) c -> p r c", p=P)),
                (rawqk[:, 1], a["L1_ffn_Wk"].rearrange("h d c -> (h d) c").rearrange("(r p) c -> p r c", p=P)),
                (w1[:, :, :], a["L0_ffn_W1"].rearrange("e c f -> c e f")),
                (w2[:, :, :, :], a["L0_ffn_W2"].rearrange("e (k p) n -> p e k n", p=P)),
            ]

            N_CONST = 4 + E + 4
            N_SPREAD = 3 + 4 * 6 + 2 + 2 + 3
            turned_to = [wqk_t[:, k, 4 * i:4 * i + 4, :].rearrange("p r n -> p (r n)") for k in range(2) for i in range(2)]
            turned_to += [wv_t[:, :], wo_t[:, :, :].rearrange("p r n -> p (r n)")]
            turned_from = [[rawqk[:, k, 4 * i + r, :] for r in range(4)] for k in range(2) for i in range(2)]
            turned_from += [[rawv[:, r, :] for r in range(4)],
                            [rawo[:, 2 * r:2 * r + 2, :].rearrange("p e d -> p (e d)") for r in range(4)]]

            @block.sync
            def _(sp):
                for dst, src in loads:
                    sp.dma_start(dst, src).then_inc(s_w, 16)

            @block.gpsimd
            def _(pool):
                nc.gpsimd.memset(ident[:, :], 0.0).then_inc(s_fill, 1)
                nc.gpsimd.memset(mask_qk[:, :], 0.0).then_inc(s_fill, 1)
                nc.gpsimd.memset(mask_kq[:, :], 0.0).then_inc(s_fill, 1)
                nc.gpsimd.memset(ones[:, :], 1.0).then_inc(s_const, 1)
                nc.gpsimd.memset(va[:, :, :, :], 0.0).then_inc(s_fill, 1)
                nc.gpsimd.memset(negmax[:, :], 0.0).then_inc(s_const, 1)
                nc.gpsimd.memset(negc[:, :, :], 0.0).then_inc(s_const, 1)
                nc.gpsimd.memset(vb[:, :, :, DH:DH + 1], 1.0).then_inc(s_const, 1)
                for e in range(E):
                    nc.gpsimd.memset(rank[:, e:e + 1], float(E - e)).then_inc(s_const, 1)
                pool.wait_ge(s_fill, 4)
                nc.gpsimd.affine_select(out=ident[:, :], in_=ident[:, :], compare_op=ALU.not_equal, fill=1.0,
                                        base=0, pattern=[[-1, P]], channel_multiplier=1).then_inc(s_const, 1)
                nc.gpsimd.affine_select(out=mask_qk[:, :], in_=mask_qk[:, :], compare_op=ALU.is_ge, fill=MASKED,
                                        base=0, pattern=[[-1, P]], channel_multiplier=1).then_inc(s_const, 1)
                nc.gpsimd.affine_select(out=mask_kq[:, :], in_=mask_kq[:, :], compare_op=ALU.is_ge, fill=MASKED,
                                        base=0, pattern=[[1, P]], channel_multiplier=-1).then_inc(s_const, 1)
                nc.gpsimd.memset(va[:, :, :, 0:H * DV].rearrange("p s t (h d) -> p s t h d", d=DV)[:, :, :, :, D:DV],
                                 1.0).then_inc(s_const, 1)

            @block.vector
            def _(dve):
                nc.vector.memset(w_stack[:, :, :, :], 0.0).then_inc(s_spread, 1)
                nc.vector.memset(bstack[:, :, :], 0.0).then_inc(s_spread, 1)
                nc.vector.memset(lo_row[:, :, :], 0.0).then_inc(s_spread, 1)
                dve.wait_ge(s_spread, 3)
                dve.wait_ge(s_w, 16 * len(loads))
                for kind in range(4):
                    rows = CC if kind == KC else P
                    w = w_stack[0:rows, kind, :, :].rearrange("p g (j r) -> p (g j) r", r=32)
                    b = bstack[:, kind, :].rearrange("p (h r) -> p h r", r=32)
                    for r in range(3):
                        nc.vector.tensor_copy(w[:, :, r * D:(r + 1) * D],
                                              raw0[0:rows, kind, :].rearrange("p (h d) -> p h d", d=D)).then_inc(s_spread, 1)
                        nc.vector.tensor_copy(b[:, :, r * D:(r + 1) * D],
                                              brow_raw[:, kind, :].rearrange("p (h d) -> p h d", d=D)).then_inc(s_spread, 1)
                    if kind in (K0, KC):
                        nc.vector.memset(b[:, :, 3 * D:3 * D + 1], 1.0).then_inc(s_spread, 1)
                nc.vector.memset(lo_row[:, 0, :].rearrange("p (j r) -> p j r", r=32)[:, :, 2 * D:3 * D], 1.0).then_inc(s_spread, 1)
                nc.vector.memset(lo_row[:, 1, :].rearrange("p (j r) -> p j r", r=32)[:, :, D:2 * D], 1.0).then_inc(s_spread, 1)
                dve.wait_ge(s_const, N_CONST)
                nc.vector.tensor_copy(ident_b[:, :], ident[:, :]).then_inc(s_spread, 1)
                nc.vector.tensor_copy(ident_r[:, :], ident[:, :]).then_inc(s_spread, 1)
                nc.vector.memset(lo_row[:, 2, :].rearrange("p (j r) -> p j r", r=32)[:, :, 3 * D:3 * D + 1], 1.0).then_inc(s_spread, 1)
                dve.wait_ge(s_turn, 1)
                nc.vector.tensor_copy(bias_c[:, :], banks[0][:, 0:4 * G]).then_inc(s_spread, 1)
                nc.vector.tensor_copy(lo_c[:, :], banks[0][:, 4 * G:4 * G + 2]).then_inc(s_spread, 1)
                nc.vector.tensor_copy(shift_c[:, :], banks[0][:, 4 * G + 2:4 * G + 3]).then_inc(s_spread, 1)
                nc.vector.tensor_copy(b1_c[:, :], banks[0][:, 32:32 + E * FC]).then_inc(s_spread, 1)
                nc.vector.tensor_copy(bqk_c[:, :], banks[0][:, 96:98]).then_inc(s_spread, 1)
                dve.wait_ge(s_spread, N_SPREAD + 5)
                for kind in range(4):
                    nc.vector.tensor_scalar(lo_bias[:, kind * G:(kind + 1) * G], bias_c[:, kind * G:(kind + 1) * G],
                                            lo_c[:, kind % 2:kind % 2 + 1], None, ALU.mult).then_inc(s_spread, 1)
                for n, dst in enumerate(turned_to):
                    dve.wait_ge(s_turn, n + 2)
                    nc.vector.tensor_copy(dst, banks[1 + n % 7][:, :]).then_inc(s_turnc, 1)

            @block.scalar
            def _(act):
                act.wait_ge(s_turn, len(turned_to) + 2)
                nc.scalar.copy(wgate_t[:, :, :].rearrange("p k n -> p (k n)"), banks[7][:, 0:2 * P]).then_inc(s_turnc, 1)

            @block.tensor
            def _(pe):
                pe.wait_ge(s_w, 16 * len(loads))
                pe.wait_ge(s_const, N_CONST)
                pe.wait_ge(s_spread, N_SPREAD)
                for i in range(4 * G):
                    pe.matmul(banks[0][:, i:i + 1], bstack[0:1, i // G, (i % G) * P:(i % G + 1) * P], ones[0:1, 0:1],
                              start=True, stop=True)
                for i in range(3):
                    pe.matmul(banks[0][:, 4 * G + i:4 * G + i + 1], lo_row[0:1, i, :], ones[0:1, 0:1], start=True, stop=True)
                pe.transpose(banks[0][:, 32:32 + E * FC], b1_rows[:, :], ident[0:E * FC, 0:E * FC])
                pe.transpose(banks[0][:, 96:98], bqk_rows[:, :], ident[0:2, 0:2]).then_inc(s_turn, 1)
                for n, srcs in enumerate(turned_from):
                    for r, src in enumerate(srcs):
                        mm = pe.transpose(banks[1 + n % 7][:, r * P:(r + 1) * P], src, ident[:, :])
                    mm.then_inc(s_turn, 1)
                for r in range(2):
                    mm = pe.transpose(banks[7][:, r * P:(r + 1) * P], rawg[:, r, :], ident[:, :])
                mm.then_inc(s_turn, 1)

        def layernorm_vector(dve, link, inp, done):
            for t in range(NT):
                link(nc.vector.bn_stats(stat[:, t, :], inp[:, t, :]), wait=(t == NT - 1))
            for t in range(NT):
                link(nc.vector.bn_aggr(mv[:, t, :], stat[:, t, :]), wait=(t == NT - 1))
            link(nc.vector.tensor_scalar(ve[:, :], mv[:, :, 1], EPS, None, ALU.add))
            link(nc.vector.tensor_scalar(rs_a[:, :].bitcast(I32), ve[:, :].bitcast(I32), 1, None, ALU.logical_shift_right))
            link(nc.vector.tensor_scalar(rstd[:, :].bitcast(I32), rs_a[:, :].bitcast(I32), -1.0, float(RSQRT_MAGIC),
                                         ALU.mult, ALU.add))
            for _ in range(4):
                link(nc.vector.tensor_tensor(rs_a[:, :], rstd[:, :], rstd[:, :], ALU.mult))
                link(nc.vector.scalar_tensor_tensor(rs_b[:, :], rs_a[:, :], -0.5, ve[:, :], ALU.mult, ALU.mult))
                link(nc.vector.scalar_tensor_tensor(rstd[:, :], rs_b[:, :], 1.5, rstd[:, :], ALU.add, ALU.mult))
            for t in range(NT):
                ins = nc.vector.tensor_scalar(xn[:, t, :], inp[:, t, :], mv[:, t, 0:1], rstd[:, t:t + 1],
                                              ALU.subtract, ALU.mult)
            ins.then_inc(done, 1)

        def top2_vector(link, vals, n):
            v = vals.rearrange("p (n e) -> p n e", e=E)
            f1 = first1[:, 0:n * E].rearrange("p (n e) -> p n e", e=E)
            f2 = first2[:, 0:n * E].rearrange("p (n e) -> p n e", e=E)
            ta = t_a[:, 0:n * E].rearrange("p (n e) -> p n e", e=E)
            tb = t_b[:, 0:n * E].rearrange("p (n e) -> p n e", e=E)
            m = t_m[:, 0:n]

            def wide(s):
                return s.unsqueeze(2).broadcast_to([P, n, E])

            ranks = rank[:, :].unsqueeze(1).broadcast_to([P, n, E])
            src = v
            for f in (f1, f2):
                link(nc.vector.tensor_reduce(m, src, AX, ALU.max))
                link(nc.vector.tensor_tensor(tb, src, wide(m), ALU.is_ge))
                link(nc.vector.tensor_tensor(tb, tb, ranks, ALU.mult))
                link(nc.vector.tensor_reduce(m, tb, AX, ALU.max))
                link(nc.vector.tensor_tensor(f, tb, wide(m), ALU.is_equal))
                if f is f1:
                    link(nc.vector.scalar_tensor_tensor(ta, f, MASKED, v, ALU.mult, ALU.add))
                    src = ta

        MAXS = [(CROSS, qt, j, gp) for qt in range(NT) for gp in range(2) for j in range(4)]
        MAXS += [(SELF, 0, j, None) for j in range(4)]
        MAXS += [(SELF, 1, j, gp) for gp in range(2) for j in range(4)]
        NS = len(MAXS)
        PER_J = 7
        assert NS == 4 * PER_J == 28

        x_tiles = a["x"].rearrange("b (t p) c -> p (b t) c", p=P)
        ctx_tiles = a["ctx_512"].rearrange("b (t p) c -> p (b t) c", p=P)
        out_tiles = out.rearrange("b (t p) c -> p (b t) c", p=P)

        with nc.Fori(0, B) as b:
            with nc.Block(no_gpsimd_drain=True) as block:

                @block.tensor
                def _(pe):
                    def turn_tokens(bank, src, done):
                        for t in range(NT):
                            mm = pe.transpose(bank[:, t * P:(t + 1) * P], src[:, t, :], ident[:, :])
                        mm.then_inc(done, 1)

                    def add_row(dst, row, stop=True):
                        return pe.matmul(dst, ones[0:1, :], row, start=False, stop=stop)

                    def add_mask(dst, mask, n):
                        return pe.matmul(dst, ident_b[:, :], mask[:, :].unsqueeze(1).broadcast_to([P, n, P]),
                                         start=False, stop=True, skip_group_check=True)

                    pe.wait_ge(S["a_in"], 32)
                    for t in range(NT):
                        pe.transpose(BA[0][0:CC, T + t * P:T + (t + 1) * P], cx[:, t, :], ident[:, :])
                    pe.wait_ge(S["a_xn"], 1)
                    turn_tokens(BA[0], xn, S["a_xt"])
                    pe.wait_ge(S["a_xc"], 2)
                    for u in range(8):
                        kind = (Q0, K0, QC, KC)[u // 2]
                        if u >= 4:
                            pe.wait_ge(S["a_split"], 2 * (u - 4) + 2)
                        for c in range(2):
                            g = 2 * (u % 2) + c
                            rows, rhs = (CC, cxT) if kind == KC else (P, xnT)
                            mm = pe.matmul(BA[u % 4][:, c * T:(c + 1) * T], w_stack[0:rows, kind, g, :], rhs[:, :],
                                           start=True, stop=True)
                        mm.then_inc(S["a_pj"], 1)
                    pe.wait_ge(S["a_split"], 10)
                    for sc in range(2):
                        for t in range(NT):
                            lhs, rhs = (xnT[:, t * P:(t + 1) * P], wv0) if sc == SELF else (cxT[:, t * P:(t + 1) * P], wcv0)
                            dst = BA[0][:, (2 * sc + t) * P:(2 * sc + t + 1) * P]
                            pe.matmul(dst, lhs, rhs[:, :], start=True, stop=False)
                            mm = add_row(dst, brow[0:1, sc, :])
                    mm.then_inc(S["a_vp"], 1)
                    pe.wait_ge(S["a_split"], 16)
                    pe.wait_ge(S["a_vc"], 1)
                    for n, (sc, qt, j, gp) in enumerate(MAXS):
                        bank = BA[n % 4]
                        if n >= 4:
                            pe.wait_ge(S["a_mx"], n - 3)
                        rows = slice(32 * j, 32 * j + 32)
                        masked = sc == SELF
                        if masked and qt == 0:
                            for g in range(4):
                                pe.matmul(bank[:, g * P:(g + 1) * P], qs[rows, sc, g, 0:P], ks[rows, sc, g, 0:P],
                                          start=(g == 0), stop=True, skip_group_check=True)
                            mm = add_mask(bank[:, :].rearrange("p (g k) -> p g k", g=4), mask_qk, 4)
                        else:
                            for c in range(2):
                                g = 2 * gp + c
                                mm = pe.matmul(bank[:, c * T:(c + 1) * T], qs[rows, sc, g, qt * P:(qt + 1) * P],
                                               ks[rows, sc, g, :], start=(c == 0), stop=True,
                                               skip_group_check=True)
                            if masked:
                                mm = add_mask(bank[:, :].rearrange("p (g k) -> p g k", g=2)[:, :, P:2 * P], mask_qk, 2)
                        mm.then_inc(S["a_s"], 1)
                    pe.wait_ge(S["a_mx"], NS)
                    for m in range(4):
                        qt, sc = m // 2, m % 2
                        for g in range(G):
                            i = (qt * 2 + sc) * G + g
                            mm = pe.transpose(BA[m][:, g * P:(g + 1) * P], negmax[:, i:i + P], ident[:, :])
                        mm.then_inc(S["a_ct"], 1)
                    pe.wait_ge(S["a_qs"], 4)

                    def values(j, sc, kt):
                        bank = BA[3] if sc == SELF else BA[2]
                        unit = PER_J * j
                        if kt == 0:
                            pe.wait_ge(S["a_ex"], unit + (PER_J if sc == SELF else 4))
                            if j >= 1:
                                pe.wait_ge(S["a_ot"], 2 * (j - 1) + (2 if sc == SELF else 1))
                        for g in range(G):
                            h = 4 * g + j
                            out_ = bank[32 * g:32 * g + 32, 0:T]
                            if sc == CROSS:
                                rhs = pa[:, (unit + g) % NPA, kt * T:(kt + 1) * T]
                            elif kt == 0:
                                rhs = pa[:, (unit + 4 + g // 2) % NPA, (g % 2) * T:(g % 2 + 1) * T]
                            else:
                                rhs = pa[:, (unit + 6) % NPA, g * P:(g + 1) * P]
                                out_ = bank[32 * g:32 * g + 32, P:T]
                            mm = pe.matmul(out_, va[:, sc, kt, h * DV:h * DV + 32], rhs, start=(kt == 0), stop=(sc == SELF or kt == 1),
                                           skip_group_check=True)
                        if kt == 1:
                            mm.then_inc(S["a_pv"], 1)

                    for n in range(NS):
                        j, k = n // PER_J, n % PER_J
                        bank = BA[n % 2]
                        rows = slice(32 * j, 32 * j + 32)
                        if n >= 2:
                            pe.wait_ge(S["a_ex"], n - 1)
                        if k < 4:
                            for kt in range(NT):
                                mm = pe.matmul(bank[:, kt * T:(kt + 1) * T], ks[rows, CROSS, k, kt * P:(kt + 1) * P],
                                               qs[rows, CROSS, k, :], start=True, stop=True)
                        elif k < 6:
                            for c in range(2):
                                g = 2 * (k - 4) + c
                                pe.matmul(bank[:, c * T:(c + 1) * T], ks[rows, SELF, g, 0:P], qs[rows, SELF, g, :],
                                          start=(c == 0), stop=True, skip_group_check=True)
                            mm = add_mask(bank[:, :].rearrange("p (g q) -> p g q", g=2)[:, :, 0:P], mask_kq, 2)
                        else:
                            for g in range(G):
                                pe.matmul(bank[:, g * P:(g + 1) * P], ks[rows, SELF, g, P:T], qs[rows, SELF, g, P:T],
                                          start=(g == 0), stop=True, skip_group_check=True)
                            mm = add_mask(bank[:, :].rearrange("p (g q) -> p g q", g=4), mask_kq, 4)
                        mm.then_inc(S["a_st"], 1)
                        if j >= 1 and k in (1, 2, 3, 4):
                            values(j - 1, (CROSS, CROSS, SELF, SELF)[k - 1], (k - 1) % 2)
                    for i in range(4):
                        values(3, (CROSS, CROSS, SELF, SELF)[i], i % 2)
                    pe.wait_ge(S["a_ot"], 8)
                    for m in range(4):
                        qt, sc = m // 2, m % 2
                        for j in range(4):
                            mm = pe.transpose(BA[m][:, j * P:(j + 1) * P], oT[:, sc, j, qt * P:(qt + 1) * P], ident[:, :])
                        mm.then_inc(S["a_tr"], 1)
                    pe.wait_ge(S["a_y"], 2)
                    turn_tokens(BA[0], y, S["a_yt"])
                    pe.wait_ge(S["a_yc"], 1)
                    for t in range(NT):
                        dst = BA[1][:, t * P:(t + 1) * P]
                        pe.matmul(dst, yT[:, t * P:(t + 1) * P], wp0[:, :], start=True, stop=False)
                        mm = add_row(dst, brow[0:1, 2, :])
                    mm.then_inc(S["a_o"], 1)

                    pe.wait_ge(S["a_xn"], 2)
                    turn_tokens(BA[2], xn, S["a_xt"])
                    pe.wait_ge(S["a_xc"], 3)
                    for t in range(NT):
                        dst = BA[3][:, t * E:(t + 1) * E]
                        pe.matmul(dst, xnT[:, t * P:(t + 1) * P], w_router[:, :], start=True, stop=False)
                        mm = add_row(dst, brow[0:1, 4, 0:E])
                    mm.then_inc(S["a_lg"], 1)

                    def hidden(u):
                        e, fp = u // 2, u % 2
                        if u >= 2:
                            pe.wait_ge(S["a_ha"] if u % 2 == 0 else S["a_hd"], u // 2)
                        for c in range(2):
                            f = (2 * fp + c) * P
                            mm = pe.matmul(BA[u % 2][:, c * T:(c + 1) * T], w1[:, e, f:f + P], xnT[:, :],
                                           start=True, stop=True)
                        mm.then_inc(S["a_h"], 1)

                    def expert_out(e):
                        pe.wait_ge(S["a_ha"], e + 1)
                        pe.wait_ge(S["a_hd"], e + 1)
                        if e == 1:
                            pe.wait_ge(S["a_lgc"], 1)
                        if e >= 2:
                            pe.wait_ge(S["a_acc"], e - 1)
                        for t in range(NT):
                            for f in range(FC):
                                mm = pe.matmul(BA[2 + e % 2][:, t * P:(t + 1) * P],
                                               hT[:, (2 * e + f // 2) % 4, f % 2, t * P:(t + 1) * P], w2[:, e, f, :],
                                               start=(f == 0), stop=(f == FC - 1))
                        mm.then_inc(S["a_yp"], 1)

                    hidden(0)
                    hidden(1)
                    for e in range(E):
                        if e + 1 < E:
                            hidden(2 * e + 2)
                            hidden(2 * e + 3)
                        expert_out(e)
                    pe.wait_ge(S["a_w"], 1)
                    pe.wait_ge(S["a_ha"], E)
                    pe.wait_ge(S["a_hd"], E)
                    for t in range(NT):
                        mm = pe.transpose(BA[0][0:E, t * P:(t + 1) * P], wr[:, t, :], ident[:, :])
                    mm.then_inc(S["a_wt"], 1)
                    pe.wait_ge(S["a_wtc"], 1)
                    for t in range(NT):
                        mm = pe.matmul(BA[1][:, t * P:(t + 1) * P], wrT[:, t * P:(t + 1) * P], b2[:, :], start=True, stop=True)
                    mm.then_inc(S["a_b2"], 1)

                    for t in range(NT):
                        pe.transpose(BB[0][0:CC, T + t * P:T + (t + 1) * P], cx[:, t, :], ident[:, :])
                    pe.wait_ge(S["b_xn"], 1)
                    turn_tokens(BB[0], xn, S["b_xt"])
                    pe.wait_ge(S["b_xc"], 2)
                    pe.matmul(BB[1][:, 0:T], wq1[:, :], xnT[:, :], start=True, stop=True)
                    pe.matmul(BB[1][:, T:2 * T], wk1[:, :], cxT[:, :], start=True, stop=True).then_inc(S["b_qk"], 1)
                    for t in range(NT):
                        dst = BB[2][:, t * P:(t + 1) * P]
                        pe.matmul(dst, cxT[:, t * P:(t + 1) * P], wv1[:, :], start=True, stop=False)
                        mm = add_row(dst, brow[0:1, 3, :])
                    mm.then_inc(S["b_qk"], 1)
                    pe.wait_ge(S["b_qc"], 2)
                    for t in range(NT):
                        mm = pe.matmul(BB[3][:, t * T:(t + 1) * T], q1T[:, t * P:(t + 1) * P], k1T[:, :], start=True, stop=True)
                    mm.then_inc(S["b_s1"], 1)
                    pe.wait_ge(S["b_e1"], 2)
                    for kt in range(NT):
                        for qt in range(NT):
                            mm = pe.transpose(BB[0][:, kt * T + qt * P:kt * T + (qt + 1) * P], p1[:, qt, kt * P:(kt + 1) * P],
                                              ident[:, :])
                    mm.then_inc(S["b_pt"], 1)
                    pe.wait_ge(S["b_pc"], 1)
                    pe.wait_ge(S["b_qc"], 3)
                    for qt in range(NT):
                        for kt in range(NT):
                            mm = pe.matmul(BB[1][:, qt * P:(qt + 1) * P], p1T[:, kt, qt * P:(qt + 1) * P], v1[:, kt, :],
                                           start=(kt == 0), stop=(kt == 1))
                    mm.then_inc(S["b_o1"], 1)

                    pe.wait_ge(S["b_xn"], 2)
                    turn_tokens(BB[2], xn, S["b_xt"])
                    pe.wait_ge(S["b_xc"], 3)
                    for t in range(NT):
                        mm = pe.matmul(BB[3][:, t * T:(t + 1) * T], xnT[:, t * P:(t + 1) * P],
                                       wgate_t[:, :, :].rearrange("p k n -> p (k n)"), start=True, stop=True)
                    mm.then_inc(S["b_g"], 1)
                    for t in range(NT):
                        pe.matmul(BB[t][:, :], xnT[:, t * P:(t + 1) * P], wv_t[:, :], start=True, stop=True).then_inc(S["b_pvj"], 1)
                    for u in range(8):
                        if u == 1:
                            pe.wait_ge(S["b_gc"], 1)
                        elif u in (2, 3):
                            pe.wait_ge(S["b_pvc"], u - 1)
                        elif u >= 4:
                            pe.wait_ge(S["b_lo"], u - 3)
                        for c in range(2):
                            mm = pe.matmul(BB[(u + 2) % 4][:, c * T:(c + 1) * T], wqk_t[:, u // 4, 2 * (u % 4) + c, :],
                                           xnT[:, :], start=True, stop=True)
                        mm.then_inc(S["b_qkp"], 1)
                    pe.wait_ge(S["b_lo"], 8)
                    for n in range(16):
                        qt, pp, j = n // 8, (n // 2) % 4, n % 2
                        rows = slice(64 * j, 64 * j + 64)
                        if n >= 4:
                            pe.wait_ge(S["b_mx"], n - 3)
                        for c in range(2):
                            mm = pe.matmul(BB[(n + 2) % 4][:, c * T:(c + 1) * T],
                                           qk_hi[rows, 0, 2 * pp + c, qt * P:(qt + 1) * P], qk_hi[rows, 1, 2 * pp + c, :],
                                           start=True, stop=True)
                        mm.then_inc(S["b_s"], 1)
                    pe.wait_ge(S["b_mx"], 16)
                    turn_tokens(BB[2], negc, S["b_ct"])
                    pe.wait_ge(S["b_cc"], 1)
                    def shifted_scores(h):
                        pr, rows = h // 2, slice(64 * (h % 2), 64 * (h % 2) + 64)
                        if h >= 2:
                            pe.wait_ge(S["b_ex"], h - 1)
                        bank = BB[h % 2]
                        c = 64 * (h % 2) + h
                        for kt in range(NT):
                            keys = slice(kt * P, (kt + 1) * P)
                            dst = bank[:, kt * T:(kt + 1) * T]
                            pe.matmul(dst, qk_lo[rows, 1, pr, keys], qk_hi[rows, 0, pr, :], start=(kt == 0), stop=False,
                                      skip_group_check=True)
                            pe.matmul(dst, qk_hi[rows, 1, pr, keys], qk_lo[rows, 0, pr, :], start=False, stop=False,
                                      skip_group_check=True)
                            pe.matmul(dst, qk_hi[rows, 1, pr, keys], qk_hi[rows, 0, pr, :], start=False, stop=True,
                                      skip_group_check=True)
                        mm = pe.matmul(bank[:, :].rearrange("p (k q) -> p k q", k=NT), ident_r[rows, c:c + 1].broadcast_to([64, P]),
                                       cT[rows, :].unsqueeze(1).broadcast_to([64, NT, T]), start=False, stop=True,
                                       skip_group_check=True)
                        mm.then_inc(S["b_st"], 1)

                    def mixed_values(hg):
                        pe.wait_ge(S["b_vm"], NT * HB // 4)
                        pe.wait_ge(S["b_ex"], 4 * hg + 4)
                        for qt in range(NT):
                            if hg >= 1:
                                pe.wait_ge(S["b_at"], 2 * (hg - 1) + qt + 1)
                            for i in range(4):
                                h = 4 * hg + i
                                for kt in range(NT):
                                    mm = pe.matmul(BB[2 + qt][:, i * (DH + 1):(i + 1) * (DH + 1)],
                                                   pb[:, h % NPB, kt * T + qt * P:kt * T + (qt + 1) * P], vb[:, kt, h, :],
                                                   start=(kt == 0), stop=(kt == 1))
                            mm.then_inc(S["b_pv"], 1)

                    for h in range(HB):
                        shifted_scores(h)
                        if h >= NPB - 1 and h % 4 == 3:
                            mixed_values(h // 4 - 1)
                    mixed_values(3)
                    for qt in range(NT):
                        pe.wait_ge(S["b_z"], (E // 2) * (qt + 1))
                        for c in range(E // 2):
                            mm = pe.transpose(BB[qt][:, c * P:(c + 1) * P], z[:, qt, c * P:(c + 1) * P], ident[:, :])
                        mm.then_inc(S["b_zt"], 1)
                    for qt in range(NT):
                        pe.wait_ge(S["b_zc"], qt + 1)
                        pe.wait_ge(S["b_at"], 8)
                        for c in range(E // 2):
                            mm = pe.matmul(BB[2 + qt][:, 0:P], zT[:, qt, c, :], wo_t[:, c, :],
                                           start=(c == 0), stop=(c == E // 2 - 1))
                        mm.then_inc(S["b_ro"], 1)

                @block.scalar
                def _(act):
                    act.wait_ge(S["a_xt"], 1)
                    nc.scalar.copy(xnT[:, :], BA[0][:, 0:T]).then_inc(S["a_xc"], 1)
                    nc.scalar.copy(cxT[:, :], BA[0][0:CC, T:2 * T]).then_inc(S["a_xc"], 1)
                    for n in range(16):
                        u, c = n // 2, n % 2
                        kind, g = (Q0, K0, QC, KC)[u // 2], 2 * (u % 2) + c
                        act.wait_ge(S["a_pj"], u + 1)
                        if n >= 4:
                            act.wait_ge(S["a_split"], n - 3)
                        nc.scalar.activation(hi_part[:, n % 4, :].bitcast(F32R), BA[u % 4][:, c * T:(c + 1) * T], ACT.Identity,
                                             bias=lo_bias[:, kind * G + g:kind * G + g + 1],
                                             scale=lo_c[:, kind % 2:kind % 2 + 1]).then_inc(S["a_mh"], 1)
                    act.wait_ge(S["a_vp"], 1)
                    nc.scalar.copy(va[:, :, :, 0:H * DV].rearrange("p s t (h d) -> p (s t) h d", d=DV)[:, :, :, 0:D],
                                   BA[0][:, :].rearrange("p (a h d) -> p a h d", a=4, d=D)).then_inc(S["a_vc"], 1)
                    for n in range(NS):
                        j = n // PER_J
                        act.wait_ge(S["a_st"], n + 1)
                        if n >= NPA:
                            old = n - NPA
                            act.wait_ge(S["a_pv"], 2 * (old // PER_J) + (1 if old % PER_J < 4 else 2))
                        nc.scalar.activation(pa[:, n % NPA, :], BA[n % 2][:, :], ACT.Exp, scale=SC0).then_inc(S["a_ex"], 1)
                    act.wait_ge(S["a_yt"], 1)
                    nc.scalar.copy(yT[:, :], BA[0][:, 0:T]).then_inc(S["a_yc"], 1)
                    act.wait_ge(S["a_xt"], 2)
                    nc.scalar.copy(xnT[:, :], BA[2][:, 0:T]).then_inc(S["a_xc"], 1)
                    act.wait_ge(S["a_lx"], 1)
                    nc.scalar.activation(ex[:, :, :], ex[:, :, :], ACT.Exp).then_inc(S["a_lx"], 1)
                    for e in range(E):
                        u = 2 * e
                        act.wait_ge(S["a_h"], u + 1)
                        if e >= 2:
                            act.wait_ge(S["a_yp"], e - 1)
                        for c in range(2):
                            ins = nc.scalar.activation(hT[:, u % 4, c, :], BA[0][:, c * T:(c + 1) * T], ACT.Relu,
                                                       bias=b1_c[:, e * FC + c:e * FC + c + 1])
                        ins.then_inc(S["a_ha"], 1)
                    act.wait_ge(S["b_xt"], 1)
                    nc.scalar.copy(xnT[:, :], BB[0][:, 0:T]).then_inc(S["b_xc"], 1)
                    nc.scalar.copy(cxT[:, :], BB[0][0:CC, T:2 * T]).then_inc(S["b_xc"], 1)
                    act.wait_ge(S["b_qk"], 1)
                    nc.scalar.activation(q1T[:, :], BB[1][:, 0:T], ACT.Identity, bias=bqk_c[:, 0:1]).then_inc(S["b_qc"], 1)
                    nc.scalar.activation(k1T[:, :], BB[1][:, T:2 * T], ACT.Identity, bias=bqk_c[:, 1:2]).then_inc(S["b_qc"], 1)
                    act.wait_ge(S["b_qk"], 2)
                    nc.scalar.copy(v1[:, :, :].rearrange("p t n -> p (t n)"), BB[2][:, 0:2 * P]).then_inc(S["b_qc"], 1)
                    act.wait_ge(S["b_m1"], 1)
                    for t in range(NT):
                        nc.scalar.activation(p1[:, t, :], BB[3][:, t * T:(t + 1) * T], ACT.Exp, bias=nm1[:, t:t + 1],
                                             accum_out=rs1[:, t:t + 1]).then_inc(S["b_e1"], 1)
                    act.wait_ge(S["b_pt"], 1)
                    nc.scalar.copy(p1T[:, :, :].rearrange("p t n -> p (t n)"), BB[0][:, :]).then_inc(S["b_pc"], 1)
                    act.wait_ge(S["b_xt"], 2)
                    nc.scalar.copy(xnT[:, :], BB[2][:, 0:T]).then_inc(S["b_xc"], 1)
                    for t in range(NT):
                        act.wait_ge(S["b_pvj"], t + 1)
                        nc.scalar.copy(pvs[:, t, :], BB[t][:, :]).then_inc(S["b_pvc"], 1)
                    for u in range(8):
                        act.wait_ge(S["b_qkp"], u + 1)
                        r = 2 * (u % 4)
                        nc.scalar.copy(qk_hi[:, u // 4, r:r + 2, :].rearrange("p r n -> p (r n)"),
                                       BB[(u + 2) % 4][:, :]).then_inc(S["b_hi"], 1)
                    act.wait_ge(S["b_gc"], 1)
                    nc.scalar.activation(eg[:, :, :], gates[:, 0, :, :], ACT.Exp, scale=-1.0).then_inc(S["b_sg"], 1)

                    def exponentials(h):
                        act.wait_ge(S["b_st"], h + 1)
                        if h >= NPB:
                            act.wait_ge(S["b_pv"], 2 * ((h - NPB) // 4 + 1))
                        nc.scalar.activation(pb[:, h % NPB, :], BB[h % 2][:, :], ACT.Exp, scale=SC1).then_inc(S["b_ex"], 1)

                    def head_outputs(hg):
                        for qt in range(NT):
                            act.wait_ge(S["b_pv"], 2 * hg + qt + 1)
                            nc.scalar.copy(at[:, qt, 4 * hg:4 * hg + 4, :].rearrange("p h d -> p (h d)"),
                                           BB[2 + qt][:, 0:4 * (DH + 1)]).then_inc(S["b_at"], 1)

                    for h in range(12):
                        exponentials(h)
                    head_outputs(0)
                    for h in range(12, HB):
                        exponentials(h)
                    for hg in range(1, 4):
                        head_outputs(hg)
                    for qt in range(NT):
                        act.wait_ge(S["b_zt"], qt + 1)
                        nc.scalar.copy(zT[:, qt, :, :].rearrange("p c n -> p (c n)"), BB[qt][:, :]).then_inc(S["b_zc"], 1)

                @block.vector
                def _(dve):
                    chain = [0]

                    def link(ins, wait=True):
                        chain[0] += 1
                        ins.then_inc(S["v_link"], 1)
                        if wait:
                            dve.wait_ge(S["v_link"], chain[0])

                    dve.wait_ge(S["a_in"], 32)
                    layernorm_vector(dve, link, x, S["a_xn"])
                    for u in range(8):
                        kind = (Q0, K0, QC, KC)[u // 2]
                        dve.wait_ge(S["a_mh"], 2 * u + 2)
                        for c in range(2):
                            n, g = 2 * u + c, 2 * (u % 2) + c
                            stack = qs if kind in (Q0, QC) else ks
                            nc.vector.scalar_tensor_tensor(stack[:, kind // 2, g, :], BA[u % 4][:, c * T:(c + 1) * T],
                                                           bias_c[:, kind * G + g:kind * G + g + 1], hi_part[:, n % 4, :],
                                                           ALU.add, ALU.subtract).then_inc(S["a_split"], 1)
                    for n, (sc, qt, j, gp) in enumerate(MAXS):
                        dve.wait_ge(S["a_s"], n + 1)
                        g0, ng = (0, 4) if gp is None else (2 * gp, 2)
                        i = 3 * D + 32 * j + (qt * 2 + sc) * G + g0
                        nc.vector.tensor_reduce(negmax[:, i:i + ng],
                                                BA[n % 4][:, :].rearrange("p (g k) -> p g k", g=ng), AX, ALU.max,
                                                negate=True).then_inc(S["a_mx"], 1)
                    for m in range(4):
                        qt, sc = m // 2, m % 2
                        dve.wait_ge(S["a_ct"], m + 1)
                        dst = qs[:, sc, :, qt * P:(qt + 1) * P]
                        nc.vector.scalar_tensor_tensor(dst, BA[m][:, :].rearrange("p (g q) -> p g q", g=G), shift_c[:, 0:1],
                                                       dst.bitcast(F32), ALU.mult, ALU.add).then_inc(S["a_qs"], 1)
                    for i in range(8):
                        sc = CROSS if i % 2 == 0 else SELF
                        dve.wait_ge(S["a_pv"], i + 1)
                        nc.vector.tensor_copy(oT[:, sc, i // 2, :], BA[2 + i % 2][:, 0:T]).then_inc(S["a_ot"], 1)
                    for qt in range(NT):
                        dve.wait_ge(S["a_tr"], 2 * qt + 2)
                        heads = [BA[2 * qt + sc][:, :].rearrange("p (h r) -> p h r", r=32) for sc in range(2)]
                        for sc in range(2):
                            link(nc.vector.reciprocal(recA[:, sc, :], heads[sc][:, :, D]), wait=(sc == 1))
                        for sc in range(2):
                            link(nc.vector.tensor_tensor(
                                yh[:, sc, :].rearrange("p (g j d) -> p j g d", g=G, j=4),
                                heads[sc][:, :, 0:D].rearrange("p (j g) d -> p j g d", j=4),
                                recA[:, sc, :].rearrange("p (j g) -> p j g", j=4).unsqueeze(3).broadcast_to([P, 4, G, D]),
                                ALU.mult), wait=(sc == 1))
                        nc.vector.tensor_tensor(y[:, qt, :], yh[:, 0, :], yh[:, 1, :], ALU.add).then_inc(S["a_y"], 1)
                        dve.wait_ge(S["a_y"], qt + 1)
                    dve.wait_ge(S["a_o"], 1)
                    link(nc.vector.tensor_tensor(x[:, :, :], x[:, :, :], BA[1][:, 0:T].rearrange("p (t n) -> p t n", t=NT), ALU.add))
                    layernorm_vector(dve, link, x, S["a_xn"])
                    dve.wait_ge(S["a_lg"], 1)
                    lgf = lg[:, :, :].rearrange("p t e -> p (t e)")
                    nc.vector.tensor_copy(lgf, BA[3][:, 0:NT * E]).then_inc(S["a_lgc"], 1)
                    dve.wait_ge(S["a_lgc"], 1)
                    top = lg[:, :, :]
                    link(nc.vector.tensor_reduce(m1[:, :], top, AX, ALU.max))
                    nc.vector.tensor_tensor(ex[:, :, :], top, m1[:, :].unsqueeze(2).broadcast_to([P, NT, E]),
                                            ALU.subtract).then_inc(S["a_lx"], 1)
                    top2_vector(link, lgf, NT)
                    f1, f2 = first1[:, 0:NT * E], first2[:, 0:NT * E]
                    link(nc.vector.tensor_tensor(f1, f1, f2, ALU.add))
                    dve.wait_ge(S["a_lx"], 2)
                    link(nc.vector.tensor_tensor(ex[:, :, :], ex[:, :, :], f1.rearrange("p (t e) -> p t e", e=E), ALU.mult))
                    link(nc.vector.tensor_reduce(m1[:, :], ex[:, :, :], AX, ALU.add))
                    link(nc.vector.reciprocal(m1[:, :], m1[:, :]))
                    nc.vector.tensor_tensor(wr[:, :, :], ex[:, :, :], m1[:, :].unsqueeze(2).broadcast_to([P, NT, E]),
                                            ALU.mult).then_inc(S["a_w"], 1)
                    dve.wait_ge(S["a_w"], 1)

                    def hidden_relu(e):
                        u = 2 * e + 1
                        dve.wait_ge(S["a_h"], u + 1)
                        if e >= 2:
                            dve.wait_ge(S["a_yp"], e - 1)
                        for c in range(2):
                            k = e * FC + 2 + c
                            ins = nc.vector.tensor_scalar(hT[:, u % 4, c, :], BA[1][:, c * T:(c + 1) * T], b1_c[:, k:k + 1], 0.0,
                                                          ALU.add, ALU.max)
                        ins.then_inc(S["a_hd"], 1)

                    def accumulate(e):
                        dve.wait_ge(S["a_yp"], e + 1)
                        if e >= 1:
                            dve.wait_ge(S["a_acc"], e)
                        for t in range(NT):
                            ins = nc.vector.scalar_tensor_tensor(x[:, t, :], BA[2 + e % 2][:, t * P:(t + 1) * P],
                                                                 wr[:, t, e:e + 1], x[:, t, :], ALU.mult, ALU.add)
                        ins.then_inc(S["a_acc"], 1)

                    for e in range(E):
                        hidden_relu(e)
                        if e >= 1:
                            accumulate(e - 1)
                    accumulate(E - 1)
                    dve.wait_ge(S["a_wt"], 1)
                    nc.vector.tensor_copy(wrT[:, :], BA[0][0:E, 0:T]).then_inc(S["a_wtc"], 1)
                    dve.wait_ge(S["a_b2"], 1)
                    dve.wait_ge(S["a_acc"], E)
                    link(nc.vector.tensor_tensor(x[:, :, :], x[:, :, :], BA[1][:, 0:T].rearrange("p (t n) -> p t n", t=NT), ALU.add))
                    layernorm_vector(dve, link, x, S["b_xn"])
                    dve.wait_ge(S["b_s1"], 1)
                    nc.vector.tensor_reduce(nm1[:, :], BB[3][:, :].rearrange("p (t k) -> p t k", t=NT), AX, ALU.max,
                                            negate=True).then_inc(S["b_m1"], 1)
                    dve.wait_ge(S["b_e1"], 2)
                    link(nc.vector.reciprocal(rr1[:, :], rs1[:, :]))
                    dve.wait_ge(S["b_o1"], 1)
                    for t in range(NT):
                        link(nc.vector.scalar_tensor_tensor(x[:, t, :], BB[1][:, t * P:(t + 1) * P], rr1[:, t:t + 1],
                                                            x[:, t, :], ALU.mult, ALU.add), wait=(t == 1))
                    layernorm_vector(dve, link, x, S["b_xn"])
                    dve.wait_ge(S["b_g"], 1)
                    nc.vector.tensor_copy(gates[:, :, :, :].rearrange("p k t n -> p t k n"),
                                          BB[3][:, :].rearrange("p (t k n) -> p t k n", t=NT, k=2)).then_inc(S["b_gc"], 1)
                    for u in range(8):
                        r = 2 * (u % 4)
                        lo = qk_lo[:, u // 4, r:r + 2, :].rearrange("p r n -> p (r n)")
                        hi = qk_hi[:, u // 4, r:r + 2, :].rearrange("p r n -> p (r n)")
                        dve.wait_ge(S["b_hi"], u + 1)
                        nc.vector.tensor_tensor(lo, BB[(u + 2) % 4][:, :], hi.bitcast(F32), ALU.subtract).then_inc(S["b_lo"], 1)
                    for n in range(16):
                        qt, pp, j = n // 8, (n // 2) % 4, n % 2
                        c = 64 * j + 4 * pp + j
                        dve.wait_ge(S["b_s"], n + 1)
                        nc.vector.tensor_reduce(negc[:, qt, c:c + 3:2], BB[(n + 2) % 4][:, :].rearrange("p (h k) -> p h k", h=2),
                                                AX, ALU.max, negate=True).then_inc(S["b_mx"], 1)
                    dve.wait_ge(S["b_ct"], 1)
                    nc.vector.tensor_copy(cT[:, :], BB[2][:, 0:T]).then_inc(S["b_cc"], 1)
                    dve.wait_ge(S["b_gc"], 1)
                    n_rows = 2 * NT * HB
                    top2_vector(link, gates[:, :, :, :].rearrange("p k t n -> p (k t n)"), n_rows)
                    link(nc.vector.tensor_tensor(first1[:, :], first1[:, :], first2[:, :], ALU.add))
                    chosen = first1[:, :].rearrange("p (k t n) -> p k t n", k=2, t=NT)
                    dve.wait_ge(S["b_sg"], 1)
                    link(nc.vector.tensor_scalar(eg[:, :, :], eg[:, :, :], 1.0, None, ALU.add))
                    link(nc.vector.reciprocal(eg[:, :, :], eg[:, :, :]))
                    link(nc.vector.tensor_tensor(mix[:, :, :], eg[:, :, :], chosen[:, 0], ALU.mult))
                    dve.wait_ge(S["b_pvc"], 2)
                    for t in range(NT):
                        for hg in range(HB // 4):
                            n = 4 * t + hg
                            heads = prod[:, :].rearrange("p (h d e) -> p h d e", h=4, d=DH)
                            link(nc.vector.tensor_tensor(
                                heads,
                                mix[:, t, 4 * hg * E:4 * (hg + 1) * E].rearrange("p (h e) -> p h e", e=E).unsqueeze(2)
                                .broadcast_to([P, 4, DH, E]),
                                pvs[:, t, :].rearrange("p (e d) -> p d e", e=E).unsqueeze(1).broadcast_to([P, 4, DH, E]),
                                ALU.mult))
                            nc.vector.tensor_reduce(vb[:, t, 4 * hg:4 * (hg + 1), 0:DH], heads, AX, ALU.add).then_inc(S["b_vm"], 1)
                            dve.wait_ge(S["b_vm"], n + 1)
                    dve.wait_ge(S["b_at"], 8)
                    link(nc.vector.reciprocal(recB[:, :], at[:, :, :, DH].rearrange("p t h -> p (t h)")))
                    link(nc.vector.tensor_tensor(mout[:, :, :].rearrange("p t (h e) -> p (t h) e", e=E),
                                                 chosen[:, 1].rearrange("p t (h e) -> p (t h) e", e=E),
                                                 recB[:, :].unsqueeze(2).broadcast_to([P, NT * HB, E]), ALU.mult))
                    for t in range(NT):
                        for c in range(E // 2):
                            n = (E // 2) * t + c
                            pair = prod[:, :].rearrange("p (e d h) -> p e d h", e=2, d=DH)
                            link(nc.vector.tensor_tensor(
                                pair,
                                mout[:, t, :].rearrange("p (h e) -> p e h", e=E)[:, 2 * c:2 * c + 2, :].unsqueeze(2)
                                .broadcast_to([P, 2, DH, HB]),
                                at[:, t, :, 0:DH].rearrange("p h d -> p d h").unsqueeze(1).broadcast_to([P, 2, DH, HB]),
                                ALU.mult))
                            nc.vector.tensor_reduce(z[:, t, c * P:(c + 1) * P].rearrange("p (e d) -> p e d", e=2), pair,
                                                    AX, ALU.add).then_inc(S["b_z"], 1)
                            dve.wait_ge(S["b_z"], n + 1)
                    for t in range(NT):
                        dve.wait_ge(S["b_ro"], t + 1)
                        nc.vector.tensor_tensor(xo[:, t, :], x[:, t, :], BB[2 + t][:, 0:P], ALU.add).then_inc(S["b_xo"], 1)

                @block.sync
                def _(sp):
                    sp.dma_start(x[:, :, :], x_tiles[:, bass.ds(b * NT, NT), :]).then_inc(S["a_in"], 16)
                    sp.dma_start(cx[:, :, :], ctx_tiles[:, bass.ds(b * NT, NT), :]).then_inc(S["a_in"], 16)
                    sp.wait_ge(S["b_xo"], NT)
                    sp.dma_start(out_tiles[:, bass.ds(b * NT, NT), :],
                                 xo[:, :, :]).then_inc(S["a_out"], 16)
                    sp.wait_ge(S["a_out"], 16)

            nc.all_engine_barrier(sems_to_clear=seq_sems)


_INS = ['x', 'ctx_512', 'L0_xattn_Wk', 'L0_xattn_bk', 'L0_xattn_Wq', 'L0_xattn_bq', 'L0_xattn_Wv', 'L0_xattn_bv',
        'L0_xattn_Wck', 'L0_xattn_bck', 'L0_xattn_Wcq', 'L0_xattn_bcq', 'L0_xattn_Wcv', 'L0_xattn_bcv', 'L0_xattn_Wp',
        'L0_xattn_bp', 'L0_ffn_W_router', 'L0_ffn_b_router', 'L0_ffn_W1', 'L0_ffn_b1', 'L0_ffn_W2', 'L0_ffn_b2',
        'L1_xattn_Wq', 'L1_xattn_bq', 'L1_xattn_Wk', 'L1_xattn_bk', 'L1_xattn_Wv', 'L1_xattn_bv', 'L1_ffn_Wq',
        'L1_ffn_Wk', 'L1_ffn_Wv', 'L1_ffn_Ws', 'L1_ffn_Wd', 'L1_ffn_Wo']


def kernel(**inputs):
    import numpy as _np
    import concourse.bacc as _bacc
    from concourse import mybir as _mybir
    from concourse.bass_utils import run_bass_kernel_spmd as _run

    nc = _bacc.Bacc("TRN2", target_bir_lowering=False, num_devices=1)
    arrays, aps = {}, {}
    for name in _INS:
        v = _np.ascontiguousarray(inputs[name])
        arrays[f"in_{name}_dram"] = v
        aps[name] = nc.dram_tensor(f"in_{name}_dram", v.shape, _mybir.dt.from_np(v.dtype), kind="ExternalInput").ap()
    out = nc.dram_tensor("out_0_dram", inputs["x"].shape, _mybir.dt.float32, kind="ExternalOutput").ap()
    transformer_program(nc, aps, out)
    r = _run(nc, [arrays], core_ids=[0])
    return r.results[0]["out_0_dram"]
```

```python
from contextlib import ExitStack

import concourse.bass as bass
from concourse import mybir

F32 = mybir.dt.float32
F32R = mybir.dt.float32r
BF16 = mybir.dt.bfloat16
I32 = mybir.dt.int32
ALU = mybir.AluOpType
ACT = mybir.ActivationFunctionType
AX = mybir.AxisListType.X

P = 128
MASKED = -1.0e30
EPS = 1.0e-5
RSQRT_MAGIC = 0x5F3759DF
SELF, CROSS = 0, 1
Q0, K0, QC, KC = range(4)


def transformer_program(nc, a, out):
    B, T, C = a["x"].shape
    CC = a["ctx_512"].shape[2]
    H = 16
    D = C // H
    NT = T // P
    G = H // 4
    E = a["L0_ffn_W_router"].shape[1]
    F = a["L0_ffn_W1"].shape[2]
    FC = F // P
    HB, DH, _ = a["L1_ffn_Wq"].shape
    PR = HB // 2
    SC0 = float(D) ** -0.5
    SC1 = float(DH) ** -0.5
    assert (C, T, D, DH, NT, HB, E) == (P, 2 * P, 8, 64, 2, 16, 8)

    ctx = ExitStack()
    with ctx:
        def sb(name, shape, dt=F32):
            return ctx.enter_context(nc.sbuf_tensor(name, shape, dt))

        def sem(name):
            return ctx.enter_context(nc.semaphore(name))

        banks = [ctx.enter_context(nc.psum_tensor(f"bank{i}", [P, 512], F32)) for i in range(8)]
        BA, BB = banks[:4], banks[4:]

        ident = sb("ident", [P, P])
        ident_b = sb("ident_b", [P, P], BF16)
        mask_qk = sb("mask_qk", [P, P], BF16)
        mask_kq = sb("mask_kq", [P, P], BF16)
        ones = sb("ones", [1, P])
        w_stack = sb("w_stack", [P, 4, G, P])
        wv0 = sb("wv0", [P, P])
        wcv0 = sb("wcv0", [CC, P])
        wp0 = sb("wp0", [P, P])
        w_router = sb("w_router", [P, E])
        w1 = sb("w1", [P, E, F])
        w2 = sb("w2", [P, E, FC, P])
        b2 = sb("b2", [E, P])
        wq1 = sb("wq1", [P, P])
        wk1 = sb("wk1", [CC, P])
        wv1 = sb("wv1", [CC, P])
        wqk_t = sb("wqk_t", [P, 2, PR, P])
        wv_t = sb("wv_t", [P, E * DH])
        wgate_t = sb("wgate_t", [P, 2, HB * E])
        wo_t = sb("wo_t", [P, E // 2, P])
        brow = sb("brow", [1, 6, P])
        bias_c = sb("bias_c", [P, 4 * G])
        lo_c = sb("lo_c", [P, 2])
        lo_bias = sb("lo_bias", [P, 4 * G])
        b1_rows = sb("b1_rows", [E * FC, P])
        b1_c = sb("b1_c", [P, E * FC])
        bqk_rows = sb("bqk_rows", [2, P])
        bqk_c = sb("bqk_c", [P, 2])
        rank = sb("rank", [P, E])
        ident_r = sb("ident_r", [P, P], F32R)
        shift_c = sb("shift_c", [P, 1])

        x_a = sb("x_a", [P, NT, C])
        cx_a = sb("cx_a", [P, NT, CC])
        xnT_a = sb("xnT_a", [P, T])
        cxT_a = sb("cxT_a", [CC, T])
        hi_part = sb("hi_part", [P, 4, T])
        qs = sb("qs", [P, 2, G, T], F32R)
        ks = sb("ks", [P, 2, G, T], F32R)
        DV = D + 1
        va = sb("va", [P, 2, NT, H * DV + 32 - DV])
        negmax = sb("negmax", [P, 3 * D + P + 32])
        NPA = 9
        pa = sb("pa", [P, NPA, 512])
        oT = [hi_part, sb("oT_cross", [P, 4, T])]
        recA = sb("recA", [P, 2, H])
        yh = sb("yh", [P, 2, C])
        yT = sb("yT", [P, T])
        lg = sb("lg", [P, NT, E])
        m1 = sb("m1", [P, NT])
        ex = sb("ex", [P, NT, E])
        wr = sb("wr", [P, NT, E])
        wrT = sb("wrT", [E, T])
        top_a = [sb(f"top_a{i}", [P, NT * E]) for i in range(4)] + [sb("top_am", [P, NT])]
        hT = pa[:, 0:4, :].rearrange("p u (c n) -> p u c n", c=2)
        x_mid = sb("x_mid", [P, NT, C])
        x_b = sb("x_b", [P, NT, C])
        cx_b = sb("cx_b", [P, NT, CC])
        xnT_b = sb("xnT_b", [P, T])
        cxT_b = sb("cxT_b", [CC, T])
        nm1 = sb("nm1", [P, NT])
        rs1 = sb("rs1", [P, NT])
        rr1 = sb("rr1", [P, NT])
        gates = sb("gates", [P, 2, NT, HB * E])
        eg = sb("eg", [P, NT, HB * E])
        mix = sb("mix", [P, NT, HB * E])
        mout = gates[:, 0, :, :]
        pvs = sb("pvs", [P, NT, E * DH])
        qk_hi = sb("qk_hi", [P, 2, PR, T], F32R)
        qk_lo = sb("qk_lo", [P, 2, PR, T], F32R)
        negc = sb("negc", [P, NT, P])
        cT = sb("cT", [P, T], F32R)
        prod = sb("prod", [P, 4 * E * DH])
        NPB = 8
        pb = sb("pb", [P, NPB, NT * T])
        p1 = pb[:, 0, :].rearrange("p (t n) -> p t n", t=NT)
        p1T = pb[:, 1, :].rearrange("p (t n) -> p t n", t=NT)
        q1T, k1T = pb[:, 2, 0:T], pb[:, 2, T:2 * T]
        v1 = pb[:, 3, 0:NT * P].rearrange("p (t n) -> p t n", t=NT)
        vb = sb("vb", [P, NT, HB, DH + 1])
        at = sb("at", [P, NT, HB, DH + 1])
        recB = sb("recB", [P, NT * HB])
        n_gate = 2 * NT * HB * E
        top_b = [sb("top_b0", [P, n_gate]), prod[:, 0:n_gate], prod[:, n_gate:2 * n_gate], prod[:, 2 * n_gate:3 * n_gate],
                 sb("top_bm", [P, 2 * NT * HB])]
        z = pb[:, 0:NT, :]
        zT = pvs[:, :, :].rearrange("p t (c n) -> p t c n", c=E // 2)
        ln = {s: dict(stat=sb(f"stat_{s}", [P, NT, 6]), mv=sb(f"mv_{s}", [P, NT, 2]), ve=sb(f"ve_{s}", [P, NT]),
                      sq=sb(f"sq_{s}", [P, NT]), half=sb(f"half_{s}", [P, NT]), rstd=sb(f"rstd_{s}", [P, NT]),
                      xn=sb(f"xn_{s}", [P, NT, C])) for s in "ab"}
        y = ln["a"]["xn"]
        xn_a, xn_b = ln["a"]["xn"], ln["b"]["xn"]

        bstack = at[0:1, :, :, :].rearrange("p t h d -> p (t h d)")[:, 0:4 * G * P].rearrange("p (k n) -> p k n", k=4)
        brow_raw = hi_part[0:1, 0:2, :].rearrange("p a n -> p (a n)").rearrange("p (k n) -> p k n", k=4)
        lo_row = hi_part[0:1, 2:4, :].rearrange("p a n -> p (a n)")[:, 0:3 * P].rearrange("p (k n) -> p k n", k=3)
        raw0 = prod[:, 0:4 * P].rearrange("p (k n) -> p k n", k=4)
        rawqk = pb[:, 0:4, :].rearrange("p a n -> p (a n)").rearrange("p (k r n) -> p k r n", k=2, r=PR)
        rawv = pb[:, 4, :].rearrange("p (r n) -> p r n", r=4)
        rawg = pb[:, 5, 0:2 * P].rearrange("p (r n) -> p r n", r=2)
        rawo = pb[:, 6, :].rearrange("p (e d) -> p e d", e=E)

        s_w = sem("s_w")
        s_const = sem("s_const")
        s_fill = sem("s_fill")
        s_spread = sem("s_spread")
        s_turn = sem("s_turn")
        s_turnc = sem("s_turnc")
        names = ["v_link", "a_in", "b_in", "a_xn", "a_xt", "a_xc", "a_pj", "a_mh", "a_split", "a_vp", "a_vc", "a_s",
                 "a_mx", "a_ct", "a_qs", "a_st", "a_ex", "a_pv", "a_ot", "a_tr", "a_y", "a_yt", "a_yc", "a_o",
                 "a_x1", "a_lg", "a_lgc", "a_lx", "a_w", "a_h", "a_ha", "a_hd", "a_yp", "a_acc", "a_wt", "a_wtc",
                 "a_b2", "b_xn", "b_xt", "b_xc", "b_qk", "b_qc", "b_s1", "b_m1", "b_e1", "b_pt", "b_pc", "b_o1",
                 "b_g", "b_gc", "b_sg", "b_pvj", "b_pvc", "b_qkp", "b_hi", "b_lo", "b_s", "b_mx", "b_ct", "b_cc",
                 "b_st", "b_ex", "b_vm", "b_pv", "b_at", "b_z", "b_zt", "b_zc", "b_ro", "b_xo", "a_out", "b_x1"]
        S = {n: sem(n) for n in names}
        first_sem = min(s.num for s in S.values())
        assert max(s.num for s in S.values()) - first_sem == len(names) - 1
        seq_sems = range(first_sem, first_sem + len(names))

        with nc.Block() as block:
            loads = [
                (raw0[:, Q0, :], a["L0_xattn_Wq"]), (raw0[:, K0, :], a["L0_xattn_Wk"]),
                (raw0[:, QC, :], a["L0_xattn_Wcq"]), (raw0[0:CC, KC, :], a["L0_xattn_Wck"]),
                (brow_raw[0:1, Q0, :], a["L0_xattn_bq"].unsqueeze(0)), (brow_raw[0:1, K0, :], a["L0_xattn_bk"].unsqueeze(0)),
                (brow_raw[0:1, QC, :], a["L0_xattn_bcq"].unsqueeze(0)), (brow_raw[0:1, KC, :], a["L0_xattn_bck"].unsqueeze(0)),
                (brow[0:1, 0, :], a["L0_xattn_bv"].unsqueeze(0)), (brow[0:1, 1, :], a["L0_xattn_bcv"].unsqueeze(0)),
                (brow[0:1, 2, :], a["L0_xattn_bp"].unsqueeze(0)), (brow[0:1, 3, :], a["L1_xattn_bv"].unsqueeze(0)),
                (brow[0:1, 4, 0:E], a["L0_ffn_b_router"].unsqueeze(0)),
                (b1_rows[:, :], a["L0_ffn_b1"].rearrange("e (c n) -> (e c) n", n=P)),
                (bqk_rows[0:1, :], a["L1_xattn_bq"].unsqueeze(0)), (bqk_rows[1:2, :], a["L1_xattn_bk"].unsqueeze(0)),
                (wv0[:, :], a["L0_xattn_Wv"]), (wcv0[:, :], a["L0_xattn_Wcv"]), (wp0[:, :], a["L0_xattn_Wp"]),
                (w_router[:, :], a["L0_ffn_W_router"]), (b2[:, :], a["L0_ffn_b2"]),
                (wq1[:, :], a["L1_xattn_Wq"]), (wk1[:, :], a["L1_xattn_Wk"]), (wv1[:, :], a["L1_xattn_Wv"]),
                (rawg[:, 0, :], a["L1_ffn_Ws"].rearrange("h e c -> (h e) c")),
                (rawg[:, 1, :], a["L1_ffn_Wd"].rearrange("h e c -> (h e) c")),
                (rawv, a["L1_ffn_Wv"].rearrange("e d c -> (e d) c").rearrange("(r p) c -> p r c", p=P)),
                (rawo, a["L1_ffn_Wo"].rearrange("e f d -> f e d")),
                (rawqk[:, 0], a["L1_ffn_Wq"].rearrange("h d c -> (h d) c").rearrange("(r p) c -> p r c", p=P)),
                (rawqk[:, 1], a["L1_ffn_Wk"].rearrange("h d c -> (h d) c").rearrange("(r p) c -> p r c", p=P)),
                (w1[:, :, :], a["L0_ffn_W1"].rearrange("e c f -> c e f")),
                (w2[:, :, :, :], a["L0_ffn_W2"].rearrange("e (k p) n -> p e k n", p=P)),
            ]

            N_CONST = 4 + E + 4
            N_SPREAD = 3 + 4 * 6 + 2 + 2 + 3
            turned_to = [wqk_t[:, k, 4 * i:4 * i + 4, :].rearrange("p r n -> p (r n)") for k in range(2) for i in range(2)]
            turned_to += [wv_t[:, :], wo_t[:, :, :].rearrange("p r n -> p (r n)")]
            turned_from = [[rawqk[:, k, 4 * i + r, :] for r in range(4)] for k in range(2) for i in range(2)]
            turned_from += [[rawv[:, r, :] for r in range(4)],
                            [rawo[:, 2 * r:2 * r + 2, :].rearrange("p e d -> p (e d)") for r in range(4)]]

            @block.sync
            def _(sp):
                for dst, src in loads:
                    sp.dma_start(dst, src).then_inc(s_w, 16)

            @block.gpsimd
            def _(pool):
                nc.gpsimd.memset(ident[:, :], 0.0).then_inc(s_fill, 1)
                nc.gpsimd.memset(mask_qk[:, :], 0.0).then_inc(s_fill, 1)
                nc.gpsimd.memset(mask_kq[:, :], 0.0).then_inc(s_fill, 1)
                nc.gpsimd.memset(ones[:, :], 1.0).then_inc(s_const, 1)
                nc.gpsimd.memset(va[:, :, :, :], 0.0).then_inc(s_fill, 1)
                nc.gpsimd.memset(negmax[:, :], 0.0).then_inc(s_const, 1)
                nc.gpsimd.memset(negc[:, :, :], 0.0).then_inc(s_const, 1)
                nc.gpsimd.memset(vb[:, :, :, DH:DH + 1], 1.0).then_inc(s_const, 1)
                for e in range(E):
                    nc.gpsimd.memset(rank[:, e:e + 1], float(E - e)).then_inc(s_const, 1)
                pool.wait_ge(s_fill, 4)
                nc.gpsimd.affine_select(out=ident[:, :], in_=ident[:, :], compare_op=ALU.not_equal, fill=1.0,
                                        base=0, pattern=[[-1, P]], channel_multiplier=1).then_inc(s_const, 1)
                nc.gpsimd.affine_select(out=mask_qk[:, :], in_=mask_qk[:, :], compare_op=ALU.is_ge, fill=MASKED,
                                        base=0, pattern=[[-1, P]], channel_multiplier=1).then_inc(s_const, 1)
                nc.gpsimd.affine_select(out=mask_kq[:, :], in_=mask_kq[:, :], compare_op=ALU.is_ge, fill=MASKED,
                                        base=0, pattern=[[1, P]], channel_multiplier=-1).then_inc(s_const, 1)
                nc.gpsimd.memset(va[:, :, :, 0:H * DV].rearrange("p s t (h d) -> p s t h d", d=DV)[:, :, :, :, D:DV],
                                 1.0).then_inc(s_const, 1)

            @block.vector
            def _(dve):
                nc.vector.memset(w_stack[:, :, :, :], 0.0).then_inc(s_spread, 1)
                nc.vector.memset(bstack[:, :, :], 0.0).then_inc(s_spread, 1)
                nc.vector.memset(lo_row[:, :, :], 0.0).then_inc(s_spread, 1)
                dve.wait_ge(s_spread, 3)
                dve.wait_ge(s_w, 16 * len(loads))
                for kind in range(4):
                    rows = CC if kind == KC else P
                    w = w_stack[0:rows, kind, :, :].rearrange("p g (j r) -> p (g j) r", r=32)
                    b = bstack[:, kind, :].rearrange("p (h r) -> p h r", r=32)
                    for r in range(3):
                        nc.vector.tensor_copy(w[:, :, r * D:(r + 1) * D],
                                              raw0[0:rows, kind, :].rearrange("p (h d) -> p h d", d=D)).then_inc(s_spread, 1)
                        nc.vector.tensor_copy(b[:, :, r * D:(r + 1) * D],
                                              brow_raw[:, kind, :].rearrange("p (h d) -> p h d", d=D)).then_inc(s_spread, 1)
                    if kind in (K0, KC):
                        nc.vector.memset(b[:, :, 3 * D:3 * D + 1], 1.0).then_inc(s_spread, 1)
                nc.vector.memset(lo_row[:, 0, :].rearrange("p (j r) -> p j r", r=32)[:, :, 2 * D:3 * D], 1.0).then_inc(s_spread, 1)
                nc.vector.memset(lo_row[:, 1, :].rearrange("p (j r) -> p j r", r=32)[:, :, D:2 * D], 1.0).then_inc(s_spread, 1)
                dve.wait_ge(s_const, N_CONST)
                nc.vector.tensor_copy(ident_b[:, :], ident[:, :]).then_inc(s_spread, 1)
                nc.vector.tensor_copy(ident_r[:, :], ident[:, :]).then_inc(s_spread, 1)
                nc.vector.memset(lo_row[:, 2, :].rearrange("p (j r) -> p j r", r=32)[:, :, 3 * D:3 * D + 1], 1.0).then_inc(s_spread, 1)
                dve.wait_ge(s_turn, 1)
                nc.vector.tensor_copy(bias_c[:, :], banks[0][:, 0:4 * G]).then_inc(s_spread, 1)
                nc.vector.tensor_copy(lo_c[:, :], banks[0][:, 4 * G:4 * G + 2]).then_inc(s_spread, 1)
                nc.vector.tensor_copy(shift_c[:, :], banks[0][:, 4 * G + 2:4 * G + 3]).then_inc(s_spread, 1)
                nc.vector.tensor_copy(b1_c[:, :], banks[0][:, 32:32 + E * FC]).then_inc(s_spread, 1)
                nc.vector.tensor_copy(bqk_c[:, :], banks[0][:, 96:98]).then_inc(s_spread, 1)
                dve.wait_ge(s_spread, N_SPREAD + 5)
                for kind in range(4):
                    nc.vector.tensor_scalar(lo_bias[:, kind * G:(kind + 1) * G], bias_c[:, kind * G:(kind + 1) * G],
                                            lo_c[:, kind % 2:kind % 2 + 1], None, ALU.mult).then_inc(s_spread, 1)
                for n, dst in enumerate(turned_to):
                    dve.wait_ge(s_turn, n + 2)
                    nc.vector.tensor_copy(dst, banks[1 + n % 7][:, :]).then_inc(s_turnc, 1)

            @block.scalar
            def _(act):
                act.wait_ge(s_turn, len(turned_to) + 2)
                nc.scalar.copy(wgate_t[:, :, :].rearrange("p k n -> p (k n)"), banks[7][:, 0:2 * P]).then_inc(s_turnc, 1)

            @block.tensor
            def _(pe):
                pe.wait_ge(s_w, 16 * len(loads))
                pe.wait_ge(s_const, N_CONST)
                pe.wait_ge(s_spread, N_SPREAD)
                for i in range(4 * G):
                    pe.matmul(banks[0][:, i:i + 1], bstack[0:1, i // G, (i % G) * P:(i % G + 1) * P], ones[0:1, 0:1],
                              start=True, stop=True)
                for i in range(3):
                    pe.matmul(banks[0][:, 4 * G + i:4 * G + i + 1], lo_row[0:1, i, :], ones[0:1, 0:1], start=True, stop=True)
                pe.transpose(banks[0][:, 32:32 + E * FC], b1_rows[:, :], ident[0:E * FC, 0:E * FC])
                pe.transpose(banks[0][:, 96:98], bqk_rows[:, :], ident[0:2, 0:2]).then_inc(s_turn, 1)
                for n, srcs in enumerate(turned_from):
                    for r, src in enumerate(srcs):
                        mm = pe.transpose(banks[1 + n % 7][:, r * P:(r + 1) * P], src, ident[:, :])
                    mm.then_inc(s_turn, 1)
                for r in range(2):
                    mm = pe.transpose(banks[7][:, r * P:(r + 1) * P], rawg[:, r, :], ident[:, :])
                mm.then_inc(s_turn, 1)

        def layernorm_vector(link, inp, s, done):
            n = ln[s]
            stat, mv, ve, sq, half, rstd = n["stat"], n["mv"], n["ve"], n["sq"], n["half"], n["rstd"]
            for t in range(NT):
                link(nc.vector.bn_stats(stat[:, t, :], inp[:, t, :]), wait=(t == NT - 1))
            for t in range(NT):
                link(nc.vector.bn_aggr(mv[:, t, :], stat[:, t, :]), wait=(t == NT - 1))
            link(nc.vector.tensor_scalar(ve[:, :], mv[:, :, 1], EPS, None, ALU.add))
            link(nc.vector.tensor_scalar(sq[:, :].bitcast(I32), ve[:, :].bitcast(I32), 1, None, ALU.logical_shift_right))
            link(nc.vector.tensor_scalar(rstd[:, :].bitcast(I32), sq[:, :].bitcast(I32), -1.0, float(RSQRT_MAGIC),
                                         ALU.mult, ALU.add))
            for _ in range(3):
                link(nc.vector.tensor_tensor(sq[:, :], rstd[:, :], rstd[:, :], ALU.mult))
                link(nc.vector.scalar_tensor_tensor(half[:, :], sq[:, :], -0.5, ve[:, :], ALU.mult, ALU.mult))
                link(nc.vector.scalar_tensor_tensor(rstd[:, :], half[:, :], 1.5, rstd[:, :], ALU.add, ALU.mult))
            for t in range(NT):
                ins = nc.vector.tensor_scalar(n["xn"][:, t, :], inp[:, t, :], mv[:, t, 0:1], rstd[:, t:t + 1],
                                              ALU.subtract, ALU.mult)
            ins.then_inc(done, 1)

        def top2_vector(link, vals, n, bufs):
            f1, f2, ta, tb = [b[:, 0:n * E].rearrange("p (n e) -> p n e", e=E) for b in bufs[:4]]
            v, m = vals.rearrange("p (n e) -> p n e", e=E), bufs[4][:, 0:n]

            def wide(s):
                return s.unsqueeze(2).broadcast_to([P, n, E])

            ranks = rank[:, :].unsqueeze(1).broadcast_to([P, n, E])
            for f, src in ((f1, v), (f2, ta)):
                link(nc.vector.tensor_reduce(m, src, AX, ALU.max))
                link(nc.vector.tensor_tensor(tb, src, wide(m), ALU.is_ge))
                link(nc.vector.tensor_tensor(tb, tb, ranks, ALU.mult))
                link(nc.vector.tensor_reduce(m, tb, AX, ALU.max))
                link(nc.vector.tensor_tensor(f, tb, wide(m), ALU.is_equal))
                if f is f1:
                    link(nc.vector.scalar_tensor_tensor(ta, f, MASKED, v, ALU.mult, ALU.add))
            link(nc.vector.tensor_tensor(f1, f1, f2, ALU.add))

        MAXS = [(CROSS, qt, j, gp) for qt in range(NT) for gp in range(2) for j in range(4)]
        MAXS += [(SELF, 0, j, None) for j in range(4)]
        MAXS += [(SELF, 1, j, gp) for gp in range(2) for j in range(4)]
        NS = len(MAXS)
        PER_J = 7
        assert NS == 4 * PER_J == 28
        KINDS = (Q0, K0, QC, KC)

        x_tiles = a["x"].rearrange("b (t p) c -> p (b t) c", p=P)
        ctx_tiles = a["ctx_512"].rearrange("b (t p) c -> p (b t) c", p=P)
        out_tiles = out.rearrange("b (t p) c -> p (b t) c", p=P)

        STEPS_A = [("a_norm1", 0, 4)] + [("a_stack", u, 1.3) for u in range(8)] + [("a_values", 0, 1)]
        STEPS_A += [("a_max", n, 0.7) for n in range(NS)] + [("a_shift", 0, 3)]
        STEPS_A += [("a_score", n, 1) for n in range(NS)] + [("a_lastpv", 0, 3), ("a_heads", 0, 4), ("a_project", 0, 2)]
        STEPS_A += [("a_norm2", 0, 4), ("a_router", 0, 3)] + [("a_expert", e, 4) for e in range(E)] + [("a_b2", 0, 2)]
        STEPS_B = [("b_norm1", 0, 4), ("b_qkv", 0, 3), ("b_one_max", 0, 2), ("b_one_turn", 0, 2), ("b_one_out", 0, 2),
                   ("b_norm2", 0, 4), ("b_gates", 0, 3)]
        STEPS_B += [("b_split", u, 1) for u in range(8)] + [("b_max", n, 0.7) for n in range(16)] + [("b_shift", 0, 1)]
        STEPS_B += [("b_top2", 0, 8)]
        for hg in range(4):
            STEPS_B += [("b_mix", n, 4) for n in (2 * hg, 2 * hg + 1)] + [("b_score", h, 1.6) for h in range(4 * hg, 4 * hg + 4)]
            STEPS_B += [("b_attend", hg - 1, 3)] if hg >= 1 else []
        STEPS_B += [("b_attend", 3, 3), ("b_weigh", 0, 1)] + [("b_gather", n, 4) for n in range(8)] + [("b_out", 0, 3)]

        def interleave(first, second):
            timed = []
            for steps in (first, second):
                total, at_ = sum(w for _, _, w in steps), 0
                for name, i, w in steps:
                    timed.append(((at_ + w / 2) / total, name, i))
                    at_ += w
            return [(name, i) for _, name, i in sorted(timed, key=lambda s: s[0])]

        def sequences(steps, seq_a, seq_b):
            with nc.Block(no_gpsimd_drain=True) as block:

                @block.sync
                def _(sp):
                    if seq_a is not None:
                        sp.dma_start(x_a[:, :, :], x_tiles[:, bass.ds(seq_a * NT, NT), :]).then_inc(S["a_in"], 16)
                        sp.dma_start(cx_a[:, :, :], ctx_tiles[:, bass.ds(seq_a * NT, NT), :]).then_inc(S["a_in"], 16)
                    if seq_b is not None:
                        sp.dma_start(cx_b[:, :, :], ctx_tiles[:, bass.ds(seq_b * NT, NT), :]).then_inc(S["b_in"], 16)
                        sp.wait_ge(S["b_xo"], NT)
                        sp.dma_start(out_tiles[:, bass.ds(seq_b * NT, NT), :], x_b[:, :, :]).then_inc(S["a_out"], 16)
                        sp.wait_ge(S["a_out"], 16)

                @block.tensor
                def _(pe):
                    def turn_tokens(bank, src, done):
                        for t in range(NT):
                            mm = pe.transpose(bank[:, t * P:(t + 1) * P], src[:, t, :], ident[:, :])
                        mm.then_inc(done, 1)

                    def add_row(dst, row):
                        return pe.matmul(dst, ones[0:1, :], row, start=False, stop=True)

                    def add_mask(dst, mask, n):
                        return pe.matmul(dst, ident_b[:, :], mask[:, :].unsqueeze(1).broadcast_to([P, n, P]),
                                         start=False, stop=True, skip_group_check=True)

                    def a_norm1(_):
                        pe.wait_ge(S["a_in"], 32)
                        for t in range(NT):
                            pe.transpose(BA[0][0:CC, T + t * P:T + (t + 1) * P], cx_a[:, t, :], ident[:, :])
                        pe.wait_ge(S["a_xn"], 1)
                        turn_tokens(BA[0], xn_a, S["a_xt"])

                    def a_stack(u):
                        kind = KINDS[u // 2]
                        pe.wait_ge(S["a_xc"], 2)
                        if u >= 4:
                            pe.wait_ge(S["a_split"], 2 * (u - 4) + 2)
                        for c in range(2):
                            g = 2 * (u % 2) + c
                            rows, rhs = (CC, cxT_a) if kind == KC else (P, xnT_a)
                            mm = pe.matmul(BA[u % 4][:, c * T:(c + 1) * T], w_stack[0:rows, kind, g, :], rhs[:, :],
                                           start=True, stop=True)
                        mm.then_inc(S["a_pj"], 1)

                    def a_values(_):
                        pe.wait_ge(S["a_split"], 10)
                        for sc in range(2):
                            for t in range(NT):
                                lhs, rhs = (xnT_a[:, t * P:(t + 1) * P], wv0) if sc == SELF else (cxT_a[:, t * P:(t + 1) * P], wcv0)
                                dst = BA[0][:, (2 * sc + t) * P:(2 * sc + t + 1) * P]
                                pe.matmul(dst, lhs, rhs[:, :], start=True, stop=False)
                                mm = add_row(dst, brow[0:1, sc, :])
                        mm.then_inc(S["a_vp"], 1)

                    def a_max(n):
                        sc, qt, j, gp = MAXS[n]
                        bank = BA[n % 4]
                        if n == 0:
                            pe.wait_ge(S["a_split"], 16)
                            pe.wait_ge(S["a_vc"], 1)
                        if n >= 4:
                            pe.wait_ge(S["a_mx"], n - 3)
                        rows = slice(32 * j, 32 * j + 32)
                        masked = sc == SELF
                        if masked and qt == 0:
                            for g in range(4):
                                pe.matmul(bank[:, g * P:(g + 1) * P], qs[rows, sc, g, 0:P], ks[rows, sc, g, 0:P],
                                          start=(g == 0), stop=True, skip_group_check=True)
                            mm = add_mask(bank[:, :].rearrange("p (g k) -> p g k", g=4), mask_qk, 4)
                        else:
                            for c in range(2):
                                g = 2 * gp + c
                                mm = pe.matmul(bank[:, c * T:(c + 1) * T], qs[rows, sc, g, qt * P:(qt + 1) * P],
                                               ks[rows, sc, g, :], start=(c == 0), stop=True, skip_group_check=True)
                            if masked:
                                mm = add_mask(bank[:, :].rearrange("p (g k) -> p g k", g=2)[:, :, P:2 * P], mask_qk, 2)
                        mm.then_inc(S["a_s"], 1)

                    def a_shift(_):
                        pe.wait_ge(S["a_mx"], NS)
                        for m in range(4):
                            qt, sc = m // 2, m % 2
                            for g in range(G):
                                i = (qt * 2 + sc) * G + g
                                mm = pe.transpose(BA[m][:, g * P:(g + 1) * P], negmax[:, i:i + P], ident[:, :])
                            mm.then_inc(S["a_ct"], 1)

                    def values(j, sc, kt):
                        bank = BA[3] if sc == SELF else BA[2]
                        unit = PER_J * j
                        if kt == 0:
                            pe.wait_ge(S["a_ex"], unit + (PER_J if sc == SELF else 4))
                            if j >= 1:
                                pe.wait_ge(S["a_ot"], 2 * (j - 1) + (2 if sc == SELF else 1))
                        for g in range(G):
                            h = 4 * g + j
                            dst = bank[32 * g:32 * g + 32, 0:T]
                            if sc == CROSS:
                                rhs = pa[:, (unit + g) % NPA, kt * T:(kt + 1) * T]
                            elif kt == 0:
                                rhs = pa[:, (unit + 4 + g // 2) % NPA, (g % 2) * T:(g % 2 + 1) * T]
                            else:
                                rhs = pa[:, (unit + 6) % NPA, g * P:(g + 1) * P]
                                dst = bank[32 * g:32 * g + 32, P:T]
                            mm = pe.matmul(dst, va[:, sc, kt, h * DV:h * DV + 32], rhs, start=(kt == 0),
                                           stop=(sc == SELF or kt == 1), skip_group_check=True)
                        if kt == 1:
                            mm.then_inc(S["a_pv"], 1)

                    VALUE_PARTS = ((CROSS, 0), (CROSS, 1), (SELF, 0), (SELF, 1))

                    def a_score(n):
                        j, k = n // PER_J, n % PER_J
                        bank = BA[n % 2]
                        rows = slice(32 * j, 32 * j + 32)
                        if n == 0:
                            pe.wait_ge(S["a_qs"], 4)
                        if n >= 2:
                            pe.wait_ge(S["a_ex"], n - 1)
                        if k < 4:
                            for kt in range(NT):
                                mm = pe.matmul(bank[:, kt * T:(kt + 1) * T], ks[rows, CROSS, k, kt * P:(kt + 1) * P],
                                               qs[rows, CROSS, k, :], start=True, stop=True)
                        elif k < 6:
                            for c in range(2):
                                g = 2 * (k - 4) + c
                                pe.matmul(bank[:, c * T:(c + 1) * T], ks[rows, SELF, g, 0:P], qs[rows, SELF, g, :],
                                          start=(c == 0), stop=True, skip_group_check=True)
                            mm = add_mask(bank[:, :].rearrange("p (g q) -> p g q", g=2)[:, :, 0:P], mask_kq, 2)
                        else:
                            for g in range(G):
                                pe.matmul(bank[:, g * P:(g + 1) * P], ks[rows, SELF, g, P:T], qs[rows, SELF, g, P:T],
                                          start=(g == 0), stop=True, skip_group_check=True)
                            mm = add_mask(bank[:, :].rearrange("p (g q) -> p g q", g=4), mask_kq, 4)
                        mm.then_inc(S["a_st"], 1)
                        if j >= 1 and k in (1, 2, 3, 4):
                            values(j - 1, *VALUE_PARTS[k - 1])

                    def a_lastpv(_):
                        for part in VALUE_PARTS:
                            values(3, *part)

                    def a_heads(_):
                        pe.wait_ge(S["a_ot"], 8)
                        for m in range(4):
                            qt, sc = m // 2, m % 2
                            for j in range(4):
                                mm = pe.transpose(BA[m][:, j * P:(j + 1) * P], oT[sc][:, j, qt * P:(qt + 1) * P], ident[:, :])
                            mm.then_inc(S["a_tr"], 1)

                    def a_project(_):
                        pe.wait_ge(S["a_y"], 2)
                        turn_tokens(BA[0], y, S["a_yt"])
                        pe.wait_ge(S["a_yc"], 1)
                        for t in range(NT):
                            dst = BA[1][:, t * P:(t + 1) * P]
                            pe.matmul(dst, yT[:, t * P:(t + 1) * P], wp0[:, :], start=True, stop=False)
                            mm = add_row(dst, brow[0:1, 2, :])
                        mm.then_inc(S["a_o"], 1)

                    def a_norm2(_):
                        pe.wait_ge(S["a_xn"], 2)
                        turn_tokens(BA[2], xn_a, S["a_xt"])

                    def hidden(u):
                        e, fp = u // 2, u % 2
                        if u >= 2:
                            pe.wait_ge(S["a_ha"] if u % 2 == 0 else S["a_hd"], u // 2)
                        for c in range(2):
                            f = (2 * fp + c) * P
                            mm = pe.matmul(BA[u % 2][:, c * T:(c + 1) * T], w1[:, e, f:f + P], xnT_a[:, :],
                                           start=True, stop=True)
                        mm.then_inc(S["a_h"], 1)

                    def a_router(_):
                        pe.wait_ge(S["a_xc"], 3)
                        for t in range(NT):
                            dst = BA[3][:, t * E:(t + 1) * E]
                            pe.matmul(dst, xnT_a[:, t * P:(t + 1) * P], w_router[:, :], start=True, stop=False)
                            mm = add_row(dst, brow[0:1, 4, 0:E])
                        mm.then_inc(S["a_lg"], 1)
                        pe.wait_ge(S["a_x1"], 1)
                        hidden(0)
                        hidden(1)

                    def a_expert(e):
                        if e + 1 < E:
                            hidden(2 * e + 2)
                            hidden(2 * e + 3)
                        pe.wait_ge(S["a_ha"], e + 1)
                        pe.wait_ge(S["a_hd"], e + 1)
                        if e == 1:
                            pe.wait_ge(S["a_lgc"], 1)
                        if e >= 2:
                            pe.wait_ge(S["a_acc"], e - 1)
                        for t in range(NT):
                            for f in range(FC):
                                mm = pe.matmul(BA[2 + e % 2][:, t * P:(t + 1) * P],
                                               hT[:, (2 * e + f // 2) % 4, f % 2, t * P:(t + 1) * P], w2[:, e, f, :],
                                               start=(f == 0), stop=(f == FC - 1))
                        mm.then_inc(S["a_yp"], 1)

                    def a_b2(_):
                        pe.wait_ge(S["a_w"], 1)
                        pe.wait_ge(S["a_ha"], E)
                        pe.wait_ge(S["a_hd"], E)
                        for t in range(NT):
                            mm = pe.transpose(BA[0][0:E, t * P:(t + 1) * P], wr[:, t, :], ident[:, :])
                        mm.then_inc(S["a_wt"], 1)
                        pe.wait_ge(S["a_wtc"], 1)
                        for t in range(NT):
                            mm = pe.matmul(BA[1][:, t * P:(t + 1) * P], wrT[:, t * P:(t + 1) * P], b2[:, :], start=True, stop=True)
                        mm.then_inc(S["a_b2"], 1)

                    def b_norm1(_):
                        pe.wait_ge(S["b_in"], 16)
                        for t in range(NT):
                            pe.transpose(BB[0][0:CC, T + t * P:T + (t + 1) * P], cx_b[:, t, :], ident[:, :])
                        pe.wait_ge(S["b_xn"], 1)
                        turn_tokens(BB[0], xn_b, S["b_xt"])

                    def b_qkv(_):
                        pe.wait_ge(S["b_xc"], 2)
                        pe.matmul(BB[1][:, 0:T], wq1[:, :], xnT_b[:, :], start=True, stop=True)
                        pe.matmul(BB[1][:, T:2 * T], wk1[:, :], cxT_b[:, :], start=True, stop=True).then_inc(S["b_qk"], 1)
                        for t in range(NT):
                            dst = BB[2][:, t * P:(t + 1) * P]
                            pe.matmul(dst, cxT_b[:, t * P:(t + 1) * P], wv1[:, :], start=True, stop=False)
                            mm = add_row(dst, brow[0:1, 3, :])
                        mm.then_inc(S["b_qk"], 1)

                    def b_one_max(_):
                        pe.wait_ge(S["b_qc"], 2)
                        for t in range(NT):
                            mm = pe.matmul(BB[3][:, t * T:(t + 1) * T], q1T[:, t * P:(t + 1) * P], k1T[:, :], start=True, stop=True)
                        mm.then_inc(S["b_s1"], 1)

                    def b_one_turn(_):
                        pe.wait_ge(S["b_e1"], 2)
                        for kt in range(NT):
                            for qt in range(NT):
                                mm = pe.transpose(BB[0][:, kt * T + qt * P:kt * T + (qt + 1) * P], p1[:, qt, kt * P:(kt + 1) * P],
                                                  ident[:, :])
                        mm.then_inc(S["b_pt"], 1)

                    def b_one_out(_):
                        pe.wait_ge(S["b_pc"], 1)
                        pe.wait_ge(S["b_qc"], 3)
                        for qt in range(NT):
                            for kt in range(NT):
                                mm = pe.matmul(BB[1][:, qt * P:(qt + 1) * P], p1T[:, kt, qt * P:(qt + 1) * P], v1[:, kt, :],
                                               start=(kt == 0), stop=(kt == 1))
                        mm.then_inc(S["b_o1"], 1)

                    def b_norm2(_):
                        pe.wait_ge(S["b_xn"], 2)
                        turn_tokens(BB[2], xn_b, S["b_xt"])

                    def b_gates(_):
                        pe.wait_ge(S["b_xc"], 3)
                        for t in range(NT):
                            mm = pe.matmul(BB[3][:, t * T:(t + 1) * T], xnT_b[:, t * P:(t + 1) * P],
                                           wgate_t[:, :, :].rearrange("p k n -> p (k n)"), start=True, stop=True)
                        mm.then_inc(S["b_g"], 1)
                        for t in range(NT):
                            pe.matmul(BB[t][:, :], xnT_b[:, t * P:(t + 1) * P], wv_t[:, :], start=True, stop=True)\
                              .then_inc(S["b_pvj"], 1)

                    def b_split(u):
                        if u == 1:
                            pe.wait_ge(S["b_gc"], 1)
                        elif u in (2, 3):
                            pe.wait_ge(S["b_pvc"], u - 1)
                        elif u >= 4:
                            pe.wait_ge(S["b_lo"], u - 3)
                        for c in range(2):
                            mm = pe.matmul(BB[(u + 2) % 4][:, c * T:(c + 1) * T], wqk_t[:, u // 4, 2 * (u % 4) + c, :],
                                           xnT_b[:, :], start=True, stop=True)
                        mm.then_inc(S["b_qkp"], 1)

                    def b_max(n):
                        qt, pp, j = n // 8, (n // 2) % 4, n % 2
                        rows = slice(64 * j, 64 * j + 64)
                        if n == 0:
                            pe.wait_ge(S["b_lo"], 8)
                        if n >= 4:
                            pe.wait_ge(S["b_mx"], n - 3)
                        for c in range(2):
                            mm = pe.matmul(BB[(n + 2) % 4][:, c * T:(c + 1) * T],
                                           qk_hi[rows, 0, 2 * pp + c, qt * P:(qt + 1) * P], qk_hi[rows, 1, 2 * pp + c, :],
                                           start=True, stop=True)
                        mm.then_inc(S["b_s"], 1)

                    def b_shift(_):
                        pe.wait_ge(S["b_mx"], 16)
                        turn_tokens(BB[2], negc, S["b_ct"])

                    def b_score(h):
                        pr, rows = h // 2, slice(64 * (h % 2), 64 * (h % 2) + 64)
                        if h == 0:
                            pe.wait_ge(S["b_cc"], 1)
                        if h >= 2:
                            pe.wait_ge(S["b_ex"], h - 1)
                        bank = BB[h % 2]
                        c = 64 * (h % 2) + h
                        for kt in range(NT):
                            keys = slice(kt * P, (kt + 1) * P)
                            dst = bank[:, kt * T:(kt + 1) * T]
                            pe.matmul(dst, qk_lo[rows, 1, pr, keys], qk_hi[rows, 0, pr, :], start=(kt == 0), stop=False,
                                      skip_group_check=True)
                            pe.matmul(dst, qk_hi[rows, 1, pr, keys], qk_lo[rows, 0, pr, :], start=False, stop=False,
                                      skip_group_check=True)
                            pe.matmul(dst, qk_hi[rows, 1, pr, keys], qk_hi[rows, 0, pr, :], start=False, stop=True,
                                      skip_group_check=True)
                        pe.matmul(bank[:, :].rearrange("p (k q) -> p k q", k=NT), ident_r[rows, c:c + 1].broadcast_to([64, P]),
                                  cT[rows, :].unsqueeze(1).broadcast_to([64, NT, T]), start=False, stop=True,
                                  skip_group_check=True).then_inc(S["b_st"], 1)

                    def b_attend(hg):
                        pe.wait_ge(S["b_vm"], NT * (hg + 1))
                        pe.wait_ge(S["b_ex"], 4 * hg + 4)
                        if hg == 0:
                            pe.wait_ge(S["b_cc"], 1)
                        for qt in range(NT):
                            if hg >= 1:
                                pe.wait_ge(S["b_at"], 2 * (hg - 1) + qt + 1)
                            for i in range(4):
                                h = 4 * hg + i
                                for kt in range(NT):
                                    mm = pe.matmul(BB[2 + qt][:, i * (DH + 1):(i + 1) * (DH + 1)],
                                                   pb[:, h % NPB, kt * T + qt * P:kt * T + (qt + 1) * P], vb[:, kt, h, :],
                                                   start=(kt == 0), stop=(kt == 1))
                            mm.then_inc(S["b_pv"], 1)

                    def b_out(_):
                        for qt in range(NT):
                            pe.wait_ge(S["b_z"], (E // 2) * (qt + 1))
                            for c in range(E // 2):
                                mm = pe.transpose(BB[qt][:, c * P:(c + 1) * P], z[:, qt, c * P:(c + 1) * P], ident[:, :])
                            mm.then_inc(S["b_zt"], 1)
                        for qt in range(NT):
                            pe.wait_ge(S["b_zc"], qt + 1)
                            pe.wait_ge(S["b_at"], 8)
                            for c in range(E // 2):
                                mm = pe.matmul(BB[2 + qt][:, 0:P], zT[:, qt, c, :], wo_t[:, c, :],
                                               start=(c == 0), stop=(c == E // 2 - 1))
                            mm.then_inc(S["b_ro"], 1)

                    own = dict(a_norm1=a_norm1, a_stack=a_stack, a_values=a_values, a_max=a_max, a_shift=a_shift,
                               a_score=a_score, a_lastpv=a_lastpv, a_heads=a_heads, a_project=a_project, a_norm2=a_norm2,
                               a_router=a_router, a_expert=a_expert, a_b2=a_b2, b_norm1=b_norm1, b_qkv=b_qkv,
                               b_one_max=b_one_max, b_one_turn=b_one_turn, b_one_out=b_one_out, b_norm2=b_norm2,
                               b_gates=b_gates, b_split=b_split, b_max=b_max, b_shift=b_shift, b_score=b_score,
                               b_attend=b_attend, b_out=b_out)
                    for name, i in steps:
                        if name in own:
                            own[name](i)

                @block.scalar
                def _(act):
                    def a_norm1(_):
                        act.wait_ge(S["a_xt"], 1)
                        nc.scalar.copy(xnT_a[:, :], BA[0][:, 0:T]).then_inc(S["a_xc"], 1)
                        nc.scalar.copy(cxT_a[:, :], BA[0][0:CC, T:2 * T]).then_inc(S["a_xc"], 1)

                    def a_stack(u):
                        act.wait_ge(S["a_pj"], u + 1)
                        kind = KINDS[u // 2]
                        for c in range(2):
                            n, k = 2 * u + c, kind * G + 2 * (u % 2) + c
                            if n >= 4:
                                act.wait_ge(S["a_split"], n - 3)
                            nc.scalar.activation(hi_part[:, n % 4, :].bitcast(F32R), BA[u % 4][:, c * T:(c + 1) * T], ACT.Identity,
                                                 bias=lo_bias[:, k:k + 1], scale=lo_c[:, kind % 2:kind % 2 + 1])\
                              .then_inc(S["a_mh"], 1)

                    def a_values(_):
                        act.wait_ge(S["a_vp"], 1)
                        nc.scalar.copy(va[:, :, :, 0:H * DV].rearrange("p s t (h d) -> p (s t) h d", d=DV)[:, :, :, 0:D],
                                       BA[0][:, :].rearrange("p (a h d) -> p a h d", a=4, d=D)).then_inc(S["a_vc"], 1)

                    def a_score(n):
                        act.wait_ge(S["a_st"], n + 1)
                        if n >= NPA:
                            old = n - NPA
                            act.wait_ge(S["a_pv"], 2 * (old // PER_J) + (1 if old % PER_J < 4 else 2))
                        nc.scalar.activation(pa[:, n % NPA, :], BA[n % 2][:, :], ACT.Exp, scale=SC0).then_inc(S["a_ex"], 1)

                    def a_project(_):
                        act.wait_ge(S["a_yt"], 1)
                        nc.scalar.copy(yT[:, :], BA[0][:, 0:T]).then_inc(S["a_yc"], 1)

                    def a_norm2(_):
                        act.wait_ge(S["a_xt"], 2)
                        nc.scalar.copy(xnT_a[:, :], BA[2][:, 0:T]).then_inc(S["a_xc"], 1)

                    def hidden_relu(e):
                        u = 2 * e
                        act.wait_ge(S["a_h"], u + 1)
                        if e >= 2:
                            act.wait_ge(S["a_yp"], e - 1)
                        for c in range(2):
                            ins = nc.scalar.activation(hT[:, u % 4, c, :], BA[0][:, c * T:(c + 1) * T], ACT.Relu,
                                                       bias=b1_c[:, e * FC + c:e * FC + c + 1])
                        ins.then_inc(S["a_ha"], 1)

                    def a_router(_):
                        act.wait_ge(S["a_lx"], 1)
                        nc.scalar.activation(ex[:, :, :], ex[:, :, :], ACT.Exp).then_inc(S["a_lx"], 1)
                        hidden_relu(0)

                    def a_expert(e):
                        if e + 1 < E:
                            hidden_relu(e + 1)

                    def b_norm1(_):
                        act.wait_ge(S["b_xt"], 1)
                        nc.scalar.copy(xnT_b[:, :], BB[0][:, 0:T]).then_inc(S["b_xc"], 1)
                        nc.scalar.copy(cxT_b[:, :], BB[0][0:CC, T:2 * T]).then_inc(S["b_xc"], 1)

                    def b_qkv(_):
                        act.wait_ge(S["b_qk"], 1)
                        nc.scalar.activation(q1T[:, :], BB[1][:, 0:T], ACT.Identity, bias=bqk_c[:, 0:1]).then_inc(S["b_qc"], 1)
                        nc.scalar.activation(k1T[:, :], BB[1][:, T:2 * T], ACT.Identity, bias=bqk_c[:, 1:2]).then_inc(S["b_qc"], 1)
                        act.wait_ge(S["b_qk"], 2)
                        nc.scalar.copy(v1[:, :, :].rearrange("p t n -> p (t n)"), BB[2][:, 0:2 * P]).then_inc(S["b_qc"], 1)

                    def b_one_max(_):
                        act.wait_ge(S["b_m1"], 1)
                        for t in range(NT):
                            nc.scalar.activation(p1[:, t, :], BB[3][:, t * T:(t + 1) * T], ACT.Exp, bias=nm1[:, t:t + 1],
                                                 accum_out=rs1[:, t:t + 1]).then_inc(S["b_e1"], 1)

                    def b_one_turn(_):
                        act.wait_ge(S["b_pt"], 1)
                        nc.scalar.copy(p1T[:, :, :].rearrange("p t n -> p (t n)"), BB[0][:, :]).then_inc(S["b_pc"], 1)

                    def b_norm2(_):
                        act.wait_ge(S["b_xt"], 2)
                        nc.scalar.copy(xnT_b[:, :], BB[2][:, 0:T]).then_inc(S["b_xc"], 1)

                    def b_gates(_):
                        for t in range(NT):
                            act.wait_ge(S["b_pvj"], t + 1)
                            nc.scalar.copy(pvs[:, t, :], BB[t][:, :]).then_inc(S["b_pvc"], 1)
                        act.wait_ge(S["b_gc"], 1)
                        nc.scalar.activation(eg[:, :, :], gates[:, 0, :, :], ACT.Exp, scale=-1.0).then_inc(S["b_sg"], 1)

                    def b_split(u):
                        act.wait_ge(S["b_qkp"], u + 1)
                        r = 2 * (u % 4)
                        nc.scalar.copy(qk_hi[:, u // 4, r:r + 2, :].rearrange("p r n -> p (r n)"),
                                       BB[(u + 2) % 4][:, :]).then_inc(S["b_hi"], 1)

                    def b_score(h):
                        act.wait_ge(S["b_st"], h + 1)
                        if h >= NPB:
                            act.wait_ge(S["b_pv"], 2 * ((h - NPB) // 4 + 1))
                        nc.scalar.activation(pb[:, h % NPB, :], BB[h % 2][:, :], ACT.Exp, scale=SC1).then_inc(S["b_ex"], 1)

                    def b_attend(hg):
                        for qt in range(NT):
                            act.wait_ge(S["b_pv"], 2 * hg + qt + 1)
                            nc.scalar.copy(at[:, qt, 4 * hg:4 * hg + 4, :].rearrange("p h d -> p (h d)"),
                                           BB[2 + qt][:, 0:4 * (DH + 1)]).then_inc(S["b_at"], 1)

                    def b_out(_):
                        for qt in range(NT):
                            act.wait_ge(S["b_zt"], qt + 1)
                            nc.scalar.copy(zT[:, qt, :, :].rearrange("p c n -> p (c n)"), BB[qt][:, :]).then_inc(S["b_zc"], 1)

                    own = dict(a_norm1=a_norm1, a_stack=a_stack, a_values=a_values, a_score=a_score, a_project=a_project,
                               a_norm2=a_norm2, a_router=a_router, a_expert=a_expert, b_norm1=b_norm1, b_qkv=b_qkv,
                               b_one_max=b_one_max, b_one_turn=b_one_turn, b_norm2=b_norm2, b_gates=b_gates,
                               b_split=b_split, b_score=b_score, b_attend=b_attend, b_out=b_out)
                    for name, i in steps:
                        if name in own:
                            own[name](i)

                @block.vector
                def _(dve):
                    chain = [0]

                    def link(ins, wait=True):
                        chain[0] += 1
                        ins.then_inc(S["v_link"], 1)
                        if wait:
                            dve.wait_ge(S["v_link"], chain[0])

                    def halves(bank):
                        return bank[:, 0:T].rearrange("p (t n) -> p t n", t=NT)

                    def a_norm1(_):
                        dve.wait_ge(S["a_in"], 32)
                        layernorm_vector(link, x_a, "a", S["a_xn"])

                    def a_stack(u):
                        kind = KINDS[u // 2]
                        dve.wait_ge(S["a_mh"], 2 * u + 2)
                        for c in range(2):
                            n, g = 2 * u + c, 2 * (u % 2) + c
                            stack = qs if kind in (Q0, QC) else ks
                            nc.vector.scalar_tensor_tensor(stack[:, kind // 2, g, :], BA[u % 4][:, c * T:(c + 1) * T],
                                                           bias_c[:, kind * G + g:kind * G + g + 1], hi_part[:, n % 4, :],
                                                           ALU.add, ALU.subtract).then_inc(S["a_split"], 1)

                    def a_max(n):
                        sc, qt, j, gp = MAXS[n]
                        dve.wait_ge(S["a_s"], n + 1)
                        g0, ng = (0, 4) if gp is None else (2 * gp, 2)
                        i = 3 * D + 32 * j + (qt * 2 + sc) * G + g0
                        nc.vector.tensor_reduce(negmax[:, i:i + ng], BA[n % 4][:, :].rearrange("p (g k) -> p g k", g=ng),
                                                AX, ALU.max, negate=True).then_inc(S["a_mx"], 1)

                    def a_shift(_):
                        for m in range(4):
                            qt, sc = m // 2, m % 2
                            dve.wait_ge(S["a_ct"], m + 1)
                            dst = qs[:, sc, :, qt * P:(qt + 1) * P]
                            nc.vector.scalar_tensor_tensor(dst, BA[m][:, :].rearrange("p (g q) -> p g q", g=G), shift_c[:, 0:1],
                                                           dst.bitcast(F32), ALU.mult, ALU.add).then_inc(S["a_qs"], 1)

                    def outputs(i):
                        sc = CROSS if i % 2 == 0 else SELF
                        dve.wait_ge(S["a_pv"], i + 1)
                        nc.vector.tensor_copy(oT[sc][:, i // 2, :], BA[2 + i % 2][:, 0:T]).then_inc(S["a_ot"], 1)

                    def a_score(n):
                        j, k = n // PER_J, n % PER_J
                        if j >= 1 and k in (3, 5):
                            outputs(2 * (j - 1) + (k - 3) // 2)

                    def a_lastpv(_):
                        outputs(6)
                        outputs(7)

                    def a_heads(_):
                        for qt in range(NT):
                            dve.wait_ge(S["a_tr"], 2 * qt + 2)
                            heads = [BA[2 * qt + sc][:, :].rearrange("p (h r) -> p h r", r=32) for sc in range(2)]
                            for sc in range(2):
                                link(nc.vector.reciprocal(recA[:, sc, :], heads[sc][:, :, D]), wait=(sc == 1))
                            for sc in range(2):
                                link(nc.vector.tensor_tensor(
                                    yh[:, sc, :].rearrange("p (g j d) -> p j g d", g=G, j=4),
                                    heads[sc][:, :, 0:D].rearrange("p (j g) d -> p j g d", j=4),
                                    recA[:, sc, :].rearrange("p (j g) -> p j g", j=4).unsqueeze(3).broadcast_to([P, 4, G, D]),
                                    ALU.mult), wait=(sc == 1))
                            nc.vector.tensor_tensor(y[:, qt, :], yh[:, 0, :], yh[:, 1, :], ALU.add).then_inc(S["a_y"], 1)
                            dve.wait_ge(S["a_y"], qt + 1)

                    def a_project(_):
                        dve.wait_ge(S["a_o"], 1)
                        nc.vector.tensor_tensor(x_a[:, :, :], x_a[:, :, :], halves(BA[1]), ALU.add).then_inc(S["a_x1"], 1)

                    def a_norm2(_):
                        dve.wait_ge(S["a_x1"], 1)
                        layernorm_vector(link, x_a, "a", S["a_xn"])

                    def hidden_relu(e):
                        u = 2 * e + 1
                        dve.wait_ge(S["a_h"], u + 1)
                        if e >= 2:
                            dve.wait_ge(S["a_yp"], e - 1)
                        for c in range(2):
                            k = e * FC + 2 + c
                            ins = nc.vector.tensor_scalar(hT[:, u % 4, c, :], BA[1][:, c * T:(c + 1) * T], b1_c[:, k:k + 1], 0.0,
                                                          ALU.add, ALU.max)
                        ins.then_inc(S["a_hd"], 1)

                    def a_router(_):
                        dve.wait_ge(S["a_lg"], 1)
                        lgf = lg[:, :, :].rearrange("p t e -> p (t e)")
                        nc.vector.tensor_copy(lgf, BA[3][:, 0:NT * E]).then_inc(S["a_lgc"], 1)
                        dve.wait_ge(S["a_lgc"], 1)
                        link(nc.vector.tensor_reduce(m1[:, :], lg[:, :, :], AX, ALU.max))
                        nc.vector.tensor_tensor(ex[:, :, :], lg[:, :, :], m1[:, :].unsqueeze(2).broadcast_to([P, NT, E]),
                                                ALU.subtract).then_inc(S["a_lx"], 1)
                        hidden_relu(0)
                        top2_vector(link, lgf, NT, top_a)
                        dve.wait_ge(S["a_lx"], 2)
                        link(nc.vector.tensor_tensor(ex[:, :, :], ex[:, :, :], top_a[0][:, :].rearrange("p (t e) -> p t e", e=E), ALU.mult))
                        link(nc.vector.tensor_reduce(m1[:, :], ex[:, :, :], AX, ALU.add))
                        link(nc.vector.reciprocal(m1[:, :], m1[:, :]))
                        nc.vector.tensor_tensor(wr[:, :, :], ex[:, :, :], m1[:, :].unsqueeze(2).broadcast_to([P, NT, E]),
                                                ALU.mult).then_inc(S["a_w"], 1)
                        dve.wait_ge(S["a_w"], 1)

                    def accumulate(e):
                        dve.wait_ge(S["a_yp"], e + 1)
                        if e >= 1:
                            dve.wait_ge(S["a_acc"], e)
                        for t in range(NT):
                            ins = nc.vector.scalar_tensor_tensor(x_a[:, t, :], BA[2 + e % 2][:, t * P:(t + 1) * P],
                                                                 wr[:, t, e:e + 1], x_a[:, t, :], ALU.mult, ALU.add)
                        ins.then_inc(S["a_acc"], 1)

                    def a_expert(e):
                        if e >= 1:
                            accumulate(e - 1)
                        if e + 1 < E:
                            hidden_relu(e + 1)

                    def a_b2(_):
                        accumulate(E - 1)
                        dve.wait_ge(S["a_wt"], 1)
                        nc.vector.tensor_copy(wrT[:, :], BA[0][0:E, 0:T]).then_inc(S["a_wtc"], 1)
                        dve.wait_ge(S["a_b2"], 1)
                        dve.wait_ge(S["a_acc"], E)
                        if seq_b is not None:
                            dve.wait_ge(S["b_x1"], 1)
                        link(nc.vector.tensor_tensor(x_mid[:, :, :], x_a[:, :, :], halves(BA[1]), ALU.add))

                    def b_norm1(_):
                        layernorm_vector(link, x_mid, "b", S["b_xn"])

                    def b_one_max(_):
                        dve.wait_ge(S["b_s1"], 1)
                        nc.vector.tensor_reduce(nm1[:, :], BB[3][:, :].rearrange("p (t k) -> p t k", t=NT), AX, ALU.max,
                                                negate=True).then_inc(S["b_m1"], 1)

                    def b_one_out(_):
                        dve.wait_ge(S["b_e1"], 2)
                        link(nc.vector.reciprocal(rr1[:, :], rs1[:, :]))
                        dve.wait_ge(S["b_o1"], 1)
                        for t in range(NT):
                            ins = nc.vector.scalar_tensor_tensor(x_b[:, t, :], BB[1][:, t * P:(t + 1) * P], rr1[:, t:t + 1],
                                                                 x_mid[:, t, :], ALU.mult, ALU.add)
                        ins.then_inc(S["b_x1"], 1)

                    def b_norm2(_):
                        dve.wait_ge(S["b_x1"], 1)
                        layernorm_vector(link, x_b, "b", S["b_xn"])

                    def b_gates(_):
                        dve.wait_ge(S["b_g"], 1)
                        nc.vector.tensor_copy(gates[:, :, :, :].rearrange("p k t n -> p t k n"),
                                              BB[3][:, :].rearrange("p (t k n) -> p t k n", t=NT, k=2)).then_inc(S["b_gc"], 1)

                    def b_split(u):
                        r = 2 * (u % 4)
                        lo = qk_lo[:, u // 4, r:r + 2, :].rearrange("p r n -> p (r n)")
                        hi = qk_hi[:, u // 4, r:r + 2, :].rearrange("p r n -> p (r n)")
                        dve.wait_ge(S["b_hi"], u + 1)
                        nc.vector.tensor_tensor(lo, BB[(u + 2) % 4][:, :], hi.bitcast(F32), ALU.subtract).then_inc(S["b_lo"], 1)

                    def b_max(n):
                        qt, pp, j = n // 8, (n // 2) % 4, n % 2
                        c = 64 * j + 4 * pp + j
                        dve.wait_ge(S["b_s"], n + 1)
                        nc.vector.tensor_reduce(negc[:, qt, c:c + 3:2], BB[(n + 2) % 4][:, :].rearrange("p (h k) -> p h k", h=2),
                                                AX, ALU.max, negate=True).then_inc(S["b_mx"], 1)

                    def b_shift(_):
                        dve.wait_ge(S["b_ct"], 1)
                        nc.vector.tensor_copy(cT[:, :], BB[2][:, 0:T]).then_inc(S["b_cc"], 1)

                    chosen = top_b[0][:, :].rearrange("p (k t n) -> p k t n", k=2, t=NT)

                    def b_top2(_):
                        dve.wait_ge(S["b_gc"], 1)
                        top2_vector(link, gates[:, :, :, :].rearrange("p k t n -> p (k t n)"), 2 * NT * HB, top_b)
                        dve.wait_ge(S["b_sg"], 1)
                        link(nc.vector.tensor_scalar(eg[:, :, :], eg[:, :, :], 1.0, None, ALU.add))
                        link(nc.vector.reciprocal(eg[:, :, :], eg[:, :, :]))
                        link(nc.vector.tensor_tensor(mix[:, :, :], eg[:, :, :], chosen[:, 0], ALU.mult))

                    def b_mix(n):
                        hg, t = n // 2, n % 2
                        if n == 0:
                            dve.wait_ge(S["b_pvc"], 2)
                        heads = prod[:, :].rearrange("p (h d e) -> p h d e", h=4, d=DH)
                        link(nc.vector.tensor_tensor(
                            heads,
                            mix[:, t, 4 * hg * E:4 * (hg + 1) * E].rearrange("p (h e) -> p h e", e=E).unsqueeze(2)
                            .broadcast_to([P, 4, DH, E]),
                            pvs[:, t, :].rearrange("p (e d) -> p d e", e=E).unsqueeze(1).broadcast_to([P, 4, DH, E]),
                            ALU.mult))
                        nc.vector.tensor_reduce(vb[:, t, 4 * hg:4 * (hg + 1), 0:DH], heads, AX, ALU.add).then_inc(S["b_vm"], 1)
                        dve.wait_ge(S["b_vm"], n + 1)

                    def b_weigh(_):
                        dve.wait_ge(S["b_at"], 8)
                        link(nc.vector.reciprocal(recB[:, :], at[:, :, :, DH].rearrange("p t h -> p (t h)")))
                        link(nc.vector.tensor_tensor(mout[:, :, :].rearrange("p t (h e) -> p (t h) e", e=E),
                                                     chosen[:, 1].rearrange("p t (h e) -> p (t h) e", e=E),
                                                     recB[:, :].unsqueeze(2).broadcast_to([P, NT * HB, E]), ALU.mult))

                    def b_gather(n):
                        t, c = n // (E // 2), n % (E // 2)
                        pair = prod[:, :].rearrange("p (e d h) -> p e d h", e=2, d=DH)
                        link(nc.vector.tensor_tensor(
                            pair,
                            mout[:, t, :].rearrange("p (h e) -> p e h", e=E)[:, 2 * c:2 * c + 2, :].unsqueeze(2)
                            .broadcast_to([P, 2, DH, HB]),
                            at[:, t, :, 0:DH].rearrange("p h d -> p d h").unsqueeze(1).broadcast_to([P, 2, DH, HB]),
                            ALU.mult))
                        nc.vector.tensor_reduce(z[:, t, c * P:(c + 1) * P].rearrange("p (e d) -> p e d", e=2), pair,
                                                AX, ALU.add).then_inc(S["b_z"], 1)
                        dve.wait_ge(S["b_z"], n + 1)

                    def b_out(_):
                        for t in range(NT):
                            dve.wait_ge(S["b_ro"], t + 1)
                            nc.vector.tensor_tensor(x_b[:, t, :], x_b[:, t, :], BB[2 + t][:, 0:P], ALU.add).then_inc(S["b_xo"], 1)

                    own = dict(a_norm1=a_norm1, a_stack=a_stack, a_max=a_max, a_shift=a_shift, a_score=a_score,
                               a_lastpv=a_lastpv, a_heads=a_heads, a_project=a_project, a_norm2=a_norm2, a_router=a_router,
                               a_expert=a_expert, a_b2=a_b2, b_norm1=b_norm1, b_one_max=b_one_max, b_one_out=b_one_out,
                               b_norm2=b_norm2, b_gates=b_gates, b_split=b_split, b_max=b_max, b_shift=b_shift,
                               b_top2=b_top2, b_mix=b_mix, b_weigh=b_weigh, b_gather=b_gather, b_out=b_out)
                    for name, i in steps:
                        if name in own:
                            own[name](i)

            nc.all_engine_barrier(sems_to_clear=seq_sems)

        sequences([(name, i) for name, i, _ in STEPS_A], 0, None)
        with nc.Fori(0, B - 1) as b:
            sequences(interleave(STEPS_A, STEPS_B), b + 1, b)
        sequences([(name, i) for name, i, _ in STEPS_B], None, B - 1)


_INS = ['x', 'ctx_512', 'L0_xattn_Wk', 'L0_xattn_bk', 'L0_xattn_Wq', 'L0_xattn_bq', 'L0_xattn_Wv', 'L0_xattn_bv',
        'L0_xattn_Wck', 'L0_xattn_bck', 'L0_xattn_Wcq', 'L0_xattn_bcq', 'L0_xattn_Wcv', 'L0_xattn_bcv', 'L0_xattn_Wp',
        'L0_xattn_bp', 'L0_ffn_W_router', 'L0_ffn_b_router', 'L0_ffn_W1', 'L0_ffn_b1', 'L0_ffn_W2', 'L0_ffn_b2',
        'L1_xattn_Wq', 'L1_xattn_bq', 'L1_xattn_Wk', 'L1_xattn_bk', 'L1_xattn_Wv', 'L1_xattn_bv', 'L1_ffn_Wq',
        'L1_ffn_Wk', 'L1_ffn_Wv', 'L1_ffn_Ws', 'L1_ffn_Wd', 'L1_ffn_Wo']


def kernel(**inputs):
    import numpy as _np
    import concourse.bacc as _bacc
    from concourse import mybir as _mybir
    from concourse.bass_utils import run_bass_kernel_spmd as _run

    nc = _bacc.Bacc("TRN2", target_bir_lowering=False, num_devices=1)
    arrays, aps = {}, {}
    for name in _INS:
        v = _np.ascontiguousarray(inputs[name])
        arrays[f"in_{name}_dram"] = v
        aps[name] = nc.dram_tensor(f"in_{name}_dram", v.shape, _mybir.dt.from_np(v.dtype), kind="ExternalInput").ap()
    out = nc.dram_tensor("out_0_dram", inputs["x"].shape, _mybir.dt.float32, kind="ExternalOutput").ap()
    transformer_program(nc, aps, out)
    r = _run(nc, [arrays], core_ids=[0])
    return r.results[0]["out_0_dram"]
```

```python
from contextlib import ExitStack

import concourse.bass as bass
from concourse import mybir

F32 = mybir.dt.float32
F32R = mybir.dt.float32r
BF16 = mybir.dt.bfloat16
I32 = mybir.dt.int32
ALU = mybir.AluOpType
ACT = mybir.ActivationFunctionType
AX = mybir.AxisListType.X

P = 128
MASKED = -1.0e30
EPS = 1.0e-5
RSQRT_MAGIC = 0x5F3759DF
SELF, CROSS = 0, 1
Q0, K0, QC, KC = range(4)


def transformer_program(nc, a, out):
    B, T, C = a["x"].shape
    CC = a["ctx_512"].shape[2]
    H = 16
    D = C // H
    NT = T // P
    G = H // 4
    E = a["L0_ffn_W_router"].shape[1]
    F = a["L0_ffn_W1"].shape[2]
    FC = F // P
    HB, DH, _ = a["L1_ffn_Wq"].shape
    PR = HB // 2
    SC0 = float(D) ** -0.5
    SC1 = float(DH) ** -0.5
    assert (C, T, D, DH, NT, HB, E) == (P, 2 * P, 8, 64, 2, 16, 8)

    ctx = ExitStack()
    with ctx:
        def sb(name, shape, dt=F32):
            return ctx.enter_context(nc.sbuf_tensor(name, shape, dt))

        def sem(name):
            return ctx.enter_context(nc.semaphore(name))

        banks = [ctx.enter_context(nc.psum_tensor(f"bank{i}", [P, 512], F32)) for i in range(8)]
        BA, BB = banks[:4], banks[4:]

        ident = sb("ident", [P, P])
        ident_b = sb("ident_b", [P, P], BF16)
        mask_qk = sb("mask_qk", [P, P], BF16)
        mask_kq = sb("mask_kq", [P, P], BF16)
        ones = sb("ones", [1, P])
        w_stack = sb("w_stack", [P, 4, G, P])
        wv0 = sb("wv0", [P, P])
        wcv0 = sb("wcv0", [CC, P])
        wp0 = sb("wp0", [P, P])
        w_router = sb("w_router", [P, E])
        w1 = sb("w1", [P, E, F])
        w2 = sb("w2", [P, E, FC, P])
        b2 = sb("b2", [E, P])
        wq1 = sb("wq1", [P, P])
        wk1 = sb("wk1", [CC, P])
        wv1 = sb("wv1", [CC, P])
        wqk_t = sb("wqk_t", [P, 2, PR, P])
        wv_t = sb("wv_t", [P, E * DH])
        wgate_t = sb("wgate_t", [P, 2, HB * E])
        wo_t = sb("wo_t", [P, E // 2, P])
        brow = sb("brow", [1, 6, P])
        bias_c = sb("bias_c", [P, 4 * G])
        lo_c = sb("lo_c", [P, 2])
        lo_bias = sb("lo_bias", [P, 4 * G])
        b1_rows = sb("b1_rows", [E * FC, P])
        b1_c = sb("b1_c", [P, E * FC])
        bqk_rows = sb("bqk_rows", [2, P])
        bqk_c = sb("bqk_c", [P, 2])
        rank = sb("rank", [P, E])
        ident_r = sb("ident_r", [P, P], F32R)
        shift_c = sb("shift_c", [P, 1])

        x_f = sb("x_f", [P, NT, C])
        cx_f = sb("cx_f", [P, NT, CC])
        x_a = sb("x_a", [P, NT, C])
        xnT_a = sb("xnT_a", [P, T])
        cxT_a = sb("cxT_a", [CC, T])
        hi_part = sb("hi_part", [P, 4, T])
        qs = sb("qs", [P, 2, G, T], F32R)
        ks = sb("ks", [P, 2, G, T], F32R)
        DV = D + 1
        va = sb("va", [P, 2, NT, H * DV + 32 - DV])
        negmax = sb("negmax", [P, 3 * D + P + 32])
        NPA = 9
        pa = sb("pa", [P, NPA, 512])
        oT = [hi_part, sb("oT_cross", [P, 4, T])]
        recA = sb("recA", [P, 2, H])
        yh = sb("yh", [P, 2, C])
        yT = sb("yT", [P, T])
        lg = sb("lg", [P, NT, E])
        m1 = sb("m1", [P, NT])
        ex = sb("ex", [P, NT, E])
        wr = sb("wr", [P, NT, E])
        wrT = sb("wrT", [E, T])
        top_a = [sb(f"top_a{i}", [P, NT * E]) for i in range(4)] + [sb("top_am", [P, NT])]
        hT = pa[:, 0:4, :].rearrange("p u (c n) -> p u c n", c=2)
        x_mid = sb("x_mid", [P, NT, C])
        p1 = pa[:, 0, :].rearrange("p (t n) -> p t n", t=NT)
        p1T = pa[:, 1, :].rearrange("p (t n) -> p t n", t=NT)
        q1T, k1T = pa[:, 2, 0:T], pa[:, 2, T:2 * T]
        v1 = pa[:, 3, 0:NT * P].rearrange("p (t n) -> p t n", t=NT)
        nm1 = sb("nm1", [P, NT])
        rs1 = sb("rs1", [P, NT])
        rr1 = sb("rr1", [P, NT])
        x_b = sb("x_b", [P, NT, C])
        xnT_b = sb("xnT_b", [P, T])
        gates = sb("gates", [P, 2, NT, HB * E])
        eg = sb("eg", [P, NT, HB * E])
        mix = sb("mix", [P, NT, HB * E])
        mout = gates[:, 0, :, :]
        pvs = sb("pvs", [P, NT, E * DH])
        qk_hi = sb("qk_hi", [P, 2, PR, T], F32R)
        qk_lo = sb("qk_lo", [P, 2, PR, T], F32R)
        negc = sb("negc", [P, NT, P])
        cT = sb("cT", [P, T], F32R)
        NG = 2 * E * DH
        prod = sb("prod", [P, 2 * NG])
        NPB = 8
        pb = sb("pb", [P, NPB, NT * T])
        vb = sb("vb", [P, NT, HB, DH + 1])
        at = sb("at", [P, NT, HB, DH + 1])
        recB = sb("recB", [P, NT * HB])
        n_gate = 2 * NT * HB * E
        top_b = [sb("top_b0", [P, n_gate]), prod[:, 0:n_gate], prod[:, n_gate:2 * n_gate], prod[:, 2 * n_gate:3 * n_gate],
                 sb("top_bm", [P, 2 * NT * HB])]
        z = pb[:, 0:NT, :]
        zT = pvs[:, :, :].rearrange("p t (c n) -> p t c n", c=E // 2)
        ln = {s: dict(stat=sb(f"stat_{s}", [P, NT, 6]), mv=sb(f"mv_{s}", [P, NT, 2]), ve=sb(f"ve_{s}", [P, NT]),
                      sq=sb(f"sq_{s}", [P, NT]), half=sb(f"half_{s}", [P, NT]), rstd=sb(f"rstd_{s}", [P, NT]),
                      xn=sb(f"xn_{s}", [P, NT, C]) if s != "f" else None) for s in "abf"}
        ln["f"]["xn"] = ln["a"]["xn"]
        y = ln["a"]["xn"]
        xn_a, xn_b = ln["a"]["xn"], ln["b"]["xn"]

        bstack = at[0:1, :, :, :].rearrange("p t h d -> p (t h d)")[:, 0:4 * G * P].rearrange("p (k n) -> p k n", k=4)
        brow_raw = hi_part[0:1, 0:2, :].rearrange("p a n -> p (a n)").rearrange("p (k n) -> p k n", k=4)
        lo_row = hi_part[0:1, 2:4, :].rearrange("p a n -> p (a n)")[:, 0:3 * P].rearrange("p (k n) -> p k n", k=3)
        raw0 = prod[:, 0:4 * P].rearrange("p (k n) -> p k n", k=4)
        rawqk = pb[:, 0:4, :].rearrange("p a n -> p (a n)").rearrange("p (k r n) -> p k r n", k=2, r=PR)
        rawv = pb[:, 4, :].rearrange("p (r n) -> p r n", r=4)
        rawg = pb[:, 5, 0:2 * P].rearrange("p (r n) -> p r n", r=2)
        rawo = pb[:, 6, :].rearrange("p (e d) -> p e d", e=E)

        s_w = sem("s_w")
        s_experts = sem("s_experts")
        s_const = sem("s_const")
        s_fill = sem("s_fill")
        s_spread = sem("s_spread")
        s_turn = sem("s_turn")
        s_turnc = sem("s_turnc")
        names = ["v_link", "f_in", "a_xn", "a_xt", "a_xc", "a_pj", "a_mh", "a_split", "a_vp", "a_vc", "a_s",
                 "a_mx", "a_ct", "a_qs", "a_st", "a_ex", "a_pv", "a_ot", "a_tr", "a_y", "a_yt", "a_yc", "a_o",
                 "a_x1", "a_lg", "a_lgc", "a_lx", "a_w", "a_h", "a_ha", "a_yp", "a_acc", "a_wt", "a_wtc",
                 "a_b2", "b_xn", "b_xt", "b_xc", "c_qk", "c_qc", "c_s1", "c_m1", "c_e1", "c_pt", "c_pc", "c_o1",
                 "b_g", "b_gc", "b_sg", "b_pvj", "b_pvc", "b_qkp", "b_hi", "b_lo", "b_s", "b_mx", "b_ct", "b_cc",
                 "b_st", "b_ex", "b_vm", "b_pv", "b_at", "b_z", "b_zt", "b_zc", "b_ro", "b_xo", "a_out", "b_x1", "f_xn", "f_xt",
                 "b_mw", "b_vp", "b_zp"]
        S = {n: sem(n) for n in names}
        first_sem = min(s.num for s in S.values())
        assert max(s.num for s in S.values()) - first_sem == len(names) - 1
        seq_sems = range(first_sem, first_sem + len(names))

        with nc.Block() as block:
            loads = [
                (raw0[:, Q0, :], a["L0_xattn_Wq"]), (raw0[:, K0, :], a["L0_xattn_Wk"]),
                (raw0[:, QC, :], a["L0_xattn_Wcq"]), (raw0[0:CC, KC, :], a["L0_xattn_Wck"]),
                (brow_raw[0:1, Q0, :], a["L0_xattn_bq"].unsqueeze(0)), (brow_raw[0:1, K0, :], a["L0_xattn_bk"].unsqueeze(0)),
                (brow_raw[0:1, QC, :], a["L0_xattn_bcq"].unsqueeze(0)), (brow_raw[0:1, KC, :], a["L0_xattn_bck"].unsqueeze(0)),
                (brow[0:1, 0, :], a["L0_xattn_bv"].unsqueeze(0)), (brow[0:1, 1, :], a["L0_xattn_bcv"].unsqueeze(0)),
                (brow[0:1, 2, :], a["L0_xattn_bp"].unsqueeze(0)), (brow[0:1, 3, :], a["L1_xattn_bv"].unsqueeze(0)),
                (brow[0:1, 4, 0:E], a["L0_ffn_b_router"].unsqueeze(0)),
                (b1_rows[:, :], a["L0_ffn_b1"].rearrange("e (c n) -> (e c) n", n=P)),
                (bqk_rows[0:1, :], a["L1_xattn_bq"].unsqueeze(0)), (bqk_rows[1:2, :], a["L1_xattn_bk"].unsqueeze(0)),
                (wv0[:, :], a["L0_xattn_Wv"]), (wcv0[:, :], a["L0_xattn_Wcv"]), (wp0[:, :], a["L0_xattn_Wp"]),
                (w_router[:, :], a["L0_ffn_W_router"]), (b2[:, :], a["L0_ffn_b2"]),
                (wq1[:, :], a["L1_xattn_Wq"]), (wk1[:, :], a["L1_xattn_Wk"]), (wv1[:, :], a["L1_xattn_Wv"]),
                (rawg[:, 0, :], a["L1_ffn_Ws"].rearrange("h e c -> (h e) c")),
                (rawg[:, 1, :], a["L1_ffn_Wd"].rearrange("h e c -> (h e) c")),
                (rawv, a["L1_ffn_Wv"].rearrange("e d c -> (e d) c").rearrange("(r p) c -> p r c", p=P)),
                (rawo, a["L1_ffn_Wo"].rearrange("e f d -> f e d")),
                (rawqk[:, 0], a["L1_ffn_Wq"].rearrange("h d c -> (h d) c").rearrange("(r p) c -> p r c", p=P)),
                (rawqk[:, 1], a["L1_ffn_Wk"].rearrange("h d c -> (h d) c").rearrange("(r p) c -> p r c", p=P)),
            ]
            expert_loads = [
                (w1[:, :, :], a["L0_ffn_W1"].rearrange("e c f -> c e f")),
                (w2[:, :, :, :], a["L0_ffn_W2"].rearrange("e (k p) n -> p e k n", p=P)),
            ]

            N_CONST = 4 + E + 4
            N_SPREAD = 3 + 4 * 6 + 2 + 2 + 3
            turned_to = [wqk_t[:, k, 4 * i:4 * i + 4, :].rearrange("p r n -> p (r n)") for k in range(2) for i in range(2)]
            turned_to += [wv_t[:, :], wo_t[:, :, :].rearrange("p r n -> p (r n)")]
            turned_from = [[rawqk[:, k, 4 * i + r, :] for r in range(4)] for k in range(2) for i in range(2)]
            turned_from += [[rawv[:, r, :] for r in range(4)],
                            [rawo[:, 2 * r:2 * r + 2, :].rearrange("p e d -> p (e d)") for r in range(4)]]

            @block.sync
            def _(sp):
                for dst, src in loads:
                    sp.dma_start(dst, src).then_inc(s_w, 16)

            @block.gpsimd
            def _(pool):
                nc.gpsimd.memset(ident[:, :], 0.0).then_inc(s_fill, 1)
                nc.gpsimd.memset(mask_qk[:, :], 0.0).then_inc(s_fill, 1)
                nc.gpsimd.memset(mask_kq[:, :], 0.0).then_inc(s_fill, 1)
                nc.gpsimd.memset(ones[:, :], 1.0).then_inc(s_const, 1)
                nc.gpsimd.memset(va[:, :, :, :], 0.0).then_inc(s_fill, 1)
                nc.gpsimd.memset(negmax[:, :], 0.0).then_inc(s_const, 1)
                nc.gpsimd.memset(negc[:, :, :], 0.0).then_inc(s_const, 1)
                nc.gpsimd.memset(vb[:, :, :, DH:DH + 1], 1.0).then_inc(s_const, 1)
                for e in range(E):
                    nc.gpsimd.memset(rank[:, e:e + 1], float(E - e)).then_inc(s_const, 1)
                pool.wait_ge(s_fill, 4)
                nc.gpsimd.affine_select(out=ident[:, :], in_=ident[:, :], compare_op=ALU.not_equal, fill=1.0,
                                        base=0, pattern=[[-1, P]], channel_multiplier=1).then_inc(s_const, 1)
                nc.gpsimd.affine_select(out=mask_qk[:, :], in_=mask_qk[:, :], compare_op=ALU.is_ge, fill=MASKED,
                                        base=0, pattern=[[-1, P]], channel_multiplier=1).then_inc(s_const, 1)
                nc.gpsimd.affine_select(out=mask_kq[:, :], in_=mask_kq[:, :], compare_op=ALU.is_ge, fill=MASKED,
                                        base=0, pattern=[[1, P]], channel_multiplier=-1).then_inc(s_const, 1)
                nc.gpsimd.memset(va[:, :, :, 0:H * DV].rearrange("p s t (h d) -> p s t h d", d=DV)[:, :, :, :, D:DV],
                                 1.0).then_inc(s_const, 1)

            @block.vector
            def _(dve):
                nc.vector.memset(w_stack[:, :, :, :], 0.0).then_inc(s_spread, 1)
                nc.vector.memset(bstack[:, :, :], 0.0).then_inc(s_spread, 1)
                nc.vector.memset(lo_row[:, :, :], 0.0).then_inc(s_spread, 1)
                dve.wait_ge(s_spread, 3)
                dve.wait_ge(s_w, 16 * len(loads))
                for kind in range(4):
                    rows = CC if kind == KC else P
                    w = w_stack[0:rows, kind, :, :].rearrange("p g (j r) -> p (g j) r", r=32)
                    b = bstack[:, kind, :].rearrange("p (h r) -> p h r", r=32)
                    for r in range(3):
                        nc.vector.tensor_copy(w[:, :, r * D:(r + 1) * D],
                                              raw0[0:rows, kind, :].rearrange("p (h d) -> p h d", d=D)).then_inc(s_spread, 1)
                        nc.vector.tensor_copy(b[:, :, r * D:(r + 1) * D],
                                              brow_raw[:, kind, :].rearrange("p (h d) -> p h d", d=D)).then_inc(s_spread, 1)
                    if kind in (K0, KC):
                        nc.vector.memset(b[:, :, 3 * D:3 * D + 1], 1.0).then_inc(s_spread, 1)
                nc.vector.memset(lo_row[:, 0, :].rearrange("p (j r) -> p j r", r=32)[:, :, 2 * D:3 * D], 1.0).then_inc(s_spread, 1)
                nc.vector.memset(lo_row[:, 1, :].rearrange("p (j r) -> p j r", r=32)[:, :, D:2 * D], 1.0).then_inc(s_spread, 1)
                dve.wait_ge(s_const, N_CONST)
                nc.vector.tensor_copy(ident_b[:, :], ident[:, :]).then_inc(s_spread, 1)
                nc.vector.tensor_copy(ident_r[:, :], ident[:, :]).then_inc(s_spread, 1)
                nc.vector.memset(lo_row[:, 2, :].rearrange("p (j r) -> p j r", r=32)[:, :, 3 * D:3 * D + 1], 1.0).then_inc(s_spread, 1)
                dve.wait_ge(s_turn, 1)
                nc.vector.tensor_copy(bias_c[:, :], banks[0][:, 0:4 * G]).then_inc(s_spread, 1)
                nc.vector.tensor_copy(lo_c[:, :], banks[0][:, 4 * G:4 * G + 2]).then_inc(s_spread, 1)
                nc.vector.tensor_copy(shift_c[:, :], banks[0][:, 4 * G + 2:4 * G + 3]).then_inc(s_spread, 1)
                nc.vector.tensor_copy(b1_c[:, :], banks[0][:, 32:32 + E * FC]).then_inc(s_spread, 1)
                nc.vector.tensor_copy(bqk_c[:, :], banks[0][:, 96:98]).then_inc(s_spread, 1)
                dve.wait_ge(s_spread, N_SPREAD + 5)
                for kind in range(4):
                    nc.vector.tensor_scalar(lo_bias[:, kind * G:(kind + 1) * G], bias_c[:, kind * G:(kind + 1) * G],
                                            lo_c[:, kind % 2:kind % 2 + 1], None, ALU.mult).then_inc(s_spread, 1)
                for n, dst in enumerate(turned_to):
                    dve.wait_ge(s_turn, n + 2)
                    nc.vector.tensor_copy(dst, banks[1 + n % 7][:, :]).then_inc(s_turnc, 1)

            @block.scalar
            def _(act):
                for dst, src in expert_loads:
                    act.dma_start(dst, src).then_inc(s_experts, 16)
                act.wait_ge(s_turn, len(turned_to) + 2)
                nc.scalar.copy(wgate_t[:, :, :].rearrange("p k n -> p (k n)"), banks[7][:, 0:2 * P]).then_inc(s_turnc, 1)

            @block.tensor
            def _(pe):
                pe.wait_ge(s_w, 16 * len(loads))
                pe.wait_ge(s_const, N_CONST)
                pe.wait_ge(s_spread, N_SPREAD)
                for i in range(4 * G):
                    pe.matmul(banks[0][:, i:i + 1], bstack[0:1, i // G, (i % G) * P:(i % G + 1) * P], ones[0:1, 0:1],
                              start=True, stop=True)
                for i in range(3):
                    pe.matmul(banks[0][:, 4 * G + i:4 * G + i + 1], lo_row[0:1, i, :], ones[0:1, 0:1], start=True, stop=True)
                pe.transpose(banks[0][:, 32:32 + E * FC], b1_rows[:, :], ident[0:E * FC, 0:E * FC])
                pe.transpose(banks[0][:, 96:98], bqk_rows[:, :], ident[0:2, 0:2]).then_inc(s_turn, 1)
                for n, srcs in enumerate(turned_from):
                    for r, src in enumerate(srcs):
                        mm = pe.transpose(banks[1 + n % 7][:, r * P:(r + 1) * P], src, ident[:, :])
                    mm.then_inc(s_turn, 1)
                for r in range(2):
                    mm = pe.transpose(banks[7][:, r * P:(r + 1) * P], rawg[:, r, :], ident[:, :])
                mm.then_inc(s_turn, 1)

        def mix_products(eng, n):
            pr, t = n // 2, n % 2
            return eng.tensor_tensor(
                prod[:, t * NG:(t + 1) * NG].rearrange("p (h d e) -> p h d e", h=2, d=DH),
                mix[:, t, 2 * pr * E:2 * (pr + 1) * E].rearrange("p (h e) -> p h e", e=E).unsqueeze(2)
                .broadcast_to([P, 2, DH, E]),
                pvs[:, t, :].rearrange("p (e d) -> p d e", e=E).unsqueeze(1).broadcast_to([P, 2, DH, E]),
                ALU.mult)

        def gather_products(eng, n):
            t, e = n // E, n % E
            return eng.tensor_tensor(
                prod[:, (n % 2) * NG:(n % 2 + 1) * NG].rearrange("p (d h) -> p d h", d=DH),
                mout[:, t, :].rearrange("p (h e) -> p e h", e=E)[:, e, :].unsqueeze(1).broadcast_to([P, DH, HB]),
                at[:, t, :, 0:DH].rearrange("p h d -> p d h"),
                ALU.mult)

        def norm_stats(link, inp, s):
            n = ln[s]
            for t in range(NT):
                link(nc.vector.bn_stats(n["stat"][:, t, :], inp[:, t, :]), wait=(t == NT - 1))
            for t in range(NT):
                link(nc.vector.bn_aggr(n["mv"][:, t, :], n["stat"][:, t, :]), wait=(t == NT - 1))
            link(nc.vector.tensor_scalar(n["ve"][:, :], n["mv"][:, :, 1], EPS, None, ALU.add))
            link(nc.vector.tensor_scalar(n["rstd"][:, :].bitcast(I32), n["ve"][:, :].bitcast(I32), -0.5, float(RSQRT_MAGIC),
                                         ALU.mult, ALU.add))

        def norm_root(link, s):
            n = ln[s]
            ve, sq, half, rstd = n["ve"], n["sq"], n["half"], n["rstd"]
            for step in range(3):
                link(nc.vector.tensor_tensor(sq[:, :], rstd[:, :], rstd[:, :], ALU.mult))
                link(nc.vector.scalar_tensor_tensor(half[:, :], sq[:, :], -0.5, ve[:, :], ALU.mult, ALU.mult))
                link(nc.vector.scalar_tensor_tensor(rstd[:, :], half[:, :], 1.5, rstd[:, :], ALU.add, ALU.mult))

        def norm_apply(inp, s, done):
            n = ln[s]
            for t in range(NT):
                ins = nc.vector.tensor_scalar(n["xn"][:, t, :], inp[:, t, :], n["mv"][:, t, 0:1], n["rstd"][:, t:t + 1],
                                              ALU.subtract, ALU.mult)
            ins.then_inc(done, 1)

        def top2_vector(link, vals, n, bufs):
            f1, f2, ta, tb = [b[:, 0:n * E].rearrange("p (n e) -> p n e", e=E) for b in bufs[:4]]
            v, m = vals.rearrange("p (n e) -> p n e", e=E), bufs[4][:, 0:n]

            def wide(s):
                return s.unsqueeze(2).broadcast_to([P, n, E])

            ranks = rank[:, :].unsqueeze(1).broadcast_to([P, n, E])
            for f, src in ((f1, v), (f2, ta)):
                link(nc.vector.tensor_reduce(m, src, AX, ALU.max))
                link(nc.vector.tensor_tensor(tb, src, wide(m), ALU.is_ge))
                link(nc.vector.tensor_tensor(tb, tb, ranks, ALU.mult))
                link(nc.vector.tensor_reduce(m, tb, AX, ALU.max))
                link(nc.vector.tensor_tensor(f, tb, wide(m), ALU.is_equal))
                if f is f1:
                    link(nc.vector.scalar_tensor_tensor(ta, f, MASKED, v, ALU.mult, ALU.add))
            link(nc.vector.tensor_tensor(f1, f1, f2, ALU.add))

        MAXS = [(CROSS, qt, j, gp) for qt in range(NT) for gp in range(2) for j in range(4)]
        MAXS += [(SELF, 0, j, None) for j in range(4)]
        MAXS += [(SELF, 1, j, gp) for gp in range(2) for j in range(4)]
        NS = len(MAXS)
        PER_J = 7
        assert NS == 4 * PER_J == 28
        KINDS = (Q0, K0, QC, KC)

        x_tiles = a["x"].rearrange("b (t p) c -> p (b t) c", p=P)
        ctx_tiles = a["ctx_512"].rearrange("b (t p) c -> p (b t) c", p=P)
        out_tiles = out.rearrange("b (t p) c -> p (b t) c", p=P)

        RUNS = {"a_max": 8, "a_score": 7, "a_expert": 4, "b_score": 4, "b_mix": 4, "b_gather": 8}
        HOLD = {
            "a_stack": 1.0, "a_values": 1.29, "a_max": (0.86, 1.88, 0.73, 2.55), "a_shift": 3,
            "a_score": (1, 0.92, 1.02, 0.99), "a_lastpv": 2.07, "a_heads": 4.0, "a_project": 1.88, "a_norm2": 4.26,
            "a_norm2_apply": 1.04, "a_router": 6.19, "a_expert": (4, 4.01), "a_b2": 12, "c_norm": 3.31,
            "f_norm": 0.77, "c_norm_apply": 1.29, "c_qkv": 3.77, "f_norm_apply": 1, "c_max": 1.57, "c_turn": 1.62,
            "c_out": 1.74, "b_norm": 2.87, "b_norm_apply": 3, "b_gates": 2.98, "b_split": 0.98, "b_top2": 8,
            "b_max": 0.7, "b_shift": 7.07, "b_score": (2.08, 0.1, 1.0, 0.76), "b_mix": (1.4, 0.8, 1.39, 1.41),
            "b_attend": 2.58, "b_weigh": 0.97, "b_gather": (4.09, 2), "b_out": 0.05}

        def share(step):
            name, i = step
            return HOLD[name][i // RUNS[name]] if name in RUNS else HOLD[name]

        STEPS_A = [("a_stack", u) for u in range(8)] + [("a_values", 0)]
        STEPS_A += [("a_max", n) for n in range(NS)] + [("a_shift", 0)]
        STEPS_A += [("a_score", n) for n in range(NS)] + [("a_lastpv", 0), ("a_heads", 0), ("a_project", 0)]
        STEPS_A += [("a_norm2", 0), ("a_norm2_apply", 0), ("a_router", 0)]
        STEPS_A += [("a_expert", e) for e in range(E)] + [("a_b2", 0)]
        STEPS_A += [("c_norm", 0), ("f_norm", 0), ("c_norm_apply", 0), ("c_qkv", 0), ("f_norm_apply", 0),
                    ("c_max", 0), ("c_turn", 0), ("c_out", 0)]
        STEPS_B = [("b_norm", 0), ("b_norm_apply", 0), ("b_gates", 0)]
        STEPS_B += [("b_split", u) for u in range(8)]
        STEPS_B += [("b_top2", 0)] + [("b_max", n) for n in range(16)] + [("b_shift", 0)]
        for hg in range(4):
            STEPS_B += [("b_score", h) for h in range(4 * hg, 4 * hg + 4)]
            STEPS_B += [("b_mix", n) for n in range(4 * hg, 4 * hg + 4)]
            STEPS_B += [("b_attend", hg - 1)] if hg >= 1 else []
        STEPS_B += [("b_attend", 3), ("b_weigh", 0)] + [("b_gather", n) for n in range(NT * E)] + [("b_out", 0)]

        def interleave(first, second):
            timed = []
            for steps in (first, second):
                total, at_ = sum(share(step) for step in steps), 0
                for name, i in steps:
                    w = share((name, i))
                    timed.append(((at_ + w / 2) / total, name, i))
                    at_ += w
            return [(name, i) for _, name, i in sorted(timed, key=lambda s: s[0])]

        def sequences(steps, seq_f, seq_a, seq_b):
            taken = {"f": seq_f, "a": seq_a, "c": seq_a, "b": seq_b}
            steps = [(name, i) for name, i in steps if taken[name[0]] is not None]

            with nc.Block(no_gpsimd_drain=True) as block:

                @block.sync
                def _(sp):
                    if seq_f is not None:
                        sp.dma_start(cx_f[:, :, :], ctx_tiles[:, bass.ds(seq_f * NT, NT), :]).then_inc(S["f_in"], 16)
                        if seq_a is not None:
                            sp.wait_ge(S["a_x1"], 1)
                        sp.dma_start(x_f[:, :, :], x_tiles[:, bass.ds(seq_f * NT, NT), :]).then_inc(S["f_in"], 16)
                    if seq_b is not None:
                        sp.wait_ge(S["b_xo"], NT)
                        sp.dma_start(out_tiles[:, bass.ds(seq_b * NT, NT), :], x_b[:, :, :]).then_inc(S["a_out"], 16)
                        sp.wait_ge(S["a_out"], 16)

                @block.tensor
                def _(pe):
                    def turn_tokens(bank, src, done):
                        for t in range(NT):
                            mm = pe.transpose(bank[:, t * P:(t + 1) * P], src[:, t, :], ident[:, :])
                        mm.then_inc(done, 1)

                    def add_row(dst, row):
                        return pe.matmul(dst, ones[0:1, :], row, start=False, stop=True)

                    def add_mask(dst, mask, n):
                        return pe.matmul(dst, ident_b[:, :], mask[:, :].unsqueeze(1).broadcast_to([P, n, P]),
                                         start=False, stop=True, skip_group_check=True)

                    def f_norm_apply(_):
                        pe.wait_ge(S["f_in"], 32)
                        if seq_a is not None:
                            pe.wait_ge(S["c_qc"], 3)
                        for t in range(NT):
                            pe.transpose(BA[2][0:CC, T + t * P:T + (t + 1) * P], cx_f[:, t, :], ident[:, :])
                        pe.wait_ge(S["f_xn"], 1)
                        turn_tokens(BA[2], xn_a, S["f_xt"])

                    def a_stack(u):
                        kind = KINDS[u // 2]
                        if u >= 4:
                            pe.wait_ge(S["a_split"], 2 * (u - 4) + 2)
                        for c in range(2):
                            g = 2 * (u % 2) + c
                            rows, rhs = (CC, cxT_a) if kind == KC else (P, xnT_a)
                            mm = pe.matmul(BA[u % 4][:, c * T:(c + 1) * T], w_stack[0:rows, kind, g, :], rhs[:, :],
                                           start=True, stop=True)
                        mm.then_inc(S["a_pj"], 1)

                    def a_values(_):
                        pe.wait_ge(S["a_split"], 10)
                        for sc in range(2):
                            for t in range(NT):
                                lhs, rhs = (xnT_a[:, t * P:(t + 1) * P], wv0) if sc == SELF else (cxT_a[:, t * P:(t + 1) * P], wcv0)
                                dst = BA[0][:, (2 * sc + t) * P:(2 * sc + t + 1) * P]
                                pe.matmul(dst, lhs, rhs[:, :], start=True, stop=False)
                                mm = add_row(dst, brow[0:1, sc, :])
                        mm.then_inc(S["a_vp"], 1)

                    def a_max(n):
                        sc, qt, j, gp = MAXS[n]
                        bank = BA[n % 4]
                        if n == 0:
                            pe.wait_ge(S["a_split"], 16)
                            pe.wait_ge(S["a_vc"], 1)
                        if n >= 4:
                            pe.wait_ge(S["a_mx"], n - 3)
                        rows = slice(32 * j, 32 * j + 32)
                        masked = sc == SELF
                        if masked and qt == 0:
                            for g in range(4):
                                pe.matmul(bank[:, g * P:(g + 1) * P], qs[rows, sc, g, 0:P], ks[rows, sc, g, 0:P],
                                          start=(g == 0), stop=True, skip_group_check=True)
                            mm = add_mask(bank[:, :].rearrange("p (g k) -> p g k", g=4), mask_qk, 4)
                        else:
                            for c in range(2):
                                g = 2 * gp + c
                                mm = pe.matmul(bank[:, c * T:(c + 1) * T], qs[rows, sc, g, qt * P:(qt + 1) * P],
                                               ks[rows, sc, g, :], start=(c == 0), stop=True, skip_group_check=True)
                            if masked:
                                mm = add_mask(bank[:, :].rearrange("p (g k) -> p g k", g=2)[:, :, P:2 * P], mask_qk, 2)
                        mm.then_inc(S["a_s"], 1)

                    def a_shift(_):
                        pe.wait_ge(S["a_mx"], NS)
                        for m in range(4):
                            qt, sc = m // 2, m % 2
                            for g in range(G):
                                i = (qt * 2 + sc) * G + g
                                mm = pe.transpose(BA[m][:, g * P:(g + 1) * P], negmax[:, i:i + P], ident[:, :])
                            mm.then_inc(S["a_ct"], 1)

                    def values(j, sc, kt):
                        bank = BA[3] if sc == SELF else BA[2]
                        unit = PER_J * j
                        if kt == 0:
                            pe.wait_ge(S["a_ex"], unit + (PER_J if sc == SELF else 4))
                            if j >= 1:
                                pe.wait_ge(S["a_ot"], 2 * (j - 1) + (2 if sc == SELF else 1))
                        for g in range(G):
                            h = 4 * g + j
                            dst = bank[32 * g:32 * g + 32, 0:T]
                            if sc == CROSS:
                                rhs = pa[:, (unit + g) % NPA, kt * T:(kt + 1) * T]
                            elif kt == 0:
                                rhs = pa[:, (unit + 4 + g // 2) % NPA, (g % 2) * T:(g % 2 + 1) * T]
                            else:
                                rhs = pa[:, (unit + 6) % NPA, g * P:(g + 1) * P]
                                dst = bank[32 * g:32 * g + 32, P:T]
                            mm = pe.matmul(dst, va[:, sc, kt, h * DV:h * DV + 32], rhs, start=(kt == 0),
                                           stop=(sc == SELF or kt == 1), skip_group_check=True)
                        if kt == 1:
                            mm.then_inc(S["a_pv"], 1)

                    VALUE_PARTS = ((CROSS, 0), (CROSS, 1), (SELF, 0), (SELF, 1))

                    def a_score(n):
                        j, k = n // PER_J, n % PER_J
                        bank = BA[n % 2]
                        rows = slice(32 * j, 32 * j + 32)
                        if n == 0:
                            pe.wait_ge(S["a_qs"], 4)
                        if n >= 2:
                            pe.wait_ge(S["a_ex"], n - 1)
                        if k < 4:
                            for kt in range(NT):
                                mm = pe.matmul(bank[:, kt * T:(kt + 1) * T], ks[rows, CROSS, k, kt * P:(kt + 1) * P],
                                               qs[rows, CROSS, k, :], start=True, stop=True)
                        elif k < 6:
                            for c in range(2):
                                g = 2 * (k - 4) + c
                                pe.matmul(bank[:, c * T:(c + 1) * T], ks[rows, SELF, g, 0:P], qs[rows, SELF, g, :],
                                          start=(c == 0), stop=True, skip_group_check=True)
                            mm = add_mask(bank[:, :].rearrange("p (g q) -> p g q", g=2)[:, :, 0:P], mask_kq, 2)
                        else:
                            for g in range(G):
                                pe.matmul(bank[:, g * P:(g + 1) * P], ks[rows, SELF, g, P:T], qs[rows, SELF, g, P:T],
                                          start=(g == 0), stop=True, skip_group_check=True)
                            mm = add_mask(bank[:, :].rearrange("p (g q) -> p g q", g=4), mask_kq, 4)
                        mm.then_inc(S["a_st"], 1)
                        if j >= 1 and k in (1, 2, 3, 4):
                            values(j - 1, *VALUE_PARTS[k - 1])

                    def a_lastpv(_):
                        for part in VALUE_PARTS:
                            values(3, *part)

                    def a_heads(_):
                        pe.wait_ge(S["a_ot"], 8)
                        for m in range(4):
                            qt, sc = m // 2, m % 2
                            for j in range(4):
                                mm = pe.transpose(BA[m][:, j * P:(j + 1) * P], oT[sc][:, j, qt * P:(qt + 1) * P], ident[:, :])
                            mm.then_inc(S["a_tr"], 1)

                    def a_project(_):
                        pe.wait_ge(S["a_y"], 2)
                        turn_tokens(BA[0], y, S["a_yt"])
                        pe.wait_ge(S["a_yc"], 1)
                        for t in range(NT):
                            dst = BA[1][:, t * P:(t + 1) * P]
                            pe.matmul(dst, yT[:, t * P:(t + 1) * P], wp0[:, :], start=True, stop=False)
                            mm = add_row(dst, brow[0:1, 2, :])
                        mm.then_inc(S["a_o"], 1)

                    def a_norm2_apply(_):
                        pe.wait_ge(S["a_xn"], 1)
                        turn_tokens(BA[2], xn_a, S["a_xt"])

                    def hidden(u):
                        e, fp = u // 2, u % 2
                        if u >= 2:
                            pe.wait_ge(S["a_ha"], u - 1)
                        for c in range(2):
                            f = (2 * fp + c) * P
                            mm = pe.matmul(BA[u % 2][:, c * T:(c + 1) * T], w1[:, e, f:f + P], xnT_a[:, :],
                                           start=True, stop=True)
                        mm.then_inc(S["a_h"], 1)

                    def a_router(_):
                        pe.wait_ge(S["a_xc"], 1)
                        for t in range(NT):
                            dst = BA[3][:, t * E:(t + 1) * E]
                            pe.matmul(dst, xnT_a[:, t * P:(t + 1) * P], w_router[:, :], start=True, stop=False)
                            mm = add_row(dst, brow[0:1, 4, 0:E])
                        mm.then_inc(S["a_lg"], 1)
                        pe.wait_ge(S["a_x1"], 1)
                        pe.wait_ge(s_experts, 32)
                        hidden(0)
                        hidden(1)

                    def a_expert(e):
                        if e + 1 < E:
                            hidden(2 * e + 2)
                            hidden(2 * e + 3)
                        pe.wait_ge(S["a_ha"], 2 * e + 2)
                        if e == 1:
                            pe.wait_ge(S["a_lgc"], 1)
                        if e >= 2:
                            pe.wait_ge(S["a_acc"], e - 1)
                        for t in range(NT):
                            for f in range(FC):
                                mm = pe.matmul(BA[2 + e % 2][:, t * P:(t + 1) * P],
                                               hT[:, (2 * e + f // 2) % 4, f % 2, t * P:(t + 1) * P], w2[:, e, f, :],
                                               start=(f == 0), stop=(f == FC - 1))
                        mm.then_inc(S["a_yp"], 1)

                    def a_b2(_):
                        pe.wait_ge(S["a_w"], 1)
                        pe.wait_ge(S["a_ha"], 2 * E)
                        for t in range(NT):
                            mm = pe.transpose(BA[0][0:E, t * P:(t + 1) * P], wr[:, t, :], ident[:, :])
                        mm.then_inc(S["a_wt"], 1)
                        pe.wait_ge(S["a_wtc"], 1)
                        for t in range(NT):
                            mm = pe.matmul(BA[1][:, t * P:(t + 1) * P], wrT[:, t * P:(t + 1) * P], b2[:, :], start=True, stop=True)
                        mm.then_inc(S["a_b2"], 1)

                    def c_norm_apply(_):
                        pe.wait_ge(S["a_xn"], 2)
                        turn_tokens(BA[0], xn_a, S["a_xt"])

                    def c_qkv(_):
                        pe.wait_ge(S["a_xc"], 2)
                        pe.matmul(BA[1][:, 0:T], wq1[:, :], xnT_a[:, :], start=True, stop=True)
                        pe.matmul(BA[1][:, T:2 * T], wk1[:, :], cxT_a[:, :], start=True, stop=True).then_inc(S["c_qk"], 1)
                        for t in range(NT):
                            dst = BA[2][:, t * P:(t + 1) * P]
                            pe.matmul(dst, cxT_a[:, t * P:(t + 1) * P], wv1[:, :], start=True, stop=False)
                            mm = add_row(dst, brow[0:1, 3, :])
                        mm.then_inc(S["c_qk"], 1)

                    def c_max(_):
                        pe.wait_ge(S["c_qc"], 2)
                        for t in range(NT):
                            mm = pe.matmul(BA[3][:, t * T:(t + 1) * T], q1T[:, t * P:(t + 1) * P], k1T[:, :], start=True, stop=True)
                        mm.then_inc(S["c_s1"], 1)

                    def c_turn(_):
                        pe.wait_ge(S["c_e1"], 2)
                        for kt in range(NT):
                            for qt in range(NT):
                                mm = pe.transpose(BA[0][:, kt * T + qt * P:kt * T + (qt + 1) * P], p1[:, qt, kt * P:(kt + 1) * P],
                                                  ident[:, :])
                        mm.then_inc(S["c_pt"], 1)

                    def c_out(_):
                        pe.wait_ge(S["c_pc"], 1)
                        pe.wait_ge(S["c_qc"], 3)
                        for qt in range(NT):
                            for kt in range(NT):
                                mm = pe.matmul(BA[1][:, qt * P:(qt + 1) * P], p1T[:, kt, qt * P:(qt + 1) * P], v1[:, kt, :],
                                               start=(kt == 0), stop=(kt == 1))
                        mm.then_inc(S["c_o1"], 1)

                    def b_norm_apply(_):
                        pe.wait_ge(S["b_xn"], 1)
                        turn_tokens(BB[2], xn_b, S["b_xt"])

                    def b_gates(_):
                        pe.wait_ge(S["b_xc"], 1)
                        for t in range(NT):
                            mm = pe.matmul(BB[3][:, t * T:(t + 1) * T], xnT_b[:, t * P:(t + 1) * P],
                                           wgate_t[:, :, :].rearrange("p k n -> p (k n)"), start=True, stop=True)
                        mm.then_inc(S["b_g"], 1)
                        for t in range(NT):
                            pe.matmul(BB[t][:, :], xnT_b[:, t * P:(t + 1) * P], wv_t[:, :], start=True, stop=True)\
                              .then_inc(S["b_pvj"], 1)

                    def b_split(u):
                        if u == 1:
                            pe.wait_ge(S["b_gc"], 1)
                        elif u in (2, 3):
                            pe.wait_ge(S["b_pvc"], u - 1)
                        elif u >= 4:
                            pe.wait_ge(S["b_lo"], u - 3)
                        for c in range(2):
                            mm = pe.matmul(BB[(u + 2) % 4][:, c * T:(c + 1) * T], wqk_t[:, u // 4, 2 * (u % 4) + c, :],
                                           xnT_b[:, :], start=True, stop=True)
                        mm.then_inc(S["b_qkp"], 1)

                    def b_max(n):
                        qt, pp, j = n // 8, (n // 2) % 4, n % 2
                        rows = slice(64 * j, 64 * j + 64)
                        if n == 0:
                            pe.wait_ge(S["b_lo"], 8)
                        if n >= 4:
                            pe.wait_ge(S["b_mx"], n - 3)
                        for c in range(2):
                            mm = pe.matmul(BB[(n + 2) % 4][:, c * T:(c + 1) * T],
                                           qk_hi[rows, 0, 2 * pp + c, qt * P:(qt + 1) * P], qk_hi[rows, 1, 2 * pp + c, :],
                                           start=True, stop=True)
                        mm.then_inc(S["b_s"], 1)

                    def b_shift(_):
                        pe.wait_ge(S["b_mx"], 16)
                        turn_tokens(BB[2], negc, S["b_ct"])

                    def b_score(h):
                        pr, rows = h // 2, slice(64 * (h % 2), 64 * (h % 2) + 64)
                        if h == 0:
                            pe.wait_ge(S["b_cc"], 1)
                        if h >= 2:
                            pe.wait_ge(S["b_ex"], h - 1)
                        bank = BB[h % 2]
                        c = 64 * (h % 2) + h
                        for kt in range(NT):
                            keys = slice(kt * P, (kt + 1) * P)
                            dst = bank[:, kt * T:(kt + 1) * T]
                            pe.matmul(dst, qk_lo[rows, 1, pr, keys], qk_hi[rows, 0, pr, :], start=(kt == 0), stop=False,
                                      skip_group_check=True)
                            pe.matmul(dst, qk_hi[rows, 1, pr, keys], qk_lo[rows, 0, pr, :], start=False, stop=False,
                                      skip_group_check=True)
                            pe.matmul(dst, qk_hi[rows, 1, pr, keys], qk_hi[rows, 0, pr, :], start=False, stop=True,
                                      skip_group_check=True)
                        pe.matmul(bank[:, :].rearrange("p (k q) -> p k q", k=NT), ident_r[rows, c:c + 1].broadcast_to([64, P]),
                                  cT[rows, :].unsqueeze(1).broadcast_to([64, NT, T]), start=False, stop=True,
                                  skip_group_check=True).then_inc(S["b_st"], 1)

                    def b_attend(hg):
                        pe.wait_ge(S["b_vm"], 2 * NT * (hg + 1))
                        pe.wait_ge(S["b_ex"], 4 * hg + 4)
                        if hg == 0:
                            pe.wait_ge(S["b_cc"], 1)
                        for qt in range(NT):
                            if hg >= 1:
                                pe.wait_ge(S["b_at"], 2 * (hg - 1) + qt + 1)
                            for i in range(4):
                                h = 4 * hg + i
                                for kt in range(NT):
                                    mm = pe.matmul(BB[2 + qt][:, i * (DH + 1):(i + 1) * (DH + 1)],
                                                   pb[:, h % NPB, kt * T + qt * P:kt * T + (qt + 1) * P], vb[:, kt, h, :],
                                                   start=(kt == 0), stop=(kt == 1))
                            mm.then_inc(S["b_pv"], 1)

                    def b_out(_):
                        for qt in range(NT):
                            pe.wait_ge(S["b_z"], E * (qt + 1))
                            for c in range(E // 2):
                                mm = pe.transpose(BB[qt][:, c * P:(c + 1) * P], z[:, qt, c * P:(c + 1) * P], ident[:, :])
                            mm.then_inc(S["b_zt"], 1)
                        for qt in range(NT):
                            pe.wait_ge(S["b_zc"], qt + 1)
                            pe.wait_ge(S["b_at"], 8)
                            for c in range(E // 2):
                                mm = pe.matmul(BB[2 + qt][:, 0:P], zT[:, qt, c, :], wo_t[:, c, :],
                                               start=(c == 0), stop=(c == E // 2 - 1))
                            mm.then_inc(S["b_ro"], 1)

                    own = dict(f_norm_apply=f_norm_apply, a_stack=a_stack, a_values=a_values, a_max=a_max, a_shift=a_shift,
                               a_score=a_score, a_lastpv=a_lastpv, a_heads=a_heads, a_project=a_project, a_norm2_apply=a_norm2_apply,
                               a_router=a_router, a_expert=a_expert, a_b2=a_b2, c_norm_apply=c_norm_apply, c_qkv=c_qkv,
                               c_max=c_max, c_turn=c_turn, c_out=c_out, b_norm_apply=b_norm_apply,
                               b_gates=b_gates, b_split=b_split, b_max=b_max, b_shift=b_shift, b_score=b_score,
                               b_attend=b_attend, b_out=b_out)
                    for name, i in steps:
                        if name in own:
                            own[name](i)

                @block.scalar
                def _(act):
                    def f_norm_apply(_):
                        act.wait_ge(S["f_xt"], 1)
                        nc.scalar.copy(xnT_a[:, :], BA[2][:, 0:T])
                        nc.scalar.copy(cxT_a[:, :], BA[2][0:CC, T:2 * T])

                    def a_stack(u):
                        act.wait_ge(S["a_pj"], u + 1)
                        kind = KINDS[u // 2]
                        for c in range(2):
                            n, k = 2 * u + c, kind * G + 2 * (u % 2) + c
                            if n >= 4:
                                act.wait_ge(S["a_split"], n - 3)
                            nc.scalar.activation(hi_part[:, n % 4, :].bitcast(F32R), BA[u % 4][:, c * T:(c + 1) * T], ACT.Identity,
                                                 bias=lo_bias[:, k:k + 1], scale=lo_c[:, kind % 2:kind % 2 + 1])\
                              .then_inc(S["a_mh"], 1)

                    def a_values(_):
                        act.wait_ge(S["a_vp"], 1)
                        nc.scalar.copy(va[:, :, :, 0:H * DV].rearrange("p s t (h d) -> p (s t) h d", d=DV)[:, :, :, 0:D],
                                       BA[0][:, :].rearrange("p (a h d) -> p a h d", a=4, d=D)).then_inc(S["a_vc"], 1)

                    def a_score(n):
                        act.wait_ge(S["a_st"], n + 1)
                        if n >= NPA:
                            old = n - NPA
                            act.wait_ge(S["a_pv"], 2 * (old // PER_J) + (1 if old % PER_J < 4 else 2))
                        nc.scalar.activation(pa[:, n % NPA, :], BA[n % 2][:, :], ACT.Exp, scale=SC0).then_inc(S["a_ex"], 1)

                    def a_project(_):
                        act.wait_ge(S["a_yt"], 1)
                        nc.scalar.copy(yT[:, :], BA[0][:, 0:T]).then_inc(S["a_yc"], 1)

                    def a_norm2_apply(_):
                        act.wait_ge(S["a_xt"], 1)
                        nc.scalar.copy(xnT_a[:, :], BA[2][:, 0:T]).then_inc(S["a_xc"], 1)

                    def hidden_relu(u):
                        act.wait_ge(S["a_h"], u + 1)
                        if u >= 4:
                            act.wait_ge(S["a_yp"], u // 2 - 1)
                        for c in range(2):
                            k = 2 * u + c
                            ins = nc.scalar.activation(hT[:, u % 4, c, :], BA[u % 2][:, c * T:(c + 1) * T], ACT.Relu,
                                                       bias=b1_c[:, k:k + 1])
                        ins.then_inc(S["a_ha"], 1)

                    def a_router(_):
                        act.wait_ge(S["a_lx"], 1)
                        nc.scalar.activation(ex[:, :, :], ex[:, :, :], ACT.Exp).then_inc(S["a_lx"], 1)
                        hidden_relu(0)
                        hidden_relu(1)

                    def a_expert(e):
                        if e + 1 < E:
                            hidden_relu(2 * e + 2)
                            hidden_relu(2 * e + 3)

                    def c_norm_apply(_):
                        act.wait_ge(S["a_xt"], 2)
                        nc.scalar.copy(xnT_a[:, :], BA[0][:, 0:T]).then_inc(S["a_xc"], 1)

                    def c_qkv(_):
                        act.wait_ge(S["c_qk"], 1)
                        nc.scalar.activation(q1T[:, :], BA[1][:, 0:T], ACT.Identity, bias=bqk_c[:, 0:1]).then_inc(S["c_qc"], 1)
                        nc.scalar.activation(k1T[:, :], BA[1][:, T:2 * T], ACT.Identity, bias=bqk_c[:, 1:2]).then_inc(S["c_qc"], 1)
                        act.wait_ge(S["c_qk"], 2)
                        nc.scalar.copy(v1[:, :, :].rearrange("p t n -> p (t n)"), BA[2][:, 0:2 * P]).then_inc(S["c_qc"], 1)

                    def c_max(_):
                        act.wait_ge(S["c_m1"], 1)
                        for t in range(NT):
                            nc.scalar.activation(p1[:, t, :], BA[3][:, t * T:(t + 1) * T], ACT.Exp, bias=nm1[:, t:t + 1],
                                                 accum_out=rs1[:, t:t + 1]).then_inc(S["c_e1"], 1)

                    def c_turn(_):
                        act.wait_ge(S["c_pt"], 1)
                        nc.scalar.copy(p1T[:, :, :].rearrange("p t n -> p (t n)"), BA[0][:, :]).then_inc(S["c_pc"], 1)

                    def b_norm_apply(_):
                        act.wait_ge(S["b_xt"], 1)
                        nc.scalar.copy(xnT_b[:, :], BB[2][:, 0:T]).then_inc(S["b_xc"], 1)

                    def b_gates(_):
                        for t in range(NT):
                            act.wait_ge(S["b_pvj"], t + 1)
                            nc.scalar.copy(pvs[:, t, :], BB[t][:, :]).then_inc(S["b_pvc"], 1)
                        act.wait_ge(S["b_gc"], 1)
                        nc.scalar.activation(eg[:, :, :], gates[:, 0, :, :], ACT.Exp, scale=-1.0).then_inc(S["b_sg"], 1)

                    def b_split(u):
                        act.wait_ge(S["b_qkp"], u + 1)
                        r = 2 * (u % 4)
                        nc.scalar.copy(qk_hi[:, u // 4, r:r + 2, :].rearrange("p r n -> p (r n)"),
                                       BB[(u + 2) % 4][:, :]).then_inc(S["b_hi"], 1)

                    def b_score(h):
                        act.wait_ge(S["b_st"], h + 1)
                        if h >= NPB:
                            act.wait_ge(S["b_pv"], 2 * ((h - NPB) // 4 + 1))
                        nc.scalar.activation(pb[:, h % NPB, :], BB[h % 2][:, :], ACT.Exp, scale=SC1).then_inc(S["b_ex"], 1)

                    def b_attend(hg):
                        for qt in range(NT):
                            act.wait_ge(S["b_pv"], 2 * hg + qt + 1)
                            nc.scalar.copy(at[:, qt, 4 * hg:4 * hg + 4, :].rearrange("p h d -> p (h d)"),
                                           BB[2 + qt][:, 0:4 * (DH + 1)]).then_inc(S["b_at"], 1)

                    def b_out(_):
                        for qt in range(NT):
                            act.wait_ge(S["b_zt"], qt + 1)
                            nc.scalar.copy(zT[:, qt, :, :].rearrange("p c n -> p (c n)"), BB[qt][:, :]).then_inc(S["b_zc"], 1)

                    own = dict(f_norm_apply=f_norm_apply, a_stack=a_stack, a_values=a_values, a_score=a_score, a_project=a_project,
                               a_norm2_apply=a_norm2_apply, a_router=a_router, a_expert=a_expert, c_norm_apply=c_norm_apply, c_qkv=c_qkv,
                               c_max=c_max, c_turn=c_turn, b_norm_apply=b_norm_apply, b_gates=b_gates,
                               b_split=b_split, b_score=b_score, b_attend=b_attend, b_out=b_out)
                    for name, i in steps:
                        if name in own:
                            own[name](i)

                @block.gpsimd
                def _(pool):
                    def b_mix(n):
                        if n % 2:
                            return
                        if n == 0:
                            pool.wait_ge(S["b_pvc"], 2)
                            pool.wait_ge(S["b_mw"], 1)
                        else:
                            pool.wait_ge(S["b_vm"], n - 1)
                        mix_products(nc.gpsimd, n).then_inc(S["b_vp"], 1)

                    def b_gather(n):
                        if n % 2:
                            return
                        if n == 0:
                            pool.wait_ge(S["b_mw"], 2)
                        else:
                            pool.wait_ge(S["b_z"], n - 1)
                        gather_products(nc.gpsimd, n).then_inc(S["b_zp"], 1)

                    own = dict(b_mix=b_mix, b_gather=b_gather)
                    for name, i in steps:
                        if name in own:
                            own[name](i)

                @block.vector
                def _(dve):
                    chain = [0]

                    def link(ins, wait=True):
                        chain[0] += 1
                        ins.then_inc(S["v_link"], 1)
                        if wait:
                            dve.wait_ge(S["v_link"], chain[0])

                    def halves(bank):
                        return bank[:, 0:T].rearrange("p (t n) -> p t n", t=NT)

                    def f_norm(_):
                        dve.wait_ge(S["f_in"], 32)
                        norm_stats(link, x_f, "f")
                        norm_root(link, "f")

                    def f_norm_apply(_):
                        if seq_a is not None:
                            dve.wait_ge(S["a_xt"], 2)
                        norm_apply(x_f, "f", S["f_xn"])

                    def a_stack(u):
                        kind = KINDS[u // 2]
                        dve.wait_ge(S["a_mh"], 2 * u + 2)
                        for c in range(2):
                            n, g = 2 * u + c, 2 * (u % 2) + c
                            stack = qs if kind in (Q0, QC) else ks
                            nc.vector.scalar_tensor_tensor(stack[:, kind // 2, g, :], BA[u % 4][:, c * T:(c + 1) * T],
                                                           bias_c[:, kind * G + g:kind * G + g + 1], hi_part[:, n % 4, :],
                                                           ALU.add, ALU.subtract).then_inc(S["a_split"], 1)

                    def a_max(n):
                        sc, qt, j, gp = MAXS[n]
                        dve.wait_ge(S["a_s"], n + 1)
                        g0, ng = (0, 4) if gp is None else (2 * gp, 2)
                        i = 3 * D + 32 * j + (qt * 2 + sc) * G + g0
                        nc.vector.tensor_reduce(negmax[:, i:i + ng], BA[n % 4][:, :].rearrange("p (g k) -> p g k", g=ng),
                                                AX, ALU.max, negate=True).then_inc(S["a_mx"], 1)

                    def a_shift(_):
                        for m in range(4):
                            qt, sc = m // 2, m % 2
                            dve.wait_ge(S["a_ct"], m + 1)
                            dst = qs[:, sc, :, qt * P:(qt + 1) * P]
                            nc.vector.scalar_tensor_tensor(dst, BA[m][:, :].rearrange("p (g q) -> p g q", g=G), shift_c[:, 0:1],
                                                           dst.bitcast(F32), ALU.mult, ALU.add).then_inc(S["a_qs"], 1)

                    def outputs(i):
                        sc = CROSS if i % 2 == 0 else SELF
                        dve.wait_ge(S["a_pv"], i + 1)
                        nc.vector.tensor_copy(oT[sc][:, i // 2, :], BA[2 + i % 2][:, 0:T]).then_inc(S["a_ot"], 1)

                    def a_score(n):
                        j, k = n // PER_J, n % PER_J
                        if j >= 1 and k in (3, 5):
                            outputs(2 * (j - 1) + (k - 3) // 2)

                    def a_lastpv(_):
                        outputs(6)
                        outputs(7)

                    def a_heads(_):
                        for qt in range(NT):
                            dve.wait_ge(S["a_tr"], 2 * qt + 2)
                            heads = [BA[2 * qt + sc][:, :].rearrange("p (h r) -> p h r", r=32) for sc in range(2)]
                            for sc in range(2):
                                link(nc.vector.reciprocal(recA[:, sc, :], heads[sc][:, :, D]), wait=(sc == 1))
                            for sc in range(2):
                                link(nc.vector.tensor_tensor(
                                    yh[:, sc, :].rearrange("p (g j d) -> p j g d", g=G, j=4),
                                    heads[sc][:, :, 0:D].rearrange("p (j g) d -> p j g d", j=4),
                                    recA[:, sc, :].rearrange("p (j g) -> p j g", j=4).unsqueeze(3).broadcast_to([P, 4, G, D]),
                                    ALU.mult), wait=(sc == 1))
                            nc.vector.tensor_tensor(y[:, qt, :], yh[:, 0, :], yh[:, 1, :], ALU.add).then_inc(S["a_y"], 1)
                            dve.wait_ge(S["a_y"], qt + 1)

                    def a_project(_):
                        dve.wait_ge(S["a_o"], 1)
                        nc.vector.tensor_tensor(x_a[:, :, :], x_f[:, :, :], halves(BA[1]), ALU.add).then_inc(S["a_x1"], 1)

                    def a_norm2(_):
                        dve.wait_ge(S["a_x1"], 1)
                        norm_stats(link, x_a, "a")
                        norm_root(link, "a")

                    def a_norm2_apply(_):
                        norm_apply(x_a, "a", S["a_xn"])

                    def a_router(_):
                        dve.wait_ge(S["a_lg"], 1)
                        lgf = lg[:, :, :].rearrange("p t e -> p (t e)")
                        nc.vector.tensor_copy(lgf, BA[3][:, 0:NT * E]).then_inc(S["a_lgc"], 1)
                        dve.wait_ge(S["a_lgc"], 1)
                        link(nc.vector.tensor_reduce(m1[:, :], lg[:, :, :], AX, ALU.max))
                        nc.vector.tensor_tensor(ex[:, :, :], lg[:, :, :], m1[:, :].unsqueeze(2).broadcast_to([P, NT, E]),
                                                ALU.subtract).then_inc(S["a_lx"], 1)
                        top2_vector(link, lgf, NT, top_a)
                        dve.wait_ge(S["a_lx"], 2)
                        link(nc.vector.tensor_tensor(ex[:, :, :], ex[:, :, :], top_a[0][:, :].rearrange("p (t e) -> p t e", e=E), ALU.mult))
                        link(nc.vector.tensor_reduce(m1[:, :], ex[:, :, :], AX, ALU.add))
                        link(nc.vector.reciprocal(m1[:, :], m1[:, :]))
                        nc.vector.tensor_tensor(wr[:, :, :], ex[:, :, :], m1[:, :].unsqueeze(2).broadcast_to([P, NT, E]),
                                                ALU.mult).then_inc(S["a_w"], 1)
                        dve.wait_ge(S["a_w"], 1)

                    def accumulate(e):
                        dve.wait_ge(S["a_yp"], e + 1)
                        if e >= 1:
                            dve.wait_ge(S["a_acc"], e)
                        for t in range(NT):
                            ins = nc.vector.scalar_tensor_tensor(x_a[:, t, :], BA[2 + e % 2][:, t * P:(t + 1) * P],
                                                                 wr[:, t, e:e + 1], x_a[:, t, :], ALU.mult, ALU.add)
                        ins.then_inc(S["a_acc"], 1)

                    def a_expert(e):
                        if e >= 1:
                            accumulate(e - 1)

                    def a_b2(_):
                        accumulate(E - 1)
                        dve.wait_ge(S["a_wt"], 1)
                        nc.vector.tensor_copy(wrT[:, :], BA[0][0:E, 0:T]).then_inc(S["a_wtc"], 1)
                        dve.wait_ge(S["a_b2"], 1)
                        dve.wait_ge(S["a_acc"], E)
                        link(nc.vector.tensor_tensor(x_a[:, :, :], x_a[:, :, :], halves(BA[1]), ALU.add))

                    def c_norm(_):
                        norm_stats(link, x_a, "a")
                        norm_root(link, "a")

                    def c_norm_apply(_):
                        norm_apply(x_a, "a", S["a_xn"])

                    def c_max(_):
                        dve.wait_ge(S["c_s1"], 1)
                        nc.vector.tensor_reduce(nm1[:, :], BA[3][:, :].rearrange("p (t k) -> p t k", t=NT), AX, ALU.max,
                                                negate=True).then_inc(S["c_m1"], 1)

                    def c_out(_):
                        dve.wait_ge(S["c_e1"], 2)
                        link(nc.vector.reciprocal(rr1[:, :], rs1[:, :]))
                        dve.wait_ge(S["c_o1"], 1)
                        if seq_b is not None:
                            dve.wait_ge(S["b_x1"], 1)
                        for t in range(NT):
                            nc.vector.scalar_tensor_tensor(x_mid[:, t, :], BA[1][:, t * P:(t + 1) * P], rr1[:, t:t + 1],
                                                           x_a[:, t, :], ALU.mult, ALU.add)

                    def b_norm(_):
                        norm_stats(link, x_mid, "b")
                        norm_root(link, "b")

                    def b_norm_apply(_):
                        norm_apply(x_mid, "b", S["b_xn"])
                        nc.vector.tensor_copy(x_b[:, :, :], x_mid[:, :, :]).then_inc(S["b_x1"], 1)

                    def b_gates(_):
                        dve.wait_ge(S["b_g"], 1)
                        nc.vector.tensor_copy(gates[:, :, :, :].rearrange("p k t n -> p t k n"),
                                              BB[3][:, :].rearrange("p (t k n) -> p t k n", t=NT, k=2)).then_inc(S["b_gc"], 1)

                    def b_split(u):
                        r = 2 * (u % 4)
                        lo = qk_lo[:, u // 4, r:r + 2, :].rearrange("p r n -> p (r n)")
                        hi = qk_hi[:, u // 4, r:r + 2, :].rearrange("p r n -> p (r n)")
                        dve.wait_ge(S["b_hi"], u + 1)
                        nc.vector.tensor_tensor(lo, BB[(u + 2) % 4][:, :], hi.bitcast(F32), ALU.subtract).then_inc(S["b_lo"], 1)

                    def b_max(n):
                        qt, pp, j = n // 8, (n // 2) % 4, n % 2
                        c = 64 * j + 4 * pp + j
                        dve.wait_ge(S["b_s"], n + 1)
                        nc.vector.tensor_reduce(negc[:, qt, c:c + 3:2], BB[(n + 2) % 4][:, :].rearrange("p (h k) -> p h k", h=2),
                                                AX, ALU.max, negate=True).then_inc(S["b_mx"], 1)

                    def b_shift(_):
                        dve.wait_ge(S["b_ct"], 1)
                        nc.vector.tensor_copy(cT[:, :], BB[2][:, 0:T]).then_inc(S["b_cc"], 1)

                    chosen = top_b[0][:, :].rearrange("p (k t n) -> p k t n", k=2, t=NT)

                    def b_top2(_):
                        dve.wait_ge(S["b_gc"], 1)
                        top2_vector(link, gates[:, :, :, :].rearrange("p k t n -> p (k t n)"), 2 * NT * HB, top_b)
                        dve.wait_ge(S["b_sg"], 1)
                        link(nc.vector.tensor_scalar(eg[:, :, :], eg[:, :, :], 1.0, None, ALU.add))
                        link(nc.vector.reciprocal(eg[:, :, :], eg[:, :, :]))
                        nc.vector.tensor_tensor(mix[:, :, :], eg[:, :, :], chosen[:, 0], ALU.mult).then_inc(S["b_mw"], 1)
                        dve.wait_ge(S["b_mw"], 1)

                    def b_mix(n):
                        pr, t = n // 2, n % 2
                        if n % 2:
                            if n == 1:
                                dve.wait_ge(S["b_pvc"], 2)
                            if n >= 3:
                                dve.wait_ge(S["b_vm"], n - 1)
                            link(mix_products(nc.vector, n))
                        else:
                            dve.wait_ge(S["b_vp"], n // 2 + 1)
                        nc.vector.tensor_reduce(vb[:, t, 2 * pr:2 * pr + 2, 0:DH],
                                                prod[:, t * NG:(t + 1) * NG].rearrange("p (h d e) -> p h d e", h=2, d=DH),
                                                AX, ALU.add).then_inc(S["b_vm"], 1)

                    def b_weigh(_):
                        dve.wait_ge(S["b_at"], 8)
                        link(nc.vector.reciprocal(recB[:, :], at[:, :, :, DH].rearrange("p t h -> p (t h)")))
                        nc.vector.tensor_tensor(mout[:, :, :].rearrange("p t (h e) -> p (t h) e", e=E),
                                                chosen[:, 1].rearrange("p t (h e) -> p (t h) e", e=E),
                                                recB[:, :].unsqueeze(2).broadcast_to([P, NT * HB, E]), ALU.mult).then_inc(S["b_mw"], 1)
                        dve.wait_ge(S["b_mw"], 2)

                    def b_gather(n):
                        t, e = n // E, n % E
                        if n % 2:
                            if n >= 3:
                                dve.wait_ge(S["b_z"], n - 1)
                            link(gather_products(nc.vector, n))
                        else:
                            dve.wait_ge(S["b_zp"], n // 2 + 1)
                        nc.vector.tensor_reduce(z[:, t, e * DH:(e + 1) * DH],
                                                prod[:, (n % 2) * NG:(n % 2 + 1) * NG].rearrange("p (d h) -> p d h", d=DH),
                                                AX, ALU.add).then_inc(S["b_z"], 1)

                    def b_out(_):
                        for t in range(NT):
                            dve.wait_ge(S["b_ro"], t + 1)
                            if t == 0:
                                dve.wait_ge(S["b_x1"], 1)
                            nc.vector.tensor_tensor(x_b[:, t, :], x_b[:, t, :], BB[2 + t][:, 0:P], ALU.add).then_inc(S["b_xo"], 1)

                    own = dict(f_norm=f_norm, f_norm_apply=f_norm_apply, a_stack=a_stack, a_max=a_max, a_shift=a_shift, a_score=a_score,
                               a_lastpv=a_lastpv, a_heads=a_heads, a_project=a_project, a_norm2=a_norm2, a_norm2_apply=a_norm2_apply, a_router=a_router,
                               a_expert=a_expert, a_b2=a_b2, c_norm=c_norm, c_norm_apply=c_norm_apply, c_max=c_max, c_out=c_out,
                               b_norm=b_norm, b_norm_apply=b_norm_apply, b_gates=b_gates, b_split=b_split, b_max=b_max, b_shift=b_shift,
                               b_top2=b_top2, b_mix=b_mix, b_weigh=b_weigh, b_gather=b_gather, b_out=b_out)
                    for name, i in steps:
                        if name in own:
                            own[name](i)

            nc.all_engine_barrier(sems_to_clear=seq_sems)

        order = interleave(STEPS_A, STEPS_B)
        sequences(order, 0, None, None)
        sequences(order, 1, 0, None)
        with nc.Fori(0, B - 2) as b:
            sequences(order, b + 2, b + 1, b)
        sequences(order, None, B - 1, B - 2)
        sequences(order, None, None, B - 1)


_INS = ['x', 'ctx_512', 'L0_xattn_Wk', 'L0_xattn_bk', 'L0_xattn_Wq', 'L0_xattn_bq', 'L0_xattn_Wv', 'L0_xattn_bv',
        'L0_xattn_Wck', 'L0_xattn_bck', 'L0_xattn_Wcq', 'L0_xattn_bcq', 'L0_xattn_Wcv', 'L0_xattn_bcv', 'L0_xattn_Wp',
        'L0_xattn_bp', 'L0_ffn_W_router', 'L0_ffn_b_router', 'L0_ffn_W1', 'L0_ffn_b1', 'L0_ffn_W2', 'L0_ffn_b2',
        'L1_xattn_Wq', 'L1_xattn_bq', 'L1_xattn_Wk', 'L1_xattn_bk', 'L1_xattn_Wv', 'L1_xattn_bv', 'L1_ffn_Wq',
        'L1_ffn_Wk', 'L1_ffn_Wv', 'L1_ffn_Ws', 'L1_ffn_Wd', 'L1_ffn_Wo']


def kernel(**inputs):
    import numpy as _np
    import concourse.bacc as _bacc
    from concourse import mybir as _mybir
    from concourse.bass_utils import run_bass_kernel_spmd as _run

    nc = _bacc.Bacc("TRN2", target_bir_lowering=False, num_devices=1)
    arrays, aps = {}, {}
    for name in _INS:
        v = _np.ascontiguousarray(inputs[name])
        arrays[f"in_{name}_dram"] = v
        aps[name] = nc.dram_tensor(f"in_{name}_dram", v.shape, _mybir.dt.from_np(v.dtype), kind="ExternalInput").ap()
    out = nc.dram_tensor("out_0_dram", inputs["x"].shape, _mybir.dt.float32, kind="ExternalOutput").ap()
    transformer_program(nc, aps, out)
    r = _run(nc, [arrays], core_ids=[0])
    return r.results[0]["out_0_dram"]
```
